# Optimizing a Trainium2 kernel written in Bass

```python
import numpy as np
import jax
import jax.numpy as jnp

def _softmax(x, axis=-1):
    return jax.nn.softmax(x, axis=axis)

def _gelu(x):
    return jax.nn.gelu(x, approximate=True)

def _silu(x):
    return jax.nn.silu(x)

def _sigmoid(x):
    return jax.nn.sigmoid(x)

def _layernorm(x, axis=-1, eps=1e-05):
    m = jnp.mean(x, axis=axis, keepdims=True)
    v = jnp.var(x, axis=axis, keepdims=True)
    return (x - m) / jnp.sqrt(v + eps)

def _scatter_add(tgt, idx, src, axis=0):
    return tgt.at[idx].add(src)

def _segment_sum(src, seg, n):
    return jax.ops.segment_sum(src, seg, n)
kernel_name = 'mk_audio_tower_d2_tok_aud1d256_r4_f2f723'

def setup_inputs(seed: int=0):
    np.random.seed(seed)
    _w = jnp.asarray

    def _rec_inputs():
        import jax
        import jax.numpy as jnp
        _rk = jax.random.key(seed)
        x = 0.000296351 + 0.99907 * jax.random.normal(jax.random.fold_in(_rk, 1), (16, 4096), jnp.float32)
        return x
    x = _rec_inputs()

    def _L0_tok_setup():
        import jax, jax.numpy as jnp
        import numpy as np
        B, L = (64, 4096)
        INTERP_FACTOR = 0.25
        WINDOW, STEP = (64, 64)
        ALPHA, BETA, TEMP = (0.12, 0.9, 1.0)
        A = -0.75

        def _cubic_w(t):
            at = jnp.abs(t)
            w_near = ((A + 2.0) * at - (A + 3.0)) * at * at + 1.0
            w_far = ((A * at - 5.0 * A) * at + 8.0 * A) * at - 4.0 * A
            return jnp.where(at <= 1.0, w_near, jnp.where(at < 2.0, w_far, 0.0))

        def cubic_interpolate_1d(signal, interp_factor):
            b, n = signal.shape
            num_points = int((n - 1) / interp_factor) + 1
            x = jnp.linspace(0.0, 1.0, num_points) * (n - 1)
            i0 = jnp.floor(x).astype(jnp.int32)
            frac = x - i0.astype(x.dtype)
            offs = jnp.arange(-1, 3)
            idx = jnp.clip(i0[:, None] + offs[None, :], 0, n - 1)
            w = _cubic_w(frac[:, None] - offs[None, :].astype(x.dtype))
            taps = signal[:, idx]
            return jnp.einsum('bpk,pk->bp', taps, w)

        def _apply_kernels(x):
            poly = (x + 1.3) ** 2
            gauss = jnp.exp(-0.5 * ((x - 0.7) / 1.0) ** 2)
            return 0.5 * poly + 0.5 * gauss

        def soft_minimum(a, b, temperature):
            b = jnp.broadcast_to(b, a.shape)
            stacked = jnp.stack([-a * temperature, -b * temperature], axis=0)
            return -jax.nn.logsumexp(stacked, axis=0) / temperature

        def _forward(signal):
            interp = cubic_interpolate_1d(signal, INTERP_FACTOR)
            n = interp.shape[1]
            n_windows = (n - WINDOW) // STEP + 1
            starts = jnp.arange(n_windows) * STEP
            idx = starts[:, None] + jnp.arange(WINDOW)[None, :]
            windows = interp[:, idx]
            kw = _apply_kernels(windows)
            M = jnp.abs(jnp.fft.fft(kw, axis=-1))
            Mmax = jnp.max(M, axis=-1, keepdims=True)
            thr = ALPHA * Mmax
            mask = jax.nn.sigmoid((M - thr) * TEMP)
            Mt = M * mask
            return soft_minimum(Mt, BETA * Mmax, TEMP)
        key = jax.random.key(seed)
        return {'signal': jax.random.normal(key, (B, L), dtype=jnp.float32)}
    _L0_tok_all = _L0_tok_setup()
    _L0_tok_in = {k: v for k, v in _L0_tok_all.items() if k in ()}
    del _L0_tok_all

    def _L0_attn_setup():
        import jax, jax.numpy as jnp
        import numpy as np
        import math
        H = 8
        DH = 16
        DEPTH = 1
        LAMBDA_INIT = 0.8 - 0.6 * math.exp(-0.3 * DEPTH)
        LN_EPS = 1e-05
        key = jax.random.key(seed)
        ks = jax.random.split(key, 12)
        dim = 64
        inner = 2 * H * DH
        b, n = (2, 512)
        s = lambda fan_in: 1.0 / math.sqrt(fan_in)
        return {'x': jax.random.normal(ks[0], (b, n, dim), jnp.float32), 'Wq': jax.random.normal(ks[1], (dim, inner), jnp.float32) * s(dim), 'Wkv': jax.random.normal(ks[2], (dim, 2 * inner), jnp.float32) * s(dim), 'Wout': jax.random.normal(ks[3], (inner, dim), jnp.float32) * s(inner), 'bout': jnp.zeros((dim,), jnp.float32), 'Wg': jax.random.normal(ks[4], (dim, inner), jnp.float32) * s(dim), 'bg': jnp.ones((inner,), jnp.float32), 'lq1': jax.random.normal(ks[5], (DH,), jnp.float32) * 0.1, 'lk1': jax.random.normal(ks[6], (DH,), jnp.float32) * 0.1, 'lq2': jax.random.normal(ks[7], (DH,), jnp.float32) * 0.1, 'lk2': jax.random.normal(ks[8], (DH,), jnp.float32) * 0.1, 'ln_gamma': jnp.ones((2 * DH,), jnp.float32), 'ln_beta': jnp.zeros((2 * DH,), jnp.float32)}
    _L0_attn_all = _L0_attn_setup()
    _L0_attn_in = {k: v for k, v in _L0_attn_all.items() if k in ('Wq', 'Wkv', 'Wout', 'bout', 'Wg', 'bg', 'lq1', 'lk1', 'lq2', 'lk2', 'ln_gamma', 'ln_beta')}
    del _L0_attn_all

    def _L0_ffn_setup():
        import math
        import jax, jax.numpy as jnp
        import numpy as np
        CAPACITY_FACTOR = 1.25
        TOP_K = 2
        LN_EPS = 1e-05

        def _layer_norm(x, gamma, beta):
            mu = jnp.mean(x, axis=-1, keepdims=True)
            var = jnp.var(x, axis=-1, keepdims=True)
            return (x - mu) * jax.lax.rsqrt(var + LN_EPS) * gamma + beta
        key = jax.random.key(seed)
        ks = jax.random.split(key, 4)
        B, S, D, F, E = (8, 1024, 64, 128, 8)
        x = jax.random.normal(ks[0], (B, S, D), dtype=jnp.float32)
        Wr = jax.random.normal(ks[1], (D, E), dtype=jnp.float32) / np.sqrt(D)
        br = jnp.zeros((E,), jnp.float32)
        W1 = jax.random.normal(ks[2], (E, D, F), dtype=jnp.float32) / np.sqrt(D)
        b1 = jnp.zeros((E, F), jnp.float32)
        W2 = jax.random.normal(ks[3], (E, F, D), dtype=jnp.float32) / np.sqrt(F)
        b2 = jnp.zeros((E, D), jnp.float32)
        gamma = jnp.ones((D,), jnp.float32)
        beta = jnp.zeros((D,), jnp.float32)
        return {'x': x, 'Wr': Wr, 'br': br, 'W1': W1, 'b1': b1, 'W2': W2, 'b2': b2, 'gamma': gamma, 'beta': beta}
    _L0_ffn_all = _L0_ffn_setup()
    _L0_ffn_in = {k: v for k, v in _L0_ffn_all.items() if k in ('Wr', 'br', 'W1', 'b1', 'W2', 'b2', 'gamma', 'beta')}
    del _L0_ffn_all

    def _L1_attn_setup():
        import jax, jax.numpy as jnp
        import numpy as np
        import math
        N, HW, D = (8, 4096, 64)
        HEADS = 8
        key = jax.random.key(seed)
        ks = jax.random.split(key, 9)
        s = 1.0 / math.sqrt(D)
        return {'x': jax.random.normal(ks[0], (N, HW, D), jnp.float32), 'Wk': jax.random.normal(ks[1], (D, D), jnp.float32) * s, 'bk': jax.random.normal(ks[2], (D,), jnp.float32) * 0.01, 'Wq': jax.random.normal(ks[3], (D, D), jnp.float32) * s, 'bq': jax.random.normal(ks[4], (D,), jnp.float32) * 0.01, 'Wv': jax.random.normal(ks[5], (D, D), jnp.float32) * s, 'bv': jax.random.normal(ks[6], (D,), jnp.float32) * 0.01, 'Wr': jax.random.normal(ks[7], (D, D), jnp.float32) * s, 'br': jax.random.normal(ks[8], (D,), jnp.float32) * 0.01}
    _L1_attn_all = _L1_attn_setup()
    _L1_attn_in = {k: v for k, v in _L1_attn_all.items() if k in ('Wk', 'bk', 'Wq', 'bq', 'Wv', 'bv', 'Wr', 'br')}
    del _L1_attn_all

    def _L1_ffn_setup():
        import jax, jax.numpy as jnp
        import numpy as np
        B, A = (1024, 8)
        IN, OUT = (64, 64)
        SH1, SH2 = (64, 128)
        EH1, EH2 = (128, 64)
        E, TOPK = (4, 2)

        def _shared_mlp(x, W1, b1, W2, b2, W3, b3):
            h = jax.nn.relu(x @ W1 + b1)
            h = jax.nn.relu(h @ W2 + b2)
            return h @ W3 + b3

        def _experts_mlp(x, eW1, eb1, eW2, eb2, eW3, eb3):
            h = jax.nn.relu(jnp.einsum('baf,efh->ebah', x, eW1) + eb1[:, None, None, :])
            h = jax.nn.relu(jnp.einsum('ebah,ehg->ebag', h, eW2) + eb2[:, None, None, :])
            o = jnp.einsum('ebag,ego->ebao', h, eW3) + eb3[:, None, None, :]
            return jnp.moveaxis(o, 0, -1)
        key = jax.random.key(seed)
        ks = jax.random.split(key, 16)
        s = 0.05
        return {'x': jax.random.normal(ks[0], (B, A, IN), jnp.float32), 'sW1': jax.random.normal(ks[1], (IN, SH1), jnp.float32) * s, 'sb1': jnp.zeros((SH1,), jnp.float32), 'sW2': jax.random.normal(ks[2], (SH1, SH2), jnp.float32) * s, 'sb2': jnp.zeros((SH2,), jnp.float32), 'sW3': jax.random.normal(ks[3], (SH2, OUT), jnp.float32) * s, 'sb3': jnp.zeros((OUT,), jnp.float32), 'eW1': jax.random.normal(ks[4], (E, IN, EH1), jnp.float32) * s, 'eb1': jnp.zeros((E, EH1), jnp.float32), 'eW2': jax.random.normal(ks[5], (E, EH1, EH2), jnp.float32) * s, 'eb2': jnp.zeros((E, EH2), jnp.float32), 'eW3': jax.random.normal(ks[6], (E, EH2, OUT), jnp.float32) * s, 'eb3': jnp.zeros((E, OUT), jnp.float32), 'gW': jax.random.normal(ks[7], (IN, E), jnp.float32) * s, 'gb': jnp.zeros((E,), jnp.float32)}
    _L1_ffn_all = _L1_ffn_setup()
    _L1_ffn_in = {k: v for k, v in _L1_ffn_all.items() if k in ('sW1', 'sb1', 'sW2', 'sb2', 'sW3', 'sb3', 'eW1', 'eb1', 'eW2', 'eb2', 'eW3', 'eb3', 'gW', 'gb')}
    del _L1_ffn_all
    return {'x': x, 'L0_attn_Wq': _L0_attn_in['Wq'], 'L0_attn_Wkv': _L0_attn_in['Wkv'], 'L0_attn_Wout': _L0_attn_in['Wout'], 'L0_attn_bout': _L0_attn_in['bout'], 'L0_attn_Wg': _L0_attn_in['Wg'], 'L0_attn_bg': _L0_attn_in['bg'], 'L0_attn_lq1': _L0_attn_in['lq1'], 'L0_attn_lk1': _L0_attn_in['lk1'], 'L0_attn_lq2': _L0_attn_in['lq2'], 'L0_attn_lk2': _L0_attn_in['lk2'], 'L0_attn_ln_gamma': _L0_attn_in['ln_gamma'], 'L0_attn_ln_beta': _L0_attn_in['ln_beta'], 'L0_ffn_Wr': _L0_ffn_in['Wr'], 'L0_ffn_br': _L0_ffn_in['br'], 'L0_ffn_W1': _L0_ffn_in['W1'], 'L0_ffn_b1': _L0_ffn_in['b1'], 'L0_ffn_W2': _L0_ffn_in['W2'], 'L0_ffn_b2': _L0_ffn_in['b2'], 'L0_ffn_gamma': _L0_ffn_in['gamma'], 'L0_ffn_beta': _L0_ffn_in['beta'], 'L1_attn_Wk': _L1_attn_in['Wk'], 'L1_attn_bk': _L1_attn_in['bk'], 'L1_attn_Wq': _L1_attn_in['Wq'], 'L1_attn_bq': _L1_attn_in['bq'], 'L1_attn_Wv': _L1_attn_in['Wv'], 'L1_attn_bv': _L1_attn_in['bv'], 'L1_attn_Wr': _L1_attn_in['Wr'], 'L1_attn_br': _L1_attn_in['br'], 'L1_ffn_sW1': _L1_ffn_in['sW1'], 'L1_ffn_sb1': _L1_ffn_in['sb1'], 'L1_ffn_sW2': _L1_ffn_in['sW2'], 'L1_ffn_sb2': _L1_ffn_in['sb2'], 'L1_ffn_sW3': _L1_ffn_in['sW3'], 'L1_ffn_sb3': _L1_ffn_in['sb3'], 'L1_ffn_eW1': _L1_ffn_in['eW1'], 'L1_ffn_eb1': _L1_ffn_in['eb1'], 'L1_ffn_eW2': _L1_ffn_in['eW2'], 'L1_ffn_eb2': _L1_ffn_in['eb2'], 'L1_ffn_eW3': _L1_ffn_in['eW3'], 'L1_ffn_eb3': _L1_ffn_in['eb3'], 'L1_ffn_gW': _L1_ffn_in['gW'], 'L1_ffn_gb': _L1_ffn_in['gb']}

def reference(x, L0_attn_Wq, L0_attn_Wkv, L0_attn_Wout, L0_attn_bout, L0_attn_Wg, L0_attn_bg, L0_attn_lq1, L0_attn_lk1, L0_attn_lq2, L0_attn_lk2, L0_attn_ln_gamma, L0_attn_ln_beta, L0_ffn_Wr, L0_ffn_br, L0_ffn_W1, L0_ffn_b1, L0_ffn_W2, L0_ffn_b2, L0_ffn_gamma, L0_ffn_beta, L1_attn_Wk, L1_attn_bk, L1_attn_Wq, L1_attn_bq, L1_attn_Wv, L1_attn_bv, L1_attn_Wr, L1_attn_br, L1_ffn_sW1, L1_ffn_sb1, L1_ffn_sW2, L1_ffn_sb2, L1_ffn_sW3, L1_ffn_sb3, L1_ffn_eW1, L1_ffn_eb1, L1_ffn_eW2, L1_ffn_eb2, L1_ffn_eW3, L1_ffn_eb3, L1_ffn_gW, L1_ffn_gb):
    import jax
    import jax.numpy as jnp

    def _L0_tok_ref(signal):
        import jax, jax.numpy as jnp
        import numpy as np
        B, L = (64, 4096)
        INTERP_FACTOR = 0.25
        WINDOW, STEP = (64, 64)
        ALPHA, BETA, TEMP = (0.12, 0.9, 1.0)
        A = -0.75

        def _cubic_w(t):
            at = jnp.abs(t)
            w_near = ((A + 2.0) * at - (A + 3.0)) * at * at + 1.0
            w_far = ((A * at - 5.0 * A) * at + 8.0 * A) * at - 4.0 * A
            return jnp.where(at <= 1.0, w_near, jnp.where(at < 2.0, w_far, 0.0))

        def cubic_interpolate_1d(signal, interp_factor):
            b, n = signal.shape
            num_points = int((n - 1) / interp_factor) + 1
            x = jnp.linspace(0.0, 1.0, num_points) * (n - 1)
            i0 = jnp.floor(x).astype(jnp.int32)
            frac = x - i0.astype(x.dtype)
            offs = jnp.arange(-1, 3)
            idx = jnp.clip(i0[:, None] + offs[None, :], 0, n - 1)
            w = _cubic_w(frac[:, None] - offs[None, :].astype(x.dtype))
            taps = signal[:, idx]
            return jnp.einsum('bpk,pk->bp', taps, w)

        def _apply_kernels(x):
            poly = (x + 1.3) ** 2
            gauss = jnp.exp(-0.5 * ((x - 0.7) / 1.0) ** 2)
            return 0.5 * poly + 0.5 * gauss

        def soft_minimum(a, b, temperature):
            b = jnp.broadcast_to(b, a.shape)
            stacked = jnp.stack([-a * temperature, -b * temperature], axis=0)
            return -jax.nn.logsumexp(stacked, axis=0) / temperature

        def _forward(signal):
            interp = cubic_interpolate_1d(signal, INTERP_FACTOR)
            n = interp.shape[1]
            n_windows = (n - WINDOW) // STEP + 1
            starts = jnp.arange(n_windows) * STEP
            idx = starts[:, None] + jnp.arange(WINDOW)[None, :]
            windows = interp[:, idx]
            kw = _apply_kernels(windows)
            M = jnp.abs(jnp.fft.fft(kw, axis=-1))
            Mmax = jnp.max(M, axis=-1, keepdims=True)
            thr = ALPHA * Mmax
            mask = jax.nn.sigmoid((M - thr) * TEMP)
            Mt = M * mask
            return soft_minimum(Mt, BETA * Mmax, TEMP)
        return _forward(signal)

    def _L0_attn_ref(x, Wq, Wkv, Wout, bout, Wg, bg, lq1, lk1, lq2, lk2, ln_gamma, ln_beta):
        import jax, jax.numpy as jnp
        import numpy as np
        import math
        H = 8
        DH = 16
        DEPTH = 1
        LAMBDA_INIT = 0.8 - 0.6 * math.exp(-0.3 * DEPTH)
        LN_EPS = 1e-05
        b, n, dim = x.shape
        scale = DH ** (-0.5)
        q = x @ Wq
        kv = x @ Wkv
        k, v = jnp.split(kv, 2, axis=-1)
        q = q.reshape(b, n, 2 * H, DH).transpose(0, 2, 1, 3) * scale
        k = k.reshape(b, n, 2 * H, DH).transpose(0, 2, 1, 3)
        v = v.reshape(b, n, H, 2 * DH).transpose(0, 2, 1, 3)
        dots = jnp.einsum('bhid,bhjd->bhij', q, k)
        attn = jax.nn.softmax(dots, axis=-1)
        lam1 = jnp.exp(jnp.sum(lq1 * lk1))
        lam2 = jnp.exp(jnp.sum(lq2 * lk2))
        lam = lam1 - lam2 + LAMBDA_INIT
        attn = attn.reshape(b, H, 2, n, n)
        attn = attn[:, :, 0] - lam * attn[:, :, 1]
        out = jnp.einsum('bhij,bhjd->bhid', attn, v)
        mu = jnp.mean(out, axis=-1, keepdims=True)
        var = jnp.var(out, axis=-1, keepdims=True)
        out = (out - mu) * jax.lax.rsqrt(var + LN_EPS) * ln_gamma + ln_beta
        out = out * (1.0 - LAMBDA_INIT)
        out = out.transpose(0, 2, 1, 3).reshape(b, n, H * 2 * DH)
        gates = x @ Wg + bg
        out = out * jax.nn.sigmoid(gates)
        return out @ Wout + bout

    def _L0_ffn_ref(x, Wr, br, W1, b1, W2, b2, gamma, beta):
        import math
        import jax, jax.numpy as jnp
        import numpy as np
        CAPACITY_FACTOR = 1.25
        TOP_K = 2
        LN_EPS = 1e-05

        def _layer_norm(x, gamma, beta):
            mu = jnp.mean(x, axis=-1, keepdims=True)
            var = jnp.var(x, axis=-1, keepdims=True)
            return (x - mu) * jax.lax.rsqrt(var + LN_EPS) * gamma + beta
        B, S, D = x.shape
        E = Wr.shape[1]
        N = B * S
        K = TOP_K
        logits = jnp.mean(x, axis=1) @ Wr + br
        routing_weights = jax.nn.softmax(logits, axis=-1)
        capacity = float(math.ceil(N * CAPACITY_FACTOR / E))
        expected_loads = routing_weights.sum(axis=0) * (N / B)
        scale = jnp.where(expected_loads > capacity, capacity / expected_loads, 1.0)
        routing_weights = jax.nn.softmax(routing_weights * scale, axis=-1)
        rw_tok = jnp.broadcast_to(routing_weights[:, None, :], (B, S, E)).reshape(N, E)
        top_w, top_i = jax.lax.top_k(rw_tok, K)
        top_w = jax.nn.softmax(top_w, axis=-1)
        xf = x.reshape(N, D)
        h = jax.nn.gelu(jnp.einsum('nd,edf->enf', xf, W1) + b1[:, None, :], approximate=False)
        y = jnp.einsum('enf,efd->end', h, W2) + b2[:, None, :]
        w_dense = jnp.zeros((N, E), x.dtype).at[jnp.arange(N)[:, None], top_i].add(top_w)
        out = jnp.einsum('ne,end->nd', w_dense, y).reshape(B, S, D)
        out = _layer_norm(out + x, gamma, beta)
        return out

    def _L1_attn_ref(x, Wk, bk, Wq, bq, Wv, bv, Wr, br):
        import jax, jax.numpy as jnp
        import numpy as np
        import math
        N, HW, D = (8, 4096, 64)
        HEADS = 8
        n, hw, d = x.shape
        heads = HEADS
        hk = d // heads
        hv = d // heads
        flat = x.reshape(n, d, hw)
        keys = jnp.einsum('kd,ndl->nkl', Wk, flat) + bk[None, :, None]
        queries = jnp.einsum('kd,ndl->nkl', Wq, flat) + bq[None, :, None]
        values = jnp.einsum('vd,ndl->nvl', Wv, flat) + bv[None, :, None]
        K = jax.nn.softmax(keys.reshape(n, heads, hk, hw), axis=3)
        Q = jax.nn.softmax(queries.reshape(n, heads, hk, hw), axis=2)
        V = values.reshape(n, heads, hv, hw)
        context = jnp.einsum('nhkl,nhvl->nhkv', K, V)
        att = jnp.einsum('nhkv,nhkl->nhvl', context, Q)
        agg = att.reshape(n, heads * hv, hw)
        out = jnp.einsum('dv,nvl->ndl', Wr, agg) + br[None, :, None]
        return out.reshape(n, hw, d)

    def _L1_ffn_ref(x, sW1, sb1, sW2, sb2, sW3, sb3, eW1, eb1, eW2, eb2, eW3, eb3, gW, gb):
        import jax, jax.numpy as jnp
        import numpy as np
        B, A = (1024, 8)
        IN, OUT = (64, 64)
        SH1, SH2 = (64, 128)
        EH1, EH2 = (128, 64)
        E, TOPK = (4, 2)

        def _shared_mlp(x, W1, b1, W2, b2, W3, b3):
            h = jax.nn.relu(x @ W1 + b1)
            h = jax.nn.relu(h @ W2 + b2)
            return h @ W3 + b3

        def _experts_mlp(x, eW1, eb1, eW2, eb2, eW3, eb3):
            h = jax.nn.relu(jnp.einsum('baf,efh->ebah', x, eW1) + eb1[:, None, None, :])
            h = jax.nn.relu(jnp.einsum('ebah,ehg->ebag', h, eW2) + eb2[:, None, None, :])
            o = jnp.einsum('ebag,ego->ebao', h, eW3) + eb3[:, None, None, :]
            return jnp.moveaxis(o, 0, -1)
        all_out = _experts_mlp(x, eW1, eb1, eW2, eb2, eW3, eb3)
        shared = _shared_mlp(x, sW1, sb1, sW2, sb2, sW3, sb3)
        gates = jax.nn.softmax(x @ gW + gb, axis=-1)
        topv, topi = jax.lax.top_k(gates, TOPK)
        topw = jax.nn.softmax(topv, axis=-1)
        sel = jnp.take_along_axis(all_out, topi[:, :, None, :], axis=-1)
        gated = jnp.sum(sel * topw[:, :, None, :], axis=-1)
        return shared + gated
    h = _L0_tok_ref(x)
    h = h + _L0_attn_ref(_layernorm(h, axis=-1), L0_attn_Wq, L0_attn_Wkv, L0_attn_Wout, L0_attn_bout, L0_attn_Wg, L0_attn_bg, L0_attn_lq1, L0_attn_lk1, L0_attn_lq2, L0_attn_lk2, L0_attn_ln_gamma, L0_attn_ln_beta)
    h = h + _L0_ffn_ref(_layernorm(h, axis=-1), L0_ffn_Wr, L0_ffn_br, L0_ffn_W1, L0_ffn_b1, L0_ffn_W2, L0_ffn_b2, L0_ffn_gamma, L0_ffn_beta)
    h = h + _L1_attn_ref(_layernorm(h, axis=-1), L1_attn_Wk, L1_attn_bk, L1_attn_Wq, L1_attn_bq, L1_attn_Wv, L1_attn_bv, L1_attn_Wr, L1_attn_br)
    h = h + _L1_ffn_ref(_layernorm(h, axis=-1), L1_ffn_sW1, L1_ffn_sb1, L1_ffn_sW2, L1_ffn_sb2, L1_ffn_sW3, L1_ffn_sb3, L1_ffn_eW1, L1_ffn_eb1, L1_ffn_eW2, L1_ffn_eb2, L1_ffn_eW3, L1_ffn_eb3, L1_ffn_gW, L1_ffn_gb)
    return h

_drawn_inputs = setup_inputs


def setup_inputs(seed=0):
    import zlib

    import numpy as np

    out = dict(_drawn_inputs(seed))
    spreads = {'L0_attn_bout': (0.0, 0.8),
     'L0_attn_bg': (1.0, 0.6),
     'L0_attn_ln_gamma': (1.0, 0.6),
     'L0_attn_ln_beta': (0.0, 0.8),
     'L0_ffn_br': (0.0, 0.369),
     'L0_ffn_b1': (0.0, 0.8),
     'L0_ffn_b2': (0.0, 0.8),
     'L0_ffn_gamma': (1.0, 0.6),
     'L0_ffn_beta': (0.0, 0.8),
     'L1_ffn_sb1': (0.0, 0.8),
     'L1_ffn_sb2': (0.0, 0.8),
     'L1_ffn_sb3': (0.0, 2.0),
     'L1_ffn_eb1': (0.0, 0.8),
     'L1_ffn_eb2': (0.0, 2.0),
     'L1_ffn_eb3': (0.0, 2.0),
     'L1_ffn_gb': (0.0, 0.8)}
    factors = {'L0_attn_Wq': 8.0,
     'L0_attn_Wg': 8.0,
     'L0_attn_lq1': 8.0,
     'L0_attn_lk1': 8.0,
     'L0_attn_lq2': 8.0,
     'L0_attn_lk2': 8.0,
     'L1_attn_Wk': 7.046,
     'L1_attn_bk': 200.0,
     'L1_attn_Wq': 8.0,
     'L1_attn_bq': 8.0,
     'L1_attn_Wv': 6.8,
     'L1_attn_bv': 27.687,
     'L1_attn_Wr': 7.79,
     'L1_attn_br': 200.0,
     'L1_ffn_sW1': 8.0,
     'L1_ffn_sW2': 8.0,
     'L1_ffn_sW3': 8.0,
     'L1_ffn_eW1': 8.0,
     'L1_ffn_eW2': 8.0,
     'L1_ffn_eW3': 8.0,
     'L1_ffn_gW': 8.0}
    for name, (base, spread) in spreads.items():
        noise = np.random.default_rng([zlib.crc32(name.encode()), seed]).standard_normal(out[name].shape)
        drawn = base * np.exp(spread * noise) if base else spread * noise
        out[name] = jnp.asarray(drawn.astype(out[name].dtype))
    for name, factor in factors.items():
        out[name] = (out[name] * factor).astype(out[name].dtype)
    return out
```

```python
import math
from contextlib import ExitStack

import numpy as np

import concourse.bass as bass
from concourse import mybir

F32 = mybir.dt.float32
BF16 = mybir.dt.bfloat16
ALU = mybir.AluOpType
ACT = mybir.ActivationFunctionType
AX = mybir.AxisListType

B = 16
L = 4096
D = 64
UP = 4
NT = (L - 1) * UP // D
TP = 128
TILES = 2 * B
NTP = 2 * TP
LAST = NT - TP
HOP = D // UP
TAPS = HOP + 3
BINS = D // 2 + 1
EPS = 1e-5
SH = 16
DH = 16
VH = 32
LAMBDA_INIT = 0.8 - 0.6 * math.exp(-0.3)
NE = 8
FH = 128
CAPACITY = float(math.ceil(B * NT * 1.25 / NE))
PAIRS = B // 2
LK = 8
ME = 4
MH = 128
STACK = 6 * DH
EARLIER = 2 * B - 1
NUMBERS = EARLIER + NE * NE
HEADS = NUMBERS + NE
SELECT = HEADS + 128
EARLIER4 = SELECT + TILES
ROUTE_COLUMNS = EARLIER4 + ME * ME
MAXROWS = 3


def after(eng, sem, value):
    if isinstance(value, int) and value <= 0:
        return
    eng.wait_ge(sem, value)


def wait_apart(eng, sem, value, passed):
    if isinstance(value, int):
        after(eng, sem, value)
    else:
        eng.wait_ge(sem, value)
        eng.sem_inc(passed, 1)


class Chain:

    def __init__(self, eng, sem, at=0):
        self.eng, self.sem, self.at = eng, sem, at

    def step(self, instruction):
        instruction.then_inc(self.sem, 1)
        self.at = self.at + 1

    def wait(self):
        self.eng.wait_ge(self.sem, self.at)

    def link(self, instruction):
        self.step(instruction)
        self.wait()


def shape_constants():
    A = -0.75

    def near(t):
        return ((A + 2) * t - (A + 3)) * t * t + 1

    def far(t):
        return ((A * t - 5 * A) * t + 8 * A) * t - 4 * A

    def near_slope(t):
        return (3 * (A + 2) * t - 2 * (A + 3)) * t

    def far_slope(t):
        return (3 * A * t - 10 * A) * t + 8 * A

    taps = np.zeros((2, TAPS, D))
    for p in range(D):
        f = (p % UP) / UP
        for off, value, slope in ((-1, far(1 + f), far_slope(1 + f)), (0, near(f), near_slope(f)),
                                  (1, near(1 - f), -near_slope(1 - f)), (2, far(2 - f), -far_slope(2 - f))):
            taps[0, p // UP + off + 1, p] += value
            taps[1, p // UP + off + 1, p] += slope
    quad = np.zeros((128, 4, 128), np.float32)
    for kind in range(2):
        for tile in range(4):
            u, i = divmod(tile, 2)
            quad[32 * tile:32 * tile + TAPS, 2 * kind + u, 64 * i:64 * i + 64] = taps[kind]
    n = (L - 1) * UP + 1
    steps = np.arange(n - 1, dtype=np.float32) * (np.float32(1) / np.float32(n - 1))
    at = np.concatenate([steps, np.ones(1, np.float32)]) * np.float32(L - 1)
    shift = np.zeros((128, TP), np.float32)
    for i in range(2):
        for t in range(TP if i == 0 else LAST):
            p = D * (TP * i + t) + np.arange(D)
            shift[64 * i:64 * i + 64, t] = at[p].astype(np.float64) - p / UP
    dft = np.zeros((128, 128), np.float32)
    angle = 2 * np.pi * np.outer(np.arange(D), np.arange(BINS)) / D
    one = 0.5 * np.concatenate([np.cos(angle), np.sin(angle[:, 1:BINS - 1])], axis=1)
    dft[:64, :64] = dft[64:, 64:] = one
    mean = np.kron(np.eye(128 // VH), np.full((VH, VH), 1.0 / VH))
    center = np.stack([np.eye(128) - mean, mean], axis=1).astype(np.float32)
    route = np.zeros((128, ROUTE_COLUMNS), np.float32)
    route[:, B - 1] = 1.0 / NT
    route[:, EARLIER:EARLIER + NE * NE] = np.tril(np.ones((NE, NE)), -1).ravel()
    route[:, NUMBERS:NUMBERS + NE] = np.arange(NE)
    route[:, HEADS:HEADS + 128] = np.kron(np.eye(128 // LK), np.ones((LK, LK)))
    route[:, SELECT:SELECT + TILES] = np.kron(np.eye(TILES), np.ones((ME, 1)))
    route[:, EARLIER4:EARLIER4 + ME * ME] = np.tril(np.ones((ME, ME)), -1).ravel()
    return {"c_route": route, "c_ident": np.eye(128, dtype=np.float32), "c_taps": quad, "c_shift": shift, "c_dft": dft, "c_center": center}


def build_tower(nc, x, k64, wout, bout, bg, lq1, lk1, lq2, lk2, ln_gamma, ln_beta,
                f_wr, f_br, f_b1, f_w2, f_b2, f_gamma, f_beta,
                a_wk, a_bk, a_wq, a_bq, a_wv, a_bv, a_wr, a_br,
                m_sb1, m_sw2, m_sb2, m_sw3, m_sb3, m_eb1, m_ew2, m_eb2, m_ew3, m_eb3, m_gb,
                c_ident, c_taps, c_shift, c_dft, c_center, c_route, out):
    NQKVG = 4 * 256
    NW1 = NE * FH
    NM1 = D + ME * MH + ME
    NK64 = NQKVG + NW1 + NM1
    KQ = TILES // 4

    with ExitStack() as ctx:
        def sb(name, shape, dt=F32):
            return ctx.enter_context(nc.sbuf_tensor(name, shape, dt))

        signals = []

        def sem(name):
            signals.append(nc.alloc_semaphore(name=name))
            return signals[-1]

        def end_stages():
            nc.clear_and_free_semaphores(signals)
            signals.clear()
            nc.all_engine_barrier()

        PS = ctx.enter_context(nc.psum_tensor("PS", [128, 8, 512], F32))

        def bank_bf16(k):
            return PS[:, k, :].bitcast(BF16)

        H = sb("H", [128, TILES, D])
        XT = sb("XT", [128, 2, B * NTP], BF16)
        SG = sb("SG", [128, 2, B * NTP])
        ident = sb("ident", [128, 128])
        identb = sb("identb", [128, 128], BF16)
        taps = sb("taps", [128, 4, 128])
        shift = sb("shift", [128, TP])
        dft = sb("dft", [128, 128])
        center = sb("center", [128, 2, 128])
        bias = sb("bias", [128, 8])
        WS = sb("WS", [128, 3, NK64], BF16)
        WO = sb("WO", [128, 2, D])
        BO = sb("BO", [128, D])
        BG = sb("BG", [128, 2])
        LV = sb("LV", [128, 4, DH])
        LS = sb("LS", [128, 8])
        GB = sb("GB", [128, 4])
        st = sb("st", [128, 6, TILES])

        scratch = nc.dram_tensor("parts_scratch", (2, 2, 3, 2, DH, 8, NTP), BF16).ap()

        consts_in = sem("consts_in"); ident_in = sem("ident_in"); windows_in = sem("windows_in"); weights_in = sem("weights_in")
        small_in = sem("small_in")
        windows_zeroed = sem("windows_zeroed"); consts_made = sem("consts_made")
        windows_turned = sem("windows_turned"); windows_copied = sem("windows_copied")
        interpolated = sem("interpolated"); points_ready = sem("points_ready")
        terms_ready = sem("terms_ready"); kernels_ready = sem("kernels_ready")
        spectrum_done = sem("spectrum_done"); squares_ready = sem("squares_ready")
        power_ready = sem("power_ready"); magnitude_ready = sem("magnitude_ready")
        excess_ready = sem("excess_ready"); mask_ready = sem("mask_ready")
        gap_ready = sem("gap_ready"); log_ready = sem("log_ready")
        centered = sem("centered"); csq_ready = sem("csq_ready"); var_ready = sem("var_ready")
        rstd_ready = sem("rstd_ready"); normed = sem("normed"); x1_ready = sem("x1_ready")
        rest_ready = sem("rest_ready"); x2_ready = sem("x2_ready"); x_split = sem("x_split")
        x_turned = sem("x_turned"); xt0_copied = sem("xt0_copied"); xt1_copied = sem("xt1_copied")
        weights_split = sem("weights_split"); gates_done = sem("gates_done"); gates_used = sem("gates_used")
        lam_products = sem("lam_products"); lam_exps = sem("lam_exps"); bout_added = sem("bout_added")
        vec_chain = sem("vec_chain"); act_chain = sem("act_chain"); pool_chain = sem("pool_chain")
        q_done = sem("q_done"); k_done = sem("k_done"); v_done = sem("v_done")
        q1_ready = sem("q1_ready"); k1_ready = sem("k1_ready")
        q_rest = sem("q_rest"); k_rest = sem("k_rest"); v_copied = sem("v_copied")
        q_parts = sem("q_parts"); k_parts = sem("k_parts")
        q_written = sem("q_written"); k_written = sem("k_written")
        stacks_in = [sem("stacks_in_even"), sem("stacks_in_odd")]
        scores_done = sem("scores_done"); maxes_taken = sem("maxes_taken")
        max_parts = sem("max_parts"); max_turned = sem("max_turned"); max_copied = sem("max_copied")
        max_rows_in = sem("max_rows_in")
        scoresT_done = sem("scoresT_done"); exps_ready = sem("exps_ready")
        quad_done = sem("quad_done"); inv_ready = sem("inv_ready"); quad_scaled = sem("quad_scaled")
        heads_out = sem("heads_out"); xc_done = sem("xc_done"); xc_copied = sem("xc_copied")
        xcsq_ready = sem("xcsq_ready"); var_done = sem("var_done"); hrstd_ready = sem("hrstd_ready")
        head_normed = sem("head_normed"); gated = sem("gated"); wout_done = sem("wout_done")
        h_updated = sem("h_updated"); act_chain2 = sem("act_chain2"); act_logs = sem("act_logs")
        max_chain = sem("max_chain"); part_chain = sem("part_chain"); gate_chain = sem("gate_chain"); ones_made = sem("ones_made")

        one = ExitStack()
        with one:
            def sa(name, shape, dt=F32):
                return one.enter_context(nc.sbuf_tensor(name, shape, dt))
            W = sa("W", [128, TILES, 32])
            SW = sa("SW", [128, KQ, TP])
            TX = sa("TX", [128, 2, KQ, TP])
            TP2 = sa("TP2", [128, 2, KQ, TP])
            TG = sa("TG", [128, 2, KQ, TP])
            SQ = sa("SQ", [128, TILES, D])
            MG = sa("MG", [128, TILES, BINS])
            MZ = sa("MZ", [128, TILES, BINS])
            ML = sa("ML", [128, TILES, BINS])
            XC = sa("XC", [128, TILES, D])
            XS = sa("XS", [128, TILES, 3 * D], BF16)
            WF = sa("WF", [128, NK64])
            WR = sa("WR", [128, NK64])

            block = one.enter_context(nc.Block("front"))

            @block.sync
            def _(sp):
                sp.wait_ge(windows_zeroed, 1)
                def src(offset, n, width):
                    return bass.AP(tensor=x.tensor, offset=offset, ap=[[HOP, n], [L, B], [1, width]])
                tiles = W[:].rearrange("p (b j) s -> p j b s", j=2)
                for lo, hi in ((0, 112), (112, LAST)):
                    sp.dma_start(tiles[1 + lo:1 + hi, 0, :, 0:TAPS], src(HOP * (1 + lo) - 1, hi - lo, TAPS)).then_inc(windows_in, 16)
                    sp.dma_start(tiles[lo:hi, 1, :, 0:TAPS], src(HOP * (TP + lo) - 1, hi - lo, TAPS)).then_inc(windows_in, 16)
                sp.dma_start(tiles[0:1, 0, :, 1:TAPS], src(0, 1, TAPS - 1)).then_inc(windows_in, 16)
                sp.dma_start(tiles[0:1, 0, :, 0:1], src(0, 1, 1), allow_slow_non_contiguous=True).then_inc(windows_in, 16)
                for half in (0, 64):
                    sp.dma_start(WF[half:half + 64, :], k64).then_inc(weights_in, 16)
                sp.dma_start(WO[:], wout.rearrange("(g p) n -> p g n", g=2)).then_inc(small_in, 16)
                sp.dma_start(BO[:], bass.AP(tensor=bout.tensor, offset=0, ap=[[0, 128], [1, D]])).then_inc(small_in, 16)
                for n, v in enumerate((lq1, lk1, lq2, lk2)):
                    sp.dma_start(LV[:, n, :], bass.AP(tensor=v.tensor, offset=0, ap=[[0, 128], [1, DH]])).then_inc(small_in, 16)

            @block.scalar
            def _(act):
                nc.scalar.preload_act_table_set("natural_log_exp_and_others")
                act.dma_start(ident[:], c_ident).then_inc(ident_in, 16)
                act.dma_start(taps[:], c_taps).then_inc(consts_in, 16)
                act.dma_start(shift[:], c_shift).then_inc(consts_in, 16)
                act.dma_start(dft[:], c_dft).then_inc(consts_in, 16)
                act.dma_start(center[:], c_center).then_inc(consts_in, 16)
                act.dma_start(BG[:], bg.rearrange("(g p) -> p g", g=2), allow_slow_non_contiguous=True).then_inc(small_in, 16)
                for n, v in enumerate((ln_gamma, ln_beta)):
                    act.dma_start(GB[:, n:n + 1], bass.AP(tensor=v.tensor, offset=0, ap=[[0, 4], [1, VH], [1, 1]]), allow_slow_non_contiguous=True).then_inc(small_in, 16)
                chain = Chain(act, act_chain)
                for k in range(2):
                    act.wait_ge(windows_turned, k + 1)
                    nc.scalar.copy(SW[:, 4 * k:4 * k + 4, :], PS[:, k, :].rearrange("p (q t) -> p q t", q=4)).then_inc(windows_copied, 1)
                act.wait_ge(consts_made, 1)
                for s, (n, u) in enumerate(((0, 0), (0, 1), (1, 0), (1, 1))):
                    act.wait_ge(points_ready, s + 1)
                    part = (slice(None), u, slice(4 * n, 4 * n + 4), slice(None))
                    chain.step(nc.scalar.activation(TG[part], TX[part], ACT.Square, bias=bias[:, 0:1]))
                    chain.step(nc.scalar.activation(TP2[part], TX[part], ACT.Square, bias=bias[:, 1:2]))
                    chain.wait()
                    nc.scalar.activation(TG[part], TG[part], ACT.Exp, scale=-0.5).then_inc(terms_ready, 1)
                for k in range(4):
                    act.wait_ge(spectrum_done, k + 1)
                    nc.scalar.activation(SQ[:, 8 * k:8 * k + 8, :], PS[:, 2 + k, :].rearrange("p (t f) -> p t f", t=8), ACT.Square).then_inc(squares_ready, 1)
                halves = [slice(0, B), slice(B, TILES)]
                for n in range(2):
                    act.wait_ge(power_ready, n + 1)
                    nc.scalar.activation(MG[:, halves[n], :], SQ[:, halves[n], 0:BINS], ACT.Sqrt).then_inc(magnitude_ready, 1)
                for n in range(2):
                    act.wait_ge(excess_ready, n + 1)
                    nc.scalar.activation(MZ[:, halves[n], :], MZ[:, halves[n], :], ACT.Sigmoid).then_inc(mask_ready, 1)
                nc.scalar.preload_act_table_set("natural_log_exp_and_others")
                for n in range(2):
                    part = (slice(None), halves[n], slice(None))
                    act.wait_ge(gap_ready, n + 1)
                    chain.link(nc.scalar.activation(ML[part], ML[part], ACT.Abs))
                    chain.link(nc.scalar.activation(ML[part], ML[part], ACT.Exp, scale=-1.0))
                    nc.scalar.activation(ML[part], ML[part], ACT.Ln, bias=bias[:, 3:4]).then_inc(log_ready, 1)
                act.wait_ge(lam_products, 2)
                nc.scalar.activation(LS[:, 2:4], LS[:, 0:2], ACT.Exp).then_inc(lam_exps, 1)
                for n in range(2):
                    part = (slice(None), halves[n], slice(None))
                    act.wait_ge(centered, n + 1)
                    nc.scalar.activation(SQ[part], XC[part], ACT.Square).then_inc(csq_ready, 1)
                    act.wait_ge(var_ready, n + 1)
                    chain.link(nc.scalar.activation(st[:, 2, halves[n]], st[:, 1, halves[n]], ACT.Ln, scale=1.0 / D, bias=bias[:, 2:3]))
                    nc.scalar.activation(st[:, 3, halves[n]], st[:, 2, halves[n]], ACT.Exp, scale=-0.5).then_inc(rstd_ready, 1)
                for n in range(2):
                    act.wait_ge(normed, n + 1)
                    nc.scalar.copy(XS[:, halves[n], D:2 * D], XC[:, halves[n], :]).then_inc(x1_ready, 1)
                    act.wait_ge(rest_ready, n + 1)
                    nc.scalar.copy(XS[:, halves[n], 0:D], XC[:, halves[n], :]).then_inc(x2_ready, 1)
                for k in range(4):
                    act.wait_ge(x_turned, 2 * k + 1)
                    nc.scalar.copy(XT[:, 0, 1024 * k:1024 * k + 1024], bank_bf16(k)).then_inc(xt0_copied, 1)
                for n in range(8):
                    for m in range(2):
                        act.wait_ge(gates_done, 2 * n + m + 1)
                        nc.scalar.activation(SG[:, m, 512 * n:512 * n + 512], PS[:, (2 * n + m) % 8, :], ACT.Sigmoid, bias=BG[:, m:m + 1]).then_inc(gates_used, 1)

            @block.gpsimd
            def _(pool):
                nc.gpsimd.memset(W[:], 0.0).then_inc(windows_zeroed, 1)
                for n, value in enumerate((-0.7, 1.3, EPS, 1.0)):
                    m = nc.gpsimd.memset(bias[:, n:n + 1], value)
                m.then_inc(consts_made, 1)
                pool.wait_ge(ident_in, 16)
                nc.gpsimd.tensor_copy(identb[:], ident[:]).then_inc(consts_made, 1)
                chain = Chain(pool, pool_chain)
                pool.wait_ge(weights_in, 32)
                for n, (lo, hi) in enumerate(((0, NQKVG), (NQKVG, NK64))):
                    chain.link(nc.gpsimd.tensor_copy(WS[:, 0, lo:hi], WF[:, lo:hi]))
                    chain.link(nc.gpsimd.tensor_tensor(WR[:, lo:hi], WF[:, lo:hi], WS[:, 0, lo:hi], ALU.subtract))
                    chain.link(nc.gpsimd.tensor_copy(WS[:, 1, lo:hi], WR[:, lo:hi]))
                    chain.link(nc.gpsimd.tensor_tensor(WS[0:64, 2, lo:hi], WR[0:64, lo:hi], WS[0:64, 1, lo:hi], ALU.subtract))
                    nc.gpsimd.tensor_copy(WS[64:128, 2, lo:hi], WS[64:128, 0, lo:hi]).then_inc(weights_split, 1)
                    pool.wait_ge(weights_split, n + 1)
                pool.wait_ge(small_in, 16 * 9)
                pool.wait_ge(centered, 2)
                chain.step(nc.gpsimd.tensor_scalar(GB[:, 2:4], GB[:, 0:2], 1.0 - LAMBDA_INIT, None, ALU.mult))
                nc.gpsimd.tensor_tensor(H[:], H[:], BO[:].unsqueeze(1).broadcast_to([128, TILES, D]), ALU.add).then_inc(bout_added, 1)

            @block.tensor
            def _(pe):
                pe.wait_ge(ident_in, 16); pe.wait_ge(consts_in, 64)
                pe.wait_ge(windows_in, 16 * 6)
                for q in range(KQ):
                    t = nc.tensor.transpose(PS[:, q // 4, 128 * (q % 4):128 * (q % 4) + 128], W[:, 4 * q:4 * q + 4, :], ident[:])
                    if q % 4 == 3:
                        t.then_inc(windows_turned, 1)
                for n in range(2):
                    pe.wait_ge(windows_copied, 2 if n else 1)
                    for u in range(2):
                        value, slope = ((2 + u, 4 + u), (6 + u, u))[n]
                        rhs = SW[:, 4 * n:4 * n + 4, :]
                        nc.tensor.matmul(PS[:, value, :], taps[:, u, :], rhs, start=True, stop=True)
                        nc.tensor.matmul(PS[:, slope, :], taps[:, 2 + u, :], rhs, start=True, stop=True).then_inc(interpolated, 1)
                for q in range(KQ):
                    for u in range(2):
                        pe.wait_ge(kernels_ready, 2 * (q // 4) + u + 1)
                        t = nc.tensor.matmul(PS[:, 2 + q // 2, 128 * (2 * (q % 2) + u):128 * (2 * (q % 2) + u) + 128],
                                             TX[:, u, q, :], dft[:], start=True, stop=True)
                    if q % 2:
                        t.then_inc(spectrum_done, 1)
                pe.wait_ge(consts_made, 2)
                for k in range(4):
                    if k % 2 == 0:
                        pe.wait_ge(x_split, k // 2 + 1)
                    for kind in range(2):
                        for t in range(8):
                            m = nc.tensor.transpose(bank_bf16(4 * kind + k)[:, 128 * t:128 * t + 128],
                                                    XS[:, 8 * k + t, D * kind:D * kind + 128], identb[:])
                        m.then_inc(x_turned, 1)
                pe.wait_ge(weights_split, 1)
                for n in range(8):
                    for m in range(2):
                        use = 2 * n + m
                        if use < 8:
                            pe.wait_ge(xt0_copied, 4)
                            pe.wait_ge(xt1_copied, 4)
                        else:
                            pe.wait_ge(gates_used, use - 7)
                        cols = slice(768 + 128 * m, 896 + 128 * m)
                        for s in range(3):
                            mm = nc.tensor.matmul(PS[:, use % 8, :], WS[:, s, cols], XT[:, s // 2, 512 * n:512 * n + 512], start=(s == 0), stop=(s == 2))
                        mm.then_inc(gates_done, 1)

            @block.vector
            def _(vec):
                chain = Chain(vec, vec_chain)
                vec.wait_ge(small_in, 16 * 9)
                for n in range(2):
                    chain.link(nc.vector.tensor_tensor(LV[:, 2 * n, :], LV[:, 2 * n, :], LV[:, 2 * n + 1, :], ALU.mult))
                    nc.vector.tensor_reduce(LS[:, n:n + 1], LV[:, 2 * n, :], AX.X, ALU.add).then_inc(lam_products, 1)
                vec.wait_ge(consts_in, 64)
                sh = shift[:].unsqueeze(1).broadcast_to([128, 4, TP])
                for s, (n, u) in enumerate(((0, 0), (0, 1), (1, 0), (1, 1))):
                    value, slope = ((2 + u, 4 + u), (6 + u, u))[n]
                    part = (slice(None), u, slice(4 * n, 4 * n + 4), slice(None))
                    vec.wait_ge(interpolated, s + 1)
                    chain.link(nc.vector.tensor_tensor(TP2[part], PS[:, slope, :].rearrange("p (q t) -> p q t", q=4), sh, ALU.mult))
                    nc.vector.tensor_tensor(TX[part], PS[:, value, :].rearrange("p (q t) -> p q t", q=4), TP2[part], ALU.add).then_inc(points_ready, 1)
                for s, (n, u) in enumerate(((0, 0), (0, 1), (1, 0), (1, 1))):
                    part = (slice(None), u, slice(4 * n, 4 * n + 4), slice(None))
                    vec.wait_ge(terms_ready, s + 1)
                    nc.vector.tensor_tensor(TX[part], TP2[part], TG[part], ALU.add).then_inc(kernels_ready, 1)
                halves = [slice(0, B), slice(B, TILES)]
                for n in range(2):
                    vec.wait_ge(squares_ready, 2 * n + 2)
                    nc.vector.tensor_tensor(SQ[:, halves[n], 1:BINS - 1], SQ[:, halves[n], 1:BINS - 1], SQ[:, halves[n], BINS:D], ALU.add).then_inc(power_ready, 1)

                def peak(n):
                    return st[:, 0, halves[n]].unsqueeze(2).broadcast_to([128, B, BINS])

                for n in range(2):
                    vec.wait_ge(magnitude_ready, n + 1)
                    chain.link(nc.vector.tensor_reduce(st[:, 0, halves[n]], MG[:, halves[n], :], AX.X, ALU.max))
                    nc.vector.scalar_tensor_tensor(out=MZ[:, halves[n], :], in0=peak(n), scalar=-0.12, in1=MG[:, halves[n], :], op0=ALU.mult, op1=ALU.add).then_inc(excess_ready, 1)
                for n in range(2):
                    part = (slice(None), halves[n], slice(None))
                    vec.wait_ge(mask_ready, n + 1)
                    chain.link(nc.vector.tensor_tensor(MG[part], MG[part], MZ[part], ALU.mult))
                    nc.vector.scalar_tensor_tensor(out=ML[part], in0=peak(n), scalar=-0.9, in1=MG[part], op0=ALU.mult, op1=ALU.add).then_inc(gap_ready, 1)
                    chain.step(nc.vector.scalar_tensor_tensor(out=MZ[part], in0=peak(n), scalar=0.9, in1=MG[part], op0=ALU.mult, op1=ALU.min))
                chain.wait()
                for n in range(2):
                    vec.wait_ge(log_ready, n + 1)
                    chain.step(nc.vector.tensor_tensor(H[:, halves[n], 0:BINS], MZ[:, halves[n], :], ML[:, halves[n], :], ALU.subtract))
                    chain.link(nc.vector.tensor_tensor(H[:, halves[n], BINS:D], MZ[:, halves[n], BINS - 2:0:-1], ML[:, halves[n], BINS - 2:0:-1], ALU.subtract))
                    chain.link(nc.vector.tensor_reduce(st[:, 0, halves[n]], H[:, halves[n], :], AX.X, ALU.add))
                    nc.vector.scalar_tensor_tensor(out=XC[:, halves[n], :], in0=st[:, 0, halves[n]].unsqueeze(2).broadcast_to([128, B, D]), scalar=-1.0 / D,
                                                   in1=H[:, halves[n], :], op0=ALU.mult, op1=ALU.add).then_inc(centered, 1)
                for n in range(2):
                    vec.wait_ge(csq_ready, n + 1)
                    nc.vector.tensor_reduce(st[:, 1, halves[n]], SQ[:, halves[n], :], AX.X, ALU.add).then_inc(var_ready, 1)
                for n in range(2):
                    vec.wait_ge(rstd_ready, n + 1)
                    nc.vector.tensor_tensor(XC[:, halves[n], :], XC[:, halves[n], :], st[:, 3, halves[n]].unsqueeze(2).broadcast_to([128, B, D]), ALU.mult).then_inc(normed, 1)
                for n in range(2):
                    part = (slice(None), halves[n], slice(None))
                    vec.wait_ge(x1_ready, n + 1)
                    nc.vector.tensor_tensor(XC[part], XC[part], XS[:, halves[n], D:2 * D], ALU.subtract).then_inc(rest_ready, 1)
                    vec.wait_ge(x2_ready, n + 1)
                    nc.vector.tensor_tensor(XS[:, halves[n], 2 * D:3 * D], XC[part], XS[:, halves[n], 0:D], ALU.subtract).then_inc(x_split, 1)
                vec.wait_ge(lam_exps, 1)
                chain.link(nc.vector.tensor_tensor(LS[:, 4:5], LS[:, 3:4], LS[:, 2:3], ALU.subtract))
                chain.link(nc.vector.tensor_scalar(LS[:, 5:6], LS[:, 4:5], -LAMBDA_INIT, None, ALU.add))
                for k in range(4):
                    vec.wait_ge(x_turned, 2 * k + 2)
                    nc.vector.tensor_copy(XT[:, 1, 1024 * k:1024 * k + 1024], bank_bf16(4 + k)).then_inc(xt1_copied, 1)


        with ExitStack() as two:
            def sa(name, shape, dt=F32):
                return two.enter_context(nc.sbuf_tensor(name, shape, dt))
            QP = [sa(f"QP{p}", [128, 2, 3, 2, NTP], BF16) for p in range(2)]
            QR = sa("QR", [128, 2, 2, NTP])
            QS = [sa(f"QS{p}", [STACK + MAXROWS, SH, NTP], BF16) for p in range(2)]
            KS = [sa(f"KS{p}", [STACK + MAXROWS, SH, NTP], BF16) for p in range(2)]
            NM = sa("NM", [128, SH, 2])
            NP = sa("NP", [128, 2, 3, SH], BF16)
            NR = sa("NR", [128, 2, SH])
            MT = sa("MT", [3 * SH, 2, TP], BF16)
            EX = [sa(f"EX{p}", [128, 4, 2, NTP]) for p in range(2)]
            V = [sa(f"V{p}", [128, 2, 8 * VH]) for p in range(2)]
            ones = sa("ones", [128, VH])
            IN = [sa(f"IN{p}", [128, NTP]) for p in range(2)]
            AH = sa("AH", [128, 4, NTP])
            O = sa("O", [128, 2, NTP])
            XB = sa("XB", [128, 2, NTP])
            XQ = sa("XQ", [128, 2, NTP])
            RS = sa("RS", [128, 2, NTP])
            Y = sa("Y", [128, 2, NTP])
            Y2 = sa("Y2", [128, 2, NTP])
            U = sa("U", [128, 2, NTP])

            pe_passed = sem("pe_passed"); pool_passed = sem("pool_passed"); sp_passed = sem("sp_passed")
            stack_in = [[sem(f"stack_in_{p}{h}") for h in range(2)] for p in range(2)]
            ORDER = [2 * (4 * g + j) + odd for g in range(2) for odd in range(2) for j in range(4)]

            class Signal:

                def __init__(self, i, c):
                    self.n = i * 2 + c if not isinstance(i, int) or i else c
                    self.p = c % 2
                    self.pair = i + c // 2 if not isinstance(i, int) or i or c >= 2 else 0
                    self.i, self.c = i, c

                def next(self, k):
                    return Signal(self.i, self.c + k)

            def upto(value, most=B):
                return min(value, most) if isinstance(value, int) else value

            def schedule(eng, prologue, step, epilogue):
                prologue()
                step(Signal(0, 0), True, True, False)
                step(Signal(0, 1), True, True, True)
                with eng.Fori(0, B // 2 - 2) as i:
                    step(Signal(i, 2), True, True, True)
                    step(Signal(i, 3), True, True, True)
                step(Signal(0, 14), False, True, True)
                step(Signal(0, 15), False, False, True)
                epilogue()

            block = two.enter_context(nc.Block("attention"))

            @block.sync
            def _(sp):
                def stack(t):
                    q_sc, k_sc = scratch[t.p, 0], scratch[t.p, 1]
                    for h in range(2):
                        wait_apart(sp, stack_in[t.p][h], t.pair * 96, sp_passed)
                    sp.wait_ge(q_parts, t.n + 1)
                    sp.dma_start(q_sc.rearrange("s g d h t -> (d h) (s g) t"), QP[t.p][:, 0].rearrange("p s g t -> p (s g) t")).then_inc(q_written, 16)
                    sp.wait_ge(k_parts, t.n + 1)
                    sp.dma_start(k_sc.rearrange("s g d h t -> (d h) (s g) t"), QP[t.p][:, 1].rearrange("p s g t -> p (s g) t")).then_inc(k_written, 16)
                    sp.wait_ge(q_written, (t.n + 1) * 16)
                    sp.wait_ge(k_written, (t.n + 1) * 16)
                    part = 2 * DH * 8 * NTP
                    for g in range(2):
                        after(sp, scoresT_done, (t.n - 2) * 16 + 8 * (g + 1))
                        heads = slice(8 * g, 8 * g + 8)
                        q0 = q_sc[0, g].offset
                        k0 = k_sc[0, g].offset
                        rows = 8 * NTP
                        for dst, base, first, reps, pstep, at in ((QS, q0, 0, 3, 0, 0), (QS, q0, 1, 2, 0, 3), (QS, q0, 2, 1, 0, 5),
                                                                  (KS, k0, 0, 3, part, 0), (KS, k0, 0, 2, part, 3), (KS, k0, 0, 1, part, 5)):
                            src = bass.AP(tensor=scratch.tensor, offset=base + first * part, ap=[[pstep, reps], [rows, DH], [1, rows]])
                            sp.dma_start(dst[t.p][DH * at:DH * (at + reps), heads, :], src).then_inc(stack_in[t.p][g], 16)

                def max_rows(t):
                    sp.wait_ge(max_copied, t.n + 1)
                    for s in range(3):
                        sp.dma_start(QS[t.p][STACK + s:STACK + s + 1, :, :], MT[SH * s:SH * s + SH, :, :].rearrange("h j t -> h (j t)")).then_inc(max_rows_in, 16)

                def prologue():
                    stack(Signal(0, 0))
                    stack(Signal(0, 1))

                def step(b, front, nxt, tail):
                    max_rows(b)
                    if front:
                        stack(b.next(2))

                schedule(sp, prologue, step, lambda: None)

            @block.tensor
            def _(pe):
                pe.wait_ge(ones_made, 2)

                def project_q(t):
                    after(pe, v_copied, t.n - 1)
                    after(pe, hrstd_ready, t.n - 3)
                    after(pe, q_rest, t.n)
                    for m in range(2):
                        for s in range(3):
                            mm = nc.tensor.matmul(PS[:, 7, NTP * m:NTP * m + NTP], WS[:, s, 128 * m:128 * m + 128],
                                                  XT[:, s // 2, bass.ds(t.n * NTP, NTP)], start=(s == 0), stop=(s == 2))
                    mm.then_inc(q_done, 1)

                def project_k(t):
                    after(pe, xc_copied, t.n - 2)
                    after(pe, xcsq_ready, t.n - 2)
                    after(pe, max_copied, t.n - 1)
                    after(pe, k_rest, t.n)
                    for m in range(2):
                        for s in range(3):
                            mm = nc.tensor.matmul(PS[:, 6, NTP * m:NTP * m + NTP], WS[:, s, 256 + 128 * m:384 + 128 * m],
                                                  XT[:, s // 2, bass.ds(t.n * NTP, NTP)], start=(s == 0), stop=(s == 2))
                    mm.then_inc(k_done, 1)

                def project_v(t):
                    pe.wait_ge(q_rest, upto(t.n + 2))
                    after(pe, hrstd_ready, t.n - 2)
                    for j in range(2):
                        for s in range(3):
                            mm = nc.tensor.matmul(PS[:, 7, 256 * j:256 * j + 256], XT[:, s // 2, bass.ds(t.n * NTP + TP * j, TP)],
                                                  WS[:, s, 512:768], start=(s == 0), stop=(s == 2))
                    mm.then_inc(v_done, 1)

                def turn_maxes(t):
                    pe.wait_ge(k_rest, upto(t.n + 2))
                    after(pe, h_updated, t.n - 1)
                    wait_apart(pe, max_parts, t.n + 1, pe_passed)
                    for j in range(2):
                        tr = nc.tensor.transpose(bank_bf16(6)[0:3 * SH, TP * j:TP * j + TP], NP[:, j].rearrange("p s h -> p (s h)"), identb[:])
                    tr.then_inc(max_turned, 1)

                def head_center(t):
                    pe.wait_ge(heads_out, t.n * 2 + 2)
                    pe.wait_ge(max_copied, upto(t.n + 2))
                    after(pe, h_updated, t.n)
                    for g in range(2):
                        mm = nc.tensor.matmul(PS[:, 6, NTP * g:NTP * g + NTP], center[:, 0, :], O[:, g, :], start=True, stop=True)
                    mm.then_inc(xc_done, 1)

                def head_variance(t):
                    pe.wait_ge(xcsq_ready, t.n + 1)
                    pe.wait_ge(v_copied, upto(t.n + 3))
                    after(pe, hrstd_ready, t.n)
                    for g in range(2):
                        mm = nc.tensor.matmul(PS[:, 7, NTP * g:NTP * g + NTP], center[:, 1, :], XQ[:, g, :], start=True, stop=True)
                    mm.then_inc(var_done, 1)

                def project_out(t):
                    pe.wait_ge(gated, t.n + 1)
                    pe.wait_ge(k_rest, upto(t.n + 4))
                    for j in range(2):
                        for g in range(2):
                            mm = nc.tensor.matmul(PS[:, 6, D * j:D * j + D], U[:, g, TP * j:TP * j + TP], WO[:, g, :], start=(g == 0), stop=(g == 1))
                    mm.then_inc(wout_done, 1)

                def scores(t, s):
                    if s % 8 == 0:
                        pe.wait_ge(stack_in[t.p][s // 8], t.pair * 96 + 96)
                    after(pe, maxes_taken, t.n * 16 + (s - 1))
                    for j in range(2):
                        mm = nc.tensor.matmul(PS[:, s % 2, NTP * j:NTP * j + NT], QS[t.p][0:STACK, s, TP * j:TP * j + TP], KS[t.p][0:STACK, s, 0:NT], start=True, stop=True)
                    mm.then_inc(scores_done, 1)

                def scores_turned(t, s):
                    if s == 0:
                        pe.wait_ge(max_rows_in, t.n * 48 + 48)
                    after(pe, exps_ready, t.n * 16 + (s - 1))
                    for j in range(2):
                        mm = nc.tensor.matmul(PS[:, 2 + s % 2, NTP * j:NTP * j + NTP], KS[t.p][:, ORDER[s], TP * j:TP * j + TP], QS[t.p][:, ORDER[s], :], start=True, stop=True)
                    mm.then_inc(scoresT_done, 1)

                def values(t, q):
                    pe.wait_ge(exps_ready, t.n * 16 + (4 * q + 4))
                    if q == 0:
                        pe.wait_ge(v_copied, t.n + 1)
                    after(pe, quad_scaled, t.n * 4 + (q - 1))
                    bank = PS[:, 4 + q % 2, :]
                    for half in range(2):
                        for j in range(2):
                            rows = TP if j == 0 else LAST
                            for c in range(4):
                                head = 4 * (q // 2) + c
                                w = V[t.p][0:rows, j, VH * head:VH * head + VH] if half == 0 else ones[0:rows, :]
                                mm = nc.tensor.matmul(bank[32 * c:32 * c + 32, NTP * half:NTP * half + NTP], w, EX[q % 2][0:rows, c, j, :], start=(j == 0), stop=(j == 1))
                    mm.then_inc(quad_done, 1)

                def prologue():
                    for c in range(2):
                        project_q(Signal(0, c))
                        project_k(Signal(0, c))
                    project_v(Signal(0, 0))
                    for s in range(SH):
                        scores(Signal(0, 0), s)

                def step(b, front, nxt, tail):
                    turn_maxes(b)
                    if front:
                        project_q(b.next(2))
                    if tail:
                        head_center(b.next(-1))
                    if nxt:
                        project_v(b.next(1))
                    if front:
                        project_k(b.next(2))
                    if tail:
                        head_variance(b.next(-1))
                    for s in range(SH):
                        if nxt:
                            scores(b.next(1), s)
                        scores_turned(b, s)
                        if s == 3 and tail:
                            project_out(b.next(-1))
                        if s % 4 == 1 and s > 4:
                            values(b, s // 4 - 1)
                    values(b, 3)

                def epilogue():
                    last = Signal(0, 15)
                    head_center(last)
                    head_variance(last)
                    project_out(last)

                schedule(pe, prologue, step, epilogue)

            @block.scalar
            def _(act):
                nc.scalar.preload_act_table_set("natural_log_exp_and_others")
                chain = Chain(act, act_chain2)

                def q_first(t):
                    act.wait_ge(q_done, t.n + 1)
                    after(act, q_written, (t.n - 1) * 16)
                    nc.scalar.activation(QP[t.p][:, 0, 0].rearrange("p g t -> p (g t)"), PS[:, 7, :], ACT.Copy, scale=DH ** -0.5).then_inc(q1_ready, 1)

                def k_first(t):
                    act.wait_ge(k_done, t.n + 1)
                    after(act, k_written, (t.n - 1) * 16)
                    nc.scalar.activation(QP[t.p][:, 1, 0].rearrange("p g t -> p (g t)"), PS[:, 6, :], ACT.Copy).then_inc(k1_ready, 1)

                def v_copy(t):
                    act.wait_ge(v_done, t.n + 1)
                    after(act, quad_done, t.n * 4 - 4)
                    nc.scalar.activation(V[t.p][:].rearrange("p j f -> p (j f)"), PS[:, 7, :], ACT.Copy).then_inc(v_copied, 1)

                def max_copy(t):
                    act.wait_ge(max_turned, t.n + 1)
                    after(act, max_rows_in, t.n * 48)
                    nc.scalar.activation(MT[:].rearrange("h j t -> h (j t)"), bank_bf16(6)[0:3 * SH, 0:NTP], ACT.Copy).then_inc(max_copied, 1)

                def head_squares(t):
                    act.wait_ge(xc_done, t.n + 1)
                    after(act, var_done, t.n)
                    nc.scalar.activation(XQ[:].rearrange("p g t -> p (g t)"), PS[:, 6, :], ACT.Square).then_inc(xcsq_ready, 1)

                def head_rstd(t):
                    act.wait_ge(var_done, t.n + 1)
                    after(act, head_normed, t.n)
                    chain.at = t.n
                    chain.link(nc.scalar.activation(RS[:].rearrange("p g t -> p (g t)"), PS[:, 7, :], ACT.Ln, bias=bias[:, 2:3]))
                    nc.scalar.activation(RS[:], RS[:], ACT.Exp, scale=-0.5).then_inc(hrstd_ready, 1)

                def exps(t, s):
                    act.wait_ge(scoresT_done, t.n * 16 + (s + 1))
                    if s % 4 == 0:
                        after(act, quad_done, t.n * 4 + (s // 4 - 1))
                    nc.scalar.activation(EX[s // 4 % 2][:, s % 4].rearrange("p j t -> p (j t)"), PS[:, 2 + s % 2, :], ACT.Exp).then_inc(exps_ready, 1)

                def inverse(t, q):
                    act.wait_ge(quad_done, t.n * 4 + (q + 1))
                    after(act, quad_scaled, t.n * 4 + (q - 1))
                    chain2.at = t.n * 4 + q
                    chain2.link(nc.scalar.activation(IN[q % 2][:], PS[:, 4 + q % 2, NTP:2 * NTP], ACT.Ln))
                    nc.scalar.activation(IN[q % 2][:], IN[q % 2][:], ACT.Exp, scale=-1.0).then_inc(inv_ready, 1)

                chain2 = Chain(act, act_logs)

                def prologue():
                    for c in range(2):
                        q_first(Signal(0, c))
                        k_first(Signal(0, c))
                    v_copy(Signal(0, 0))

                def step(b, front, nxt, tail):
                    max_copy(b)
                    if front:
                        q_first(b.next(2))
                    if tail:
                        head_squares(b.next(-1))
                    if nxt:
                        v_copy(b.next(1))
                    if front:
                        k_first(b.next(2))
                    if tail:
                        head_rstd(b.next(-1))
                    for s in range(SH):
                        exps(b, s)
                        if s % 4 == 3 and s > 4:
                            inverse(b, s // 4 - 1)
                    inverse(b, 3)

                def epilogue():
                    head_squares(Signal(0, 15))
                    head_rstd(Signal(0, 15))

                schedule(act, prologue, step, epilogue)

            @block.vector
            def _(vec):
                chain = Chain(vec, max_chain)

                def flat(a):
                    return a[:].rearrange("p g t -> p (g t)")

                def q_left(t):
                    vec.wait_ge(q1_ready, t.n + 1)
                    after(vec, q_parts, t.n)
                    nc.vector.scalar_tensor_tensor(out=QR[:, 0].rearrange("p g t -> p (g t)"), in0=PS[:, 7, :], scalar=DH ** -0.5,
                                                   in1=QP[t.p][:, 0, 0].rearrange("p g t -> p (g t)"), op0=ALU.mult, op1=ALU.subtract).then_inc(q_rest, 1)

                def k_left(t):
                    vec.wait_ge(k1_ready, t.n + 1)
                    after(vec, k_parts, t.n)
                    nc.vector.tensor_tensor(QR[:, 1].rearrange("p g t -> p (g t)"), PS[:, 6, :], QP[t.p][:, 1, 0].rearrange("p g t -> p (g t)"), ALU.subtract).then_inc(k_rest, 1)

                def xc_copy(t):
                    vec.wait_ge(xc_done, t.n + 1)
                    vec.wait_ge(xcsq_ready, t.n + 1)
                    after(vec, head_normed, t.n)
                    nc.vector.tensor_copy(flat(XB), PS[:, 6, :]).then_inc(xc_copied, 1)

                def head_norm(t):
                    vec.wait_ge(hrstd_ready, t.n + 1)
                    vec.wait_ge(xc_copied, t.n + 1)
                    after(vec, gated, t.n)
                    nc.vector.tensor_tensor(flat(Y), flat(XB), flat(RS), ALU.mult).then_inc(head_normed, 1)

                def take_max(t, s):
                    vec.wait_ge(scores_done, t.n * 16 + (s + 1))
                    nc.vector.tensor_reduce(NM[:, s, :], PS[:, s % 2, :].rearrange("p (j k) -> p j k", j=2)[:, :, 0:NT], AX.X, ALU.max, negate=True).then_inc(maxes_taken, 1)

                def split_max(t):
                    vec.wait_ge(maxes_taken, t.n * 16 + 16)
                    after(vec, max_turned, t.n)
                    nm = NM[:].rearrange("p h j -> p j h")
                    chain.at = t.n * 3
                    chain.link(nc.vector.tensor_copy(NP[:, :, 0, :], nm))
                    chain.link(nc.vector.tensor_tensor(NR[:], nm, NP[:, :, 0, :], ALU.subtract))
                    chain.link(nc.vector.tensor_copy(NP[:, :, 1, :], NR[:]))
                    nc.vector.tensor_tensor(NP[:, :, 2, :], NR[:], NP[:, :, 1, :], ALU.subtract).then_inc(max_parts, 1)

                def scale_quad(t, q):
                    vec.wait_ge(inv_ready, t.n * 4 + (q + 1))
                    after(vec, heads_out, t.n * 2)
                    av = PS[:, 4 + q % 2, 0:NTP]
                    if q % 2 == 0:
                        ins = nc.vector.tensor_tensor(AH[:, q, :], av, IN[q % 2][:], ALU.mult)
                    else:
                        ins = nc.vector.scalar_tensor_tensor(out=AH[:, q, :], in0=av, scalar=LS[:, 5:6], in1=IN[q % 2][:], op0=ALU.mult, op1=ALU.mult)
                    ins.then_inc(quad_scaled, 1)

                def update(t):
                    vec.wait_ge(wout_done, t.n + 1)
                    h = H[:, bass.ds(t.n * 2, 2), :]
                    nc.vector.tensor_tensor(h, PS[:, 6, 0:2 * D].rearrange("p (j f) -> p j f", j=2), h, ALU.add).then_inc(h_updated, 1)

                def prologue():
                    for c in range(2):
                        q_left(Signal(0, c))
                        k_left(Signal(0, c))
                    for s in range(SH):
                        take_max(Signal(0, 0), s)
                    split_max(Signal(0, 0))

                def step(b, front, nxt, tail):
                    if front:
                        q_left(b.next(2))
                    if tail:
                        xc_copy(b.next(-1))
                    if front:
                        k_left(b.next(2))
                    if tail:
                        head_norm(b.next(-1))
                    for s in range(SH):
                        if nxt:
                            take_max(b.next(1), s)
                        if s == 5 and tail:
                            update(b.next(-1))
                        if s % 4 == 3 and s > 4:
                            scale_quad(b, s // 4 - 1)
                    if nxt:
                        split_max(b.next(1))
                    scale_quad(b, 3)

                def epilogue():
                    last = Signal(0, 15)
                    xc_copy(last)
                    head_norm(last)
                    update(last)

                schedule(vec, prologue, step, epilogue)

            @block.gpsimd
            def _(pool):
                nc.gpsimd.memset(ones[:], 1.0).then_inc(ones_made, 1)
                pool.wait_ge(ones_made, 1)
                for p in range(2):
                    m = nc.gpsimd.memset(KS[p][STACK:STACK + MAXROWS, :, :], 1.0)
                m.then_inc(ones_made, 1)
                pool.wait_ge(ones_made, 2)
                chain = Chain(pool, part_chain)
                links = Chain(pool, gate_chain)

                def parts(t, which, rest, ready):
                    wait_apart(pool, rest, t.n + 1, pool_passed)
                    src = QR[:, which]
                    dst = QP[t.p][:, which]
                    chain.at = t.n * 2 + which
                    chain.link(nc.gpsimd.tensor_copy(dst[:, 1], src))
                    nc.gpsimd.tensor_tensor(dst[:, 2], src, dst[:, 1], ALU.subtract).then_inc(ready, 1)

                def gate(t):
                    wait_apart(pool, head_normed, t.n + 1, pool_passed)
                    links.at = t.n
                    links.link(nc.gpsimd.tensor_scalar(Y2[:], Y[:], GB[:, 2:3], GB[:, 3:4], ALU.mult, ALU.add))
                    after(pool, wout_done, t.n)
                    nc.gpsimd.tensor_tensor(U[:], Y2[:], SG[:, :, bass.ds(t.n * NTP, NTP)], ALU.mult).then_inc(gated, 1)

                def join(t, g):
                    pool.wait_ge(quad_scaled, t.n * 4 + (2 * g + 2))
                    after(pool, xc_done, t.n)
                    nc.gpsimd.tensor_tensor(O[:, g, :], AH[:, 2 * g, :], AH[:, 2 * g + 1, :], ALU.add).then_inc(heads_out, 1)

                def prologue():
                    for c in range(2):
                        parts(Signal(0, c), 0, q_rest, q_parts)
                        parts(Signal(0, c), 1, k_rest, k_parts)

                def step(b, front, nxt, tail):
                    if front:
                        parts(b.next(2), 0, q_rest, q_parts)
                        parts(b.next(2), 1, k_rest, k_parts)
                    if tail:
                        gate(b.next(-1))
                    join(b, 0)
                    join(b, 1)

                schedule(pool, prologue, step, lambda: gate(Signal(0, 15)))

        end_stages()
        late = ctx.enter_context(ExitStack())

        def sl(name, shape, dt=F32):
            return late.enter_context(nc.sbuf_tensor(name, shape, dt))

        XN = sl("XN", [128, TILES, D])
        XR = sl("XR", [128, TILES, D])
        SQ2 = sl("SQ2", [128, TILES, D])
        XS2 = sl("XS2", [128, TILES, 3 * D], BF16)
        W2 = sl("W2", [128, NE, D])
        RT = sl("RT", [128, ROUTE_COLUMNS])
        WR8 = sl("WR8", [D, NE])
        BR8 = sl("BR8", [B, NE])
        B1 = sl("B1", [NE, FH])
        B2 = sl("B2", [NE, D])
        GA = sl("GA", [128, 2, D])
        route_in = sem("route_in")
        QUARTERS = 4
        QT = TILES // QUARTERS

        def quarter(n):
            return slice(QT * n, QT * n + QT)

        def across(column, width):
            return column.unsqueeze(2).broadcast_to([128, QT, width])

        class Norm:

            def __init__(self, name, src, dst):
                self.src, self.dst = src, dst
                self.centered, self.squared, self.summed = sem(name + "_centered"), sem(name + "_squared"), sem(name + "_summed")
                self.rstd, self.done, self.chain = sem(name + "_rstd"), sem(name + "_done"), sem(name + "_chain")
                self.logs = sem(name + "_logs")

            def vector(self, ready=None):
                src, dst = self.src, self.dst
                chain = Chain(nc.vector, self.chain)
                for n in range(QUARTERS):
                    if ready is not None:
                        nc.vector.wait_ge(ready, n + 1)
                    chain.link(nc.vector.tensor_reduce(st[:, 0, quarter(n)], src[:, quarter(n), :], AX.X, ALU.add))
                    nc.vector.scalar_tensor_tensor(out=dst[:, quarter(n), :], in0=across(st[:, 0, quarter(n)], D), scalar=-1.0 / D,
                                                   in1=src[:, quarter(n), :], op0=ALU.mult, op1=ALU.add).then_inc(self.centered, 1)
                for n in range(QUARTERS):
                    nc.vector.wait_ge(self.squared, n + 1)
                    nc.vector.tensor_reduce(st[:, 1, quarter(n)], SQ2[:, quarter(n), :], AX.X, ALU.add).then_inc(self.summed, 1)
                for n in range(QUARTERS):
                    nc.vector.wait_ge(self.rstd, n + 1)
                    nc.vector.tensor_tensor(dst[:, quarter(n), :], dst[:, quarter(n), :], across(st[:, 3, quarter(n)], D), ALU.mult).then_inc(self.done, 1)

            def scalar(self):
                chain = Chain(nc.scalar, self.logs)
                for n in range(QUARTERS):
                    nc.scalar.wait_ge(self.centered, n + 1)
                    nc.scalar.activation(SQ2[:, quarter(n), :], self.dst[:, quarter(n), :], ACT.Square).then_inc(self.squared, 1)
                for n in range(QUARTERS):
                    nc.scalar.wait_ge(self.summed, n + 1)
                    chain.link(nc.scalar.activation(st[:, 2, quarter(n)], st[:, 1, quarter(n)], ACT.Ln, scale=1.0 / D, bias=bias[:, 2:3]))
                    nc.scalar.activation(st[:, 3, quarter(n)], st[:, 2, quarter(n)], ACT.Exp, scale=-0.5).then_inc(self.rstd, 1)

        class Turn:

            def __init__(self, name, src, rest):
                self.src, self.rest = src, rest
                self.first, self.left, self.second, self.third = sem(name + "_first"), sem(name + "_left"), sem(name + "_second"), sem(name + "_third")
                self.turned, self.copied0, self.copied1 = sem(name + "_turned"), sem(name + "_copied0"), sem(name + "_copied1")

            def vector(self):
                for n in range(QUARTERS):
                    nc.vector.wait_ge(self.first, n + 1)
                    nc.vector.tensor_tensor(self.rest[:, quarter(n), :], self.src[:, quarter(n), :], XS2[:, quarter(n), D:2 * D], ALU.subtract).then_inc(self.left, 1)
                for n in range(QUARTERS):
                    nc.vector.wait_ge(self.second, n + 1)
                    nc.vector.tensor_tensor(XS2[:, quarter(n), 2 * D:3 * D], self.rest[:, quarter(n), :], XS2[:, quarter(n), 0:D], ALU.subtract).then_inc(self.third, 1)
                for n in range(QUARTERS):
                    nc.vector.wait_ge(self.turned, 2 * n + 2)
                    nc.vector.tensor_copy(XT[:, 1, 1024 * n:1024 * n + 1024], bank_bf16(4 + n)).then_inc(self.copied1, 1)

            def scalar(self, normed):
                for n in range(QUARTERS):
                    nc.scalar.wait_ge(normed, n + 1)
                    nc.scalar.copy(XS2[:, quarter(n), D:2 * D], self.src[:, quarter(n), :]).then_inc(self.first, 1)
                for n in range(QUARTERS):
                    nc.scalar.wait_ge(self.left, n + 1)
                    nc.scalar.copy(XS2[:, quarter(n), 0:D], self.rest[:, quarter(n), :]).then_inc(self.second, 1)
                for n in range(QUARTERS):
                    nc.scalar.wait_ge(self.turned, 2 * n + 1)
                    nc.scalar.copy(XT[:, 0, 1024 * n:1024 * n + 1024], bank_bf16(n)).then_inc(self.copied0, 1)

            def tensor(self):
                for n in range(QUARTERS):
                    nc.tensor.wait_ge(self.third, n + 1)
                    for kind in range(2):
                        for t in range(8):
                            m = nc.tensor.transpose(bank_bf16(4 * kind + n)[:, 128 * t:128 * t + 128], XS2[:, 8 * n + t, D * kind:D * kind + 128], identb[:])
                        m.then_inc(self.turned, 1)

        WB = sl("WB", [128, B, 4])
        WI = sl("WI", [1, B, 2], mybir.dt.int32)
        B1S = sl("B1S", [FH, 2 * B])
        XM = sl("XM", [D, B])
        R = sl("R", [B, 16, NE])
        RQ = sl("RQ", [B, 2, NE, NE])
        RC = sl("RC", [B, 16])
        R4 = sl("R4", [B, B, 4])
        OT = sl("OT", [NE, 3, B])
        BE = sl("BE", [NE, B, D])
        ones8 = sl("ones8", [B, 128])
        fnorm = Norm("fnorm", H, XN)
        fturn = Turn("fturn", XN, SQ2)
        vec_small = sem("vec_small"); rstep = sem("rstep"); r_pe = sem("r_pe"); r_act = sem("r_act"); residual_ready = sem("residual_ready")
        ones8_made = sem("ones8_made")
        with nc.Block("routing") as blk:
            @blk.sync
            def _(sp):
                sp.dma_start(RT[:], c_route).then_inc(route_in, 16)
                sp.dma_start(WR8[:], f_wr).then_inc(route_in, 16)
                sp.dma_start(BR8[:], bass.AP(tensor=f_br.tensor, offset=0, ap=[[0, B], [1, NE]])).then_inc(route_in, 16)
                sp.dma_start(B1[:], f_b1).then_inc(route_in, 16)
                sp.dma_start(B2[:], f_b2).then_inc(route_in, 16)
                sp.dma_start(W2[:], f_w2.rearrange("e f d -> f e d")).then_inc(route_in, 16)
                for n, v in enumerate((f_gamma, f_beta)):
                    sp.dma_start(GA[:, n, :], bass.AP(tensor=v.tensor, offset=0, ap=[[0, 128], [1, D]])).then_inc(route_in, 16)

            @blk.gpsimd
            def _(pool):
                nc.gpsimd.memset(ones8[:], 1.0).then_inc(ones8_made, 1)

            @blk.scalar
            def _(act):
                nc.scalar.preload_act_table_set("natural_log_exp_and_others")
                fnorm.scalar()
                fturn.scalar(fnorm.done)
                act.wait_ge(rstep, 3)
                nc.scalar.activation(R[:, 2, :], R[:, 1, :], ACT.Exp).then_inc(r_act, 1)
                act.wait_ge(rstep, 13)
                nc.scalar.activation(R[:, 5, :], R[:, 4, :], ACT.Exp).then_inc(r_act, 1)
                act.wait_ge(rstep, 30)
                nc.scalar.activation(RC[:, 9:10], RC[:, 8:9], ACT.Exp).then_inc(r_act, 1)

            @blk.tensor
            def _(pe):
                fturn.tensor()
                pe.wait_ge(route_in, 16 * 8)
                pe.wait_ge(fturn.copied0, 4)
                for t in range(TILES):
                    rows = TP if t % 2 == 0 else LAST
                    b = t // 2
                    mm = nc.tensor.matmul(PS[0:D, 0, 0:B], XN[0:rows, t, :], RT[0:rows, B - 1 - b:2 * B - 1 - b], start=(t == 0), stop=(t == TILES - 1))
                mm.then_inc(r_pe, 1)
                pe.wait_ge(rstep, 1)
                nc.tensor.matmul(PS[0:B, 1, 0:NE], XM[:], WR8[:], start=True, stop=True).then_inc(r_pe, 1)
                pe.wait_ge(ones8_made, 1)
                pe.wait_ge(rstep, 7)
                nc.tensor.matmul(PS[0:B, 2, 0:NE], ones8[:, 0:B], R[:, 3, :], start=True, stop=True).then_inc(r_pe, 1)
                pe.wait_ge(rstep, 36)
                for n, row in enumerate((10, 11, 12)):
                    tr = nc.tensor.transpose(PS[0:NE, 3, B * n:B * n + B], R[:, row, :], ident[0:B, 0:B])
                tr.then_inc(r_pe, 1)
                nc.tensor.matmul(PS[:, 0, 0:4 * B], ones8[:], R4[:].rearrange("p b f -> p (b f)"), start=True, stop=True).then_inc(r_pe, 1)
                pe.wait_ge(rstep, 38)
                nc.tensor.matmul(PS[:, 1, 0:2 * B], B1[:], OT[:, 0:2, :].rearrange("e s b -> e (s b)"), start=True, stop=True).then_inc(r_pe, 1)
                for n in range(2):
                    mm = nc.tensor.matmul(PS[:, 4 + n, :], ones8[0:NE, :], BE[:, 8 * n:8 * n + 8, :].rearrange("e b f -> e (b f)"), start=True, stop=True)
                mm.then_inc(r_pe, 1)

            @blk.vector
            def _(vec):
                fnorm.vector()
                fturn.vector()
                v = nc.vector
                c = Chain(vec, rstep)
                vec.wait_ge(r_pe, 1)
                c.link(v.tensor_copy(XM[:], PS[0:D, 0, 0:B]))
                vec.wait_ge(r_pe, 2)
                c.link(v.tensor_tensor(R[:, 0, :], PS[0:B, 1, 0:NE], BR8[:], ALU.add))
                nc.vector.tensor_reduce(RC[:, 0:1], R[:, 0, :], AX.X, ALU.max).then_inc(vec_small, 1)
                vec.wait_ge(vec_small, 1)
                c.link(v.tensor_scalar(R[:, 1, :], R[:, 0, :], RC[:, 0:1], None, ALU.subtract))
                vec.wait_ge(r_act, 1)
                c.link(v.tensor_reduce(RC[:, 1:2], R[:, 2, :], AX.X, ALU.add))
                c.link(v.reciprocal(RC[:, 2:3], RC[:, 1:2]))
                c.link(v.memset(RC[:, 3:4], 1.0))
                c.link(v.tensor_scalar(R[:, 3, :], R[:, 2, :], RC[:, 2:3], None, ALU.mult))
                vec.wait_ge(r_pe, 3)
                c.link(v.tensor_scalar(R[:, 6, :], PS[0:B, 2, 0:NE], float(NT), None, ALU.mult))
                c.link(v.reciprocal(R[:, 7, :], R[:, 6, :]))
                c.link(v.tensor_scalar(R[:, 8, :], R[:, 7, :], CAPACITY, 1.0, ALU.mult, ALU.min))
                c.link(v.tensor_tensor(R[:, 9, :], R[:, 3, :], R[:, 8, :], ALU.mult))
                c.link(v.tensor_reduce(RC[:, 4:5], R[:, 9, :], AX.X, ALU.max))
                c.link(v.tensor_scalar(R[:, 4, :], R[:, 9, :], RC[:, 4:5], None, ALU.subtract))
                vec.wait_ge(r_act, 2)
                c.link(v.tensor_reduce(RC[:, 5:6], R[:, 5, :], AX.X, ALU.add))
                c.link(v.reciprocal(RC[:, 6:7], RC[:, 5:6]))
                c.link(v.tensor_scalar(R[:, 13, :], R[:, 5, :], RC[:, 6:7], None, ALU.mult))
                w = R[:, 13, :]
                others = w.unsqueeze(1).broadcast_to([B, NE, NE])
                own = w.unsqueeze(2).broadcast_to([B, NE, NE])
                earlier = RT[0:B, EARLIER:EARLIER + NE * NE].rearrange("p (e j) -> p e j", e=NE)
                c.link(v.tensor_tensor(RQ[:, 0], others, own, ALU.is_gt))
                c.link(v.tensor_tensor(RQ[:, 1], others, own, ALU.is_equal))
                c.link(v.tensor_tensor(RQ[:, 1], RQ[:, 1], earlier, ALU.mult))
                c.link(v.tensor_tensor(RQ[:, 0], RQ[:, 0], RQ[:, 1], ALU.add))
                c.link(v.tensor_reduce(R[:, 14, :], RQ[:, 0], AX.X, ALU.add))
                c.link(v.tensor_scalar(R[:, 10, :], R[:, 14, :], 0.0, None, ALU.is_equal))
                c.link(v.tensor_scalar(R[:, 11, :], R[:, 14, :], 1.0, None, ALU.is_equal))
                numbers = RT[0:B, NUMBERS:NUMBERS + NE]
                for s in range(2):
                    c.link(v.tensor_tensor(R[:, 15, :], R[:, 10 + s, :], w, ALU.mult))
                    c.link(v.tensor_reduce(RC[:, 6 + s:7 + s], R[:, 15, :], AX.X, ALU.add))
                    if s == 0:
                        c.link(v.memset(RC[:, 15:16], 0.0))
                c.link(v.memset(RC[:, 14:15], 0.0))
                c.link(v.tensor_tensor(RC[:, 8:9], RC[:, 7:8], RC[:, 6:7], ALU.subtract))
                vec.wait_ge(r_act, 3)
                c.link(v.tensor_scalar(RC[:, 13:14], RC[:, 9:10], 1.0, None, ALU.add))
                c.link(v.reciprocal(RC[:, 10:11], RC[:, 13:14]))
                c.link(v.tensor_tensor(RC[:, 11:12], RC[:, 9:10], RC[:, 10:11], ALU.mult))
                c.link(v.tensor_scalar(R[:, 12, :], R[:, 10, :], RC[:, 10:11], None, ALU.mult))
                c.link(v.scalar_tensor_tensor(out=R[:, 12, :], in0=R[:, 11, :], scalar=RC[:, 11:12], in1=R[:, 12, :], op0=ALU.mult, op1=ALU.add))
                diag = ident[0:B, 0:B]
                small = Chain(vec, vec_small, 1)
                for s in range(2):
                    small.link(v.tensor_scalar(R4[:, :, s], diag, RC[:, 10 + s:11 + s], None, ALU.mult))
                    small.link(v.tensor_tensor(R[:, 15, :], R[:, 10 + s, :], numbers, ALU.mult))
                    small.link(v.tensor_reduce(RC[:, 12:13], R[:, 15, :], AX.X, ALU.add))
                    small.link(v.tensor_scalar(R4[:, :, 2 + s], diag, RC[:, 12:13], None, ALU.mult))
                c.link(v.memset(RC[:, 0:1], 0.0))
                vec.wait_ge(r_pe, 4)
                c.link(v.tensor_copy(OT[:].rearrange("e s b -> e (s b)"), PS[0:NE, 3, 0:3 * B]))
                c.link(v.tensor_tensor(BE[:], B2[:].unsqueeze(1).broadcast_to([NE, B, D]), OT[:, 2, :].unsqueeze(2).broadcast_to([NE, B, D]), ALU.mult))
                vec.wait_ge(r_pe, 5)
                c.link(v.tensor_copy(WB[:].rearrange("p b f -> p (b f)"), PS[:, 0, 0:4 * B]))
                c.link(v.tensor_copy(WI[:], WB[0:1, :, 2:4]))
                vec.wait_ge(r_pe, 6)
                c.link(v.tensor_copy(B1S[:], PS[:, 1, 0:2 * B]))
                vec.wait_ge(r_pe, 7)
                for n in range(2):
                    for j in range(2):
                        tiles = slice(B * n, B * n + B)
                        out4 = XR[:, tiles, :].rearrange("p (b j) f -> p j b f", j=2)[:, j]
                        in4 = XN[:, tiles, :].rearrange("p (b j) f -> p j b f", j=2)[:, j]
                        c.link(v.tensor_tensor(out4, PS[:, 4 + n, :].rearrange("p (b f) -> p b f", f=D), in4, ALU.add))

        with ExitStack() as three:
            def sa(name, shape, dt=F32):
                return three.enter_context(nc.sbuf_tensor(name, shape, dt))
            GE = [sa(f"GE{p}", [FH, 2, NTP]) for p in range(2)]
            TA = sa("TA", [128, 2, 2, D])
            pe_passed = sem("pe_passed_ffn")
            hidden_done = sem("hidden_done"); gelu_ready = sem("gelu_ready"); expert_done = sem("expert_done")
            mix_chain = sem("mix_chain"); mixed = sem("mixed")

            with nc.Block("ffn") as blk:
                @blk.tensor
                def _(pe):
                    def hidden(n, p):
                        wait_apart(pe, gelu_ready, (n - 1) * 2, pe_passed)
                        for s in range(2):
                            e = pe.value_load(WI[0:1, bass.ds(n, 1), s:s + 1], min_val=0, max_val=NE - 1)
                            for k in range(3):
                                mm = nc.tensor.matmul(PS[:, p, NTP * s:NTP * s + NTP], WS[:, k, bass.ds(e * FH + NQKVG, FH)],
                                                      XT[:, k // 2, bass.ds(n * NTP, NTP)], start=(k == 0), stop=(k == 2))
                        mm.then_inc(hidden_done, 1)

                    def experts(n, p):
                        after(pe, mixed, n - 1)
                        wait_apart(pe, gelu_ready, n * 2 + 2, pe_passed)
                        for s in range(2):
                            e = pe.value_load(WI[0:1, bass.ds(n, 1), s:s + 1], min_val=0, max_val=NE - 1)
                            for j in range(2):
                                mm = nc.tensor.matmul(PS[:, 2 + p, D * (2 * j + s):D * (2 * j + s) + D], GE[p][:, s, TP * j:TP * j + TP],
                                                      W2[:, bass.ds(e, 1), :].rearrange("p e d -> p (e d)"), start=True, stop=True)
                        mm.then_inc(expert_done, 1)

                    hidden(0, 0)
                    hidden(1, 1)
                    experts(0, 0)
                    hidden(2, 0)
                    experts(1, 1)
                    with pe.Fori(0, PAIRS - 2) as i:
                        hidden(i * 2 + 3, 1)
                        experts(i * 2 + 2, 0)
                        hidden(i * 2 + 4, 0)
                        experts(i * 2 + 3, 1)
                    hidden(B - 1, 1)
                    experts(B - 2, 0)
                    experts(B - 1, 1)

                @blk.scalar
                def _(act):
                    nc.scalar.preload_act_table(ACT.Gelu)

                    def gelu(n, p):
                        act.wait_ge(hidden_done, n + 1)
                        after(act, expert_done, n - 1)
                        for s in range(2):
                            nc.scalar.activation(GE[p][:, s, :], PS[:, p, NTP * s:NTP * s + NTP], ACT.Gelu, bias=B1S[:, bass.ds(n + B * s, 1)]).then_inc(gelu_ready, 1)

                    gelu(0, 0)
                    gelu(1, 1)
                    with act.Fori(0, 7) as i:
                        gelu(i * 2 + 2, 0)
                        gelu(i * 2 + 3, 1)

                @blk.vector
                def _(vec):
                    chain = Chain(vec, mix_chain)

                    def mix(n, p):
                        vec.wait_ge(expert_done, n + 1)
                        y = PS[:, 2 + p, 0:4 * D].rearrange("p (j s f) -> p s j f", j=2, s=2)
                        xr = XR[:, bass.ds(n * 2, 2), :]
                        chain.at = n
                        chain.link(nc.vector.scalar_tensor_tensor(out=TA[:, p], in0=y[:, 0], scalar=WB[:, bass.ds(n, 1), 0], in1=xr, op0=ALU.mult, op1=ALU.add))
                        nc.vector.scalar_tensor_tensor(out=xr, in0=y[:, 1], scalar=WB[:, bass.ds(n, 1), 1], in1=TA[:, p], op0=ALU.mult, op1=ALU.add).then_inc(mixed, 1)

                    with vec.Fori(0, 8) as i:
                        mix(i * 2, 0)
                        mix(i * 2 + 1, 1)

        end_stages()
        onorm = Norm("onorm", XR, XR)
        anorm = Norm("anorm", H, XN)
        flat_scratch = nc.dram_tensor("flat_scratch", (B, NTP, D), F32).ap()
        back_scratch = nc.dram_tensor("back_scratch", (B, NTP, D), F32).ap()

        def as_rows(scratch, pair):
            return bass.AP(tensor=scratch.tensor, offset=pair * (2 * NTP * D), ap=[[NTP * D, 2], [NT, D], [1, NT]])

        with ExitStack() as four:
            def sa(name, shape, dt=F32):
                return four.enter_context(nc.sbuf_tensor(name, shape, dt))
            AW = sa("AW", [128, 4, 128])
            AB = sa("AB", [128, 2])
            AR = sa("AR", [128, 2, 128])
            FL = [sa(f"FL{p}", [128, NTP]) for p in range(2)]
            KB = sa("KB", [128, NTP]); KE = [sa(f"KE{p}", [128, NTP]) for p in range(2)]
            KM = sa("KM", [128, 4])
            QB = sa("QB", [128, 2, 128]); QE = [sa(f"QE{p}", [128, 2, 128]) for p in range(2)]
            QM = sa("QM", [128, 4, 32])
            VT = [sa(f"VT{p}", [128, 2, 128]) for p in range(2)]
            KT = sa("KT", [128, 2, 128]); QF = sa("QF", [128, NTP]); CT = sa("CT", [128, 128])
            AG = sa("AG", [128, NTP]); OF = [sa(f"OF{p}", [128, NTP]) for p in range(2)]
            a_weights_in = sem("a_weights_in"); aw_zeroed = sem("aw_zeroed"); residual_added = sem("residual_added")
            gamma_chain = sem("gamma_chain"); flat_written = sem("flat_written"); fl_zeroed = sem("fl_zeroed")
            flat_in = [sem("flat_in_even"), sem("flat_in_odd")]
            sp_passed = sem("sp_passed_attention")
            ka_done = sem("ka_done"); qv_done = sem("qv_done"); kb_ready = sem("kb_ready"); kmax_ready = sem("kmax_ready")
            ke_ready = sem("ke_ready"); ka_chain = sem("ka_chain"); qshift_ready = sem("qshift_ready"); qexp_ready = sem("qexp_ready")
            qa_chain = sem("qa_chain"); qsoft_ready = sem("qsoft_ready"); vt_ready = sem("vt_ready")
            kt_turned = sem("kt_turned"); qf_turned = sem("qf_turned"); kt_copied = sem("kt_copied"); qf_copied = sem("qf_copied")
            context_done = sem("context_done"); context_ready = sem("context_ready"); agg_done = sem("agg_done")
            agg_copied = sem("agg_copied"); proj_done = sem("proj_done"); of_ready = sem("of_ready"); of_written = [sem("of_written_even"), sem("of_written_odd")]
            back_in = sem("back_in")

            with nc.Block("residual") as blk:
                @blk.gpsimd
                def _(pool):
                    nc.gpsimd.memset(AW[:], 0.0).then_inc(aw_zeroed, 1)
                    for p in range(2):
                        m = nc.gpsimd.memset(FL[p][:], 0.0)
                    m.then_inc(fl_zeroed, 1)

                @blk.sync
                def _(sp):
                    sp.wait_ge(aw_zeroed, 1)
                    for n, w in enumerate((a_wk, a_wq, a_wv, a_wr)):
                        for half in (0, 64):
                            sp.dma_start(AW[half:half + 64, n, half:half + 64], w).then_inc(a_weights_in, 16)
                    for half in (0, 64):
                        for n, w in enumerate((a_bk, a_br)):
                            sp.dma_start(AB[half:half + 64, n:n + 1], w.rearrange("(p a) -> p a", a=1), allow_slow_non_contiguous=True).then_inc(a_weights_in, 16)
                        for n, w in enumerate((a_bq, a_bv)):
                            sp.dma_start(AR[:, n, half:half + 64], bass.AP(tensor=w.tensor, offset=0, ap=[[0, 128], [1, D]])).then_inc(a_weights_in, 16)
                    for n in range(QUARTERS):
                        sp.wait_ge(anorm.done, n + 1)
                        src = XN[:, quarter(n), :]
                        dst = flat_scratch[4 * n:4 * n + 4].rearrange("b (j t) f -> t (b j) f", j=2)
                        sp.dma_start(dst, src).then_inc(flat_written, 16)
                    sp.dma_start(back_scratch[:, NT, :], XN[0:B, 0, :]).then_inc(flat_written, 16)
                    sp.wait_ge(flat_written, 16 * 5)
                    sp.wait_ge(a_weights_in, 16 * 16)

                @blk.scalar
                def _(act):
                    nc.scalar.preload_act_table_set("natural_log_exp_and_others")
                    onorm.scalar()
                    anorm.scalar()

                @blk.vector
                def _(vec):
                    onorm.vector()
                    chain = Chain(vec, gamma_chain)
                    for n in range(QUARTERS):
                        xr = XR[:, quarter(n), :]
                        if n == 0:
                            vec.wait_ge(onorm.done, QUARTERS)
                        chain.link(nc.vector.tensor_tensor(xr, xr, GA[:, 0, :].unsqueeze(1).broadcast_to([128, QT, D]), ALU.mult))
                        chain.link(nc.vector.tensor_tensor(xr, xr, GA[:, 1, :].unsqueeze(1).broadcast_to([128, QT, D]), ALU.add))
                        nc.vector.tensor_tensor(H[:, quarter(n), :], H[:, quarter(n), :], xr, ALU.add).then_inc(residual_added, 1)
                    anorm.vector(residual_added)

            def schedule(eng, front, back):
                front(0, 0, 0)
                for n in range(2):
                    front(n + 1, (n + 1) % 2, (n + 1) // 2)
                    back(n, n % 2, n // 2)
                with eng.Fori(0, PAIRS // 2 - 2) as i:
                    front(i * 2 + 3, 1, i + 1)
                    back(i * 2 + 2, 0, i + 1)
                    front(i * 2 + 4, 0, i + 2)
                    back(i * 2 + 3, 1, i + 1)
                front(PAIRS - 1, 1, PAIRS // 2 - 1)
                back(PAIRS - 2, 0, PAIRS // 2 - 1)
                back(PAIRS - 1, 1, PAIRS // 2 - 1)

            with nc.Block("linear_attention") as blk:
                @blk.sync
                def _(sp):
                    def load(n, p):
                        wait_apart(sp, qv_done, n - 1, sp_passed)
                        sp.dma_start(FL[p][:, 0:NT], as_rows(flat_scratch, n)).then_inc(flat_in[p], 16)

                    def store(n, p):
                        wait_apart(sp, of_ready, n + 1, sp_passed)
                        sp.dma_start(as_rows(back_scratch, n), OF[p][:, 0:NT]).then_inc(of_written[p], 16)

                    load(0, 0)
                    load(1, 1)
                    with sp.Fori(0, 3) as i:
                        load(i * 2 + 2, 0)
                        store(i * 2, 0)
                        load(i * 2 + 3, 1)
                        store(i * 2 + 1, 1)
                    store(6, 0)
                    store(7, 1)
                    for p in range(2):
                        sp.wait_ge(of_written[p], 16 * PAIRS // 2)
                    for n in range(QUARTERS):
                        sp.dma_start(XR[:, quarter(n), :], back_scratch[4 * n:4 * n + 4].rearrange("b (j t) f -> t (b j) f", j=2)).then_inc(back_in, 16)
                    sp.wait_ge(back_in, 16 * QUARTERS)

                @blk.tensor
                def _(pe):
                    def project(n, p, turn):
                        pe.wait_ge(flat_in[p], turn * 16 + 16)
                        after(pe, kb_ready, n - 1)
                        nc.tensor.matmul(PS[:, p, 0:NTP], AW[:, 0, :], FL[p][:], start=True, stop=True).then_inc(ka_done, 1)
                        after(pe, qshift_ready, n - 1)
                        after(pe, vt_ready, n - 1)
                        for which in range(2):
                            for j in range(2):
                                mm = nc.tensor.matmul(PS[:, 2 + p, 256 * which + 128 * j:256 * which + 128 * j + 128], FL[p][:, TP * j:TP * j + TP], AW[:, 1 + which, :], start=True, stop=True)
                        mm.then_inc(qv_done, 1)

                    def attend(n, p, turn):
                        pe.wait_ge(ke_ready, n + 1)
                        after(pe, kt_copied, n)
                        for j in range(2):
                            rows = TP if j == 0 else LAST
                            tr = nc.tensor.transpose(PS[0:rows, 4, 128 * j:128 * j + 128], KE[p][:, TP * j:TP * j + rows], ident[:])
                        tr.then_inc(kt_turned, 1)
                        pe.wait_ge(qsoft_ready, n + 1)
                        after(pe, qf_copied, n)
                        for j in range(2):
                            tr = nc.tensor.transpose(PS[:, 5, 128 * j:128 * j + 128], QE[p][:, j, :], ident[:])
                        tr.then_inc(qf_turned, 1)
                        pe.wait_ge(kt_copied, n + 1)
                        pe.wait_ge(vt_ready, n + 1)
                        after(pe, agg_copied, n)
                        for j in range(2):
                            rows = TP if j == 0 else LAST
                            mm = nc.tensor.matmul(PS[:, 6, 0:128], KT[0:rows, j, :], VT[p][0:rows, j, :], start=(j == 0), stop=(j == 1))
                        mm.then_inc(context_done, 1)
                        pe.wait_ge(context_ready, n + 1)
                        pe.wait_ge(qf_copied, n + 1)
                        nc.tensor.matmul(PS[:, 6, 0:NTP], CT[:], QF[:], start=True, stop=True).then_inc(agg_done, 1)
                        pe.wait_ge(agg_copied, n + 1)
                        after(pe, of_ready, n)
                        nc.tensor.matmul(PS[:, 7, 0:NTP], AW[:, 3, :], AG[:], start=True, stop=True).then_inc(proj_done, 1)

                    schedule(pe, project, attend)

                @blk.scalar
                def _(act):
                    def soften(n, p, turn):
                        act.wait_ge(kmax_ready, n + 1)
                        after(act, kt_turned, n - 1)
                        nc.scalar.activation(KE[p][:, 0:NT], KB[:, 0:NT], ACT.Exp, bias=KM[:, 0:1], accum_out=KM[:, 2 + p:3 + p]).then_inc(ke_ready, 1)
                        act.wait_ge(qshift_ready, n + 1)
                        after(act, qf_turned, n - 1)
                        nc.scalar.activation(QE[p][:], QB[:], ACT.Exp).then_inc(qexp_ready, 1)

                    def copies(n, p, turn):
                        act.wait_ge(kt_turned, n + 1)
                        after(act, context_done, n)
                        nc.scalar.copy(KT[:, 0, :], PS[:, 4, 0:128])
                        nc.scalar.copy(KT[0:LAST, 1, :], PS[0:LAST, 4, 128:256]).then_inc(kt_copied, 1)
                        act.wait_ge(qf_turned, n + 1)
                        after(act, agg_done, n)
                        nc.scalar.copy(QF[:], PS[:, 5, 0:NTP]).then_inc(qf_copied, 1)
                        act.wait_ge(agg_done, n + 1)
                        after(act, proj_done, n)
                        nc.scalar.copy(AG[:], PS[:, 6, 0:NTP]).then_inc(agg_copied, 1)
                        act.wait_ge(proj_done, n + 1)
                        after(act, of_written[p], turn * 16)
                        nc.scalar.activation(OF[p][:], PS[:, 7, 0:NTP], ACT.Identity, bias=AB[:, 1:2]).then_inc(of_ready, 1)

                    schedule(act, soften, copies)

                @blk.vector
                def _(vec):
                    kchain = Chain(vec, ka_chain)
                    qchain = Chain(vec, qa_chain)

                    def keys_queries(n, p, turn):
                        vec.wait_ge(ka_done, n + 1)
                        after(vec, ke_ready, n)
                        nc.vector.tensor_scalar(KB[:, 0:NT], PS[:, p, 0:NT], AB[:, 0:1], None, ALU.add).then_inc(kb_ready, 1)
                        vec.wait_ge(kb_ready, n + 1)
                        nc.vector.tensor_reduce(KM[:, 0:1], KB[:, 0:NT], AX.X, ALU.max, negate=True).then_inc(kmax_ready, 1)
                        vec.wait_ge(qv_done, n + 1)
                        after(vec, context_done, n - 1)
                        half = PS[:, 2 + p, :].rearrange("p (w j c) -> p w j c", w=2, j=2)
                        nc.vector.tensor_tensor(VT[p][:], half[:, 1], AR[:, 1, :].unsqueeze(1).broadcast_to([128, 2, 128]), ALU.add).then_inc(vt_ready, 1)
                        after(vec, qexp_ready, n)
                        qchain.at = n * 4
                        qchain.link(nc.vector.tensor_tensor(QB[:], half[:, 0], AR[:, 0, :].unsqueeze(1).broadcast_to([128, 2, 128]), ALU.add))
                        groups = QB[:].rearrange("p j (g k) -> p (j g) k", k=LK)
                        qchain.link(nc.vector.tensor_reduce(QM[:, 0, :], groups, AX.X, ALU.max))
                        nc.vector.tensor_tensor(groups, groups, QM[:, 0, :].unsqueeze(2).broadcast_to([128, 32, LK]), ALU.subtract).then_inc(qshift_ready, 1)
                        vec.wait_ge(qexp_ready, n + 1)
                        egroups = QE[p][:].rearrange("p j (g k) -> p (j g) k", k=LK)
                        qchain.link(nc.vector.tensor_reduce(QM[:, 1, :], egroups, AX.X, ALU.add))
                        qchain.link(nc.vector.reciprocal(QM[:, 2, :], QM[:, 1, :]))
                        nc.vector.tensor_tensor(egroups, egroups, QM[:, 2, :].unsqueeze(2).broadcast_to([128, 32, LK]), ALU.mult).then_inc(qsoft_ready, 1)

                    def context(n, p, turn):
                        vec.wait_ge(ke_ready, n + 1)
                        after(vec, context_ready, n)
                        kchain.at = n
                        kchain.link(nc.vector.reciprocal(KM[:, 1:2], KM[:, 2 + p:3 + p]))
                        vec.wait_ge(context_done, n + 1)
                        after(vec, agg_done, n)
                        nc.vector.scalar_tensor_tensor(out=CT[:], in0=PS[:, 6, 0:128], scalar=KM[:, 1:2], in1=RT[:, HEADS:HEADS + 128],
                                                       op0=ALU.mult, op1=ALU.mult).then_inc(context_ready, 1)

                    schedule(vec, keys_queries, context)
                    vec.wait_ge(back_in, 16 * QUARTERS)
                    nc.vector.tensor_tensor(H[:], H[:], XR[:], ALU.add).then_inc(residual_added, 1)
                    vec.wait_ge(residual_added, QUARTERS + 1)

        end_stages()
        mnorm = Norm("mnorm", H, XN)
        mturn = Turn("mturn", XN, SQ2)
        HB = XR
        M1 = NQKVG + NW1
        GATE = M1 + D + ME * MH
        GROUPS = 1 + ME
        with ExitStack() as five:
            def sa(name, shape, dt=F32):
                return five.enter_context(nc.sbuf_tensor(name, shape, dt))
            MW2 = sa("MW2", [MH, ME, D])
            SW2 = sa("SW2", [128, 128])
            EW3 = sa("EW3", [128, ME // 2, 128])
            SW3 = sa("SW3", [128, D])
            MB1 = sa("MB1", [128, GROUPS])
            MB2 = sa("MB2", [128, 1 + ME // 2])
            SB3 = sa("SB3", [128, D])
            EB3 = sa("EB3", [128, D])
            GBB = sa("GBB", [128, ME])
            BD = sa("BD", [128, TILES, D])
            ZL = sa("ZL", [128, TILES, ME])
            G1 = sa("G1", [128, TILES, ME])
            G2 = sa("G2", [128, TILES, ME])
            GQ = sa("GQ", [128, 2, TILES, ME, ME])
            GS = sa("GS", [128, 6, TILES])
            G5 = sa("G5", [128, TILES, GROUPS])
            GT = sa("GT", [128, TP])
            H1 = sa("H1", [128, GROUPS, NTP])
            H2 = sa("H2", [128, 1 + ME // 2, NTP])
            WM = sa("WM", [128, 2, GROUPS, D])
            MO = sa("MO", [128, 2, D])
            sp_passed = sem("sp_passed_experts")
            m_zeroed = sem("m_zeroed"); m_weights_in = sem("m_weights_in"); biases_spread = sem("biases_spread")
            logits_done = sem("logits_done"); gate_steps = sem("gate_steps"); gate_exps = sem("gate_exps")
            weights_ready = sem("weights_ready"); weights_turned = sem("weights_turned"); turned_copied = sem("turned_copied")
            bias_done = sem("bias_done"); sums_ready = sem("sums_ready")
            first_done = sem("first_done"); first_relu = sem("first_relu"); second_done = sem("second_done")
            second_relu = sem("second_relu"); third_done = sem("third_done"); weighted = sem("weighted")
            sum_chain = sem("sum_chain"); token_ready = sem("token_ready"); out_written = sem("out_written")

            with nc.Block("gates") as blk:
                @blk.sync
                def _(sp):
                    sp.dma_start(GBB[:], bass.AP(tensor=m_gb.tensor, offset=0, ap=[[0, 128], [1, ME]])).then_inc(m_weights_in, 16)
                    sp.dma_start(SB3[:], bass.AP(tensor=m_sb3.tensor, offset=0, ap=[[0, 128], [1, D]])).then_inc(m_weights_in, 16)
                    sp.dma_start(EB3[:], bass.AP(tensor=m_eb3.tensor, offset=0, ap=[[0, TILES], [D, ME], [1, D]])).then_inc(m_weights_in, 16)
                    sp.dma_start(MW2[:], m_ew2.rearrange("e h g -> h e g")).then_inc(m_weights_in, 16)
                    sp.dma_start(SW3[:], m_sw3).then_inc(m_weights_in, 16)
                    sp.dma_start(MB1[:, 1:GROUPS], m_eb1.rearrange("e h -> h e"), allow_slow_non_contiguous=True).then_inc(m_weights_in, 16)
                    for half in range(2):
                        sp.dma_start(MB2[D * half:D * half + D, 0:2], m_eb2.rearrange("(q r) g -> g r q", r=2)[:, half], allow_slow_non_contiguous=True).then_inc(m_weights_in, 16)
                    sp.dma_start(MB2[:, 2:3], m_sb2.rearrange("(p a) -> p a", a=1), allow_slow_non_contiguous=True).then_inc(m_weights_in, 16)
                    sp.wait_ge(m_zeroed, 1)
                    sp.dma_start(MB1[0:D, 0:1], m_sb1.rearrange("(p a) -> p a", a=1), allow_slow_non_contiguous=True).then_inc(m_weights_in, 16)
                    sp.dma_start(SW2[0:D, :], m_sw2).then_inc(m_weights_in, 16)
                    for half in range(2):
                        sp.dma_start(EW3[D * half:D * half + D, :, D * half:D * half + D], m_ew3.rearrange("(q r) g f -> r g q f", r=2)[half]).then_inc(m_weights_in, 16)
                    sp.wait_ge(m_weights_in, 16 * 13)

                @blk.gpsimd
                def _(pool):
                    nc.gpsimd.memset(MB1[:, 0:1], 0.0)
                    nc.gpsimd.memset(SW2[:], 0.0)
                    nc.gpsimd.memset(G5[:, :, ME:GROUPS], 1.0)
                    nc.gpsimd.memset(EW3[:], 0.0).then_inc(m_zeroed, 1)
                    pool.wait_ge(m_weights_in, 16 * 13)
                    select = RT[:, SELECT:SELECT + TILES].unsqueeze(2).broadcast_to([128, TILES, D])
                    nc.gpsimd.tensor_tensor(BD[:], EB3[:].unsqueeze(1).broadcast_to([128, TILES, D]), select, ALU.mult).then_inc(biases_spread, 1)

                @blk.scalar
                def _(act):
                    nc.scalar.preload_act_table_set("natural_log_exp_and_others")
                    mnorm.scalar()
                    mturn.scalar(mnorm.done)
                    act.wait_ge(gate_steps, 3)
                    nc.scalar.activation(G1[:], ZL[:], ACT.Exp).then_inc(gate_exps, 1)
                    act.wait_ge(gate_steps, 17)
                    nc.scalar.activation(GS[:, 4, :], GS[:, 3, :], ACT.Exp).then_inc(gate_exps, 1)

                @blk.tensor
                def _(pe):
                    mturn.tensor()
                    pe.wait_ge(mturn.copied0, QUARTERS)
                    pe.wait_ge(mturn.copied1, QUARTERS)
                    for t in range(TILES):
                        for s in range(3):
                            mm = nc.tensor.matmul(PS[:, 0, ME * t:ME * t + ME], XT[:, s // 2, TP * t:TP * t + TP], WS[:, s, GATE:GATE + ME], start=(s == 0), stop=(s == 2))
                    mm.then_inc(logits_done, 1)
                    pe.wait_ge(weights_ready, 1)
                    nc.tensor.transpose(PS[:, 1, 0:TP], G1[:].rearrange("p t e -> p (t e)"), ident[:]).then_inc(weights_turned, 1)
                    pe.wait_ge(turned_copied, 1)
                    pe.wait_ge(biases_spread, 1)
                    for n in range(QUARTERS):
                        nc.tensor.matmul(PS[:, 2 + n, :], GT[:], BD[:, quarter(n), :], start=True, stop=True).then_inc(bias_done, 1)

                @blk.vector
                def _(vec):
                    mnorm.vector()
                    mturn.vector()
                    c = Chain(vec, gate_steps)
                    v = nc.vector

                    def each(column):
                        return column.unsqueeze(2).broadcast_to([128, TILES, ME])

                    vec.wait_ge(logits_done, 1)
                    vec.wait_ge(m_weights_in, 16 * 13)
                    c.link(v.tensor_tensor(ZL[:], PS[:, 0, 0:TILES * ME].rearrange("p (t e) -> p t e", e=ME), GBB[:].unsqueeze(1).broadcast_to([128, TILES, ME]), ALU.add))
                    c.link(v.tensor_reduce(GS[:, 0, :], ZL[:], AX.X, ALU.max))
                    c.link(v.tensor_tensor(ZL[:], ZL[:], each(GS[:, 0, :]), ALU.subtract))
                    vec.wait_ge(gate_exps, 1)
                    c.link(v.tensor_reduce(GS[:, 0, :], G1[:], AX.X, ALU.add))
                    c.link(v.reciprocal(GS[:, 1, :], GS[:, 0, :]))
                    c.link(v.tensor_tensor(G1[:], G1[:], each(GS[:, 1, :]), ALU.mult))
                    others = G1[:].unsqueeze(2).broadcast_to([128, TILES, ME, ME])
                    own = G1[:].unsqueeze(3).broadcast_to([128, TILES, ME, ME])
                    earlier = RT[:, EARLIER4:EARLIER4 + ME * ME].rearrange("p (e j) -> p e j", e=ME).unsqueeze(1).broadcast_to([128, TILES, ME, ME])
                    c.step(v.tensor_tensor(GQ[:, 0], others, own, ALU.is_gt))
                    c.link(v.tensor_tensor(GQ[:, 1], others, own, ALU.is_equal))
                    c.link(v.tensor_tensor(GQ[:, 1], GQ[:, 1], earlier, ALU.mult))
                    c.link(v.tensor_tensor(GQ[:, 0], GQ[:, 0], GQ[:, 1], ALU.add))
                    c.link(v.tensor_reduce(G2[:], GQ[:, 0], AX.X, ALU.add))
                    for s in range(2):
                        c.link(v.scalar_tensor_tensor(out=GQ[:, 0, :, 0, :], in0=G2[:], scalar=float(s), in1=G1[:], op0=ALU.is_equal, op1=ALU.mult))
                        c.link(v.tensor_reduce(GS[:, 1 + s, :], GQ[:, 0, :, 0, :], AX.X, ALU.add))
                    c.link(v.memset(GS[:, 5, :], 1.0))
                    c.link(v.tensor_tensor(GS[:, 3, :], GS[:, 2, :], GS[:, 1, :], ALU.subtract))
                    vec.wait_ge(gate_exps, 2)
                    c.link(v.tensor_tensor(GS[:, 0, :], GS[:, 4, :], GS[:, 5, :], ALU.add))
                    c.link(v.reciprocal(GS[:, 1, :], GS[:, 0, :]))
                    c.link(v.tensor_tensor(GS[:, 2, :], GS[:, 4, :], GS[:, 1, :], ALU.mult))
                    for s in range(2):
                        c.link(v.scalar_tensor_tensor(out=GQ[:, s, :, 0, :], in0=G2[:], scalar=float(s), in1=each(GS[:, 1 + s, :]), op0=ALU.is_equal, op1=ALU.mult))
                    c.link(v.tensor_tensor(G5[:, :, 0:ME], GQ[:, 0, :, 0, :], GQ[:, 1, :, 0, :], ALU.add))
                    v.tensor_copy(G1[:], G5[:, :, 0:ME]).then_inc(weights_ready, 1)
                    c.link(v.tensor_tensor(HB[:], H[:], SB3[:].unsqueeze(1).broadcast_to([128, TILES, D]), ALU.add))
                    vec.wait_ge(weights_turned, 1)
                    v.tensor_copy(GT[:], PS[:, 1, 0:TP]).then_inc(turned_copied, 1)
                    for n in range(QUARTERS):
                        vec.wait_ge(bias_done, n + 1)
                        v.tensor_tensor(HB[:, quarter(n), :], HB[:, quarter(n), :], PS[:, 2 + n, :].rearrange("p (t f) -> p t f", f=D), ALU.add).then_inc(sums_ready, 1)
                    vec.wait_ge(sums_ready, QUARTERS)

            with nc.Block("experts") as blk:
                @blk.tensor
                def _(pe):
                    def place(g):
                        return PS[:, g // 2, NTP * (g % 2):NTP * (g % 2) + NTP]

                    def first(n):
                        for g in range(GROUPS):
                            if g % 2 == 0:
                                after(pe, first_relu, (n - 1) * GROUPS + min(g + 2, GROUPS))
                            column = M1 if g == 0 else M1 + D + MH * (g - 1)
                            for s in range(3):
                                mm = nc.tensor.matmul(place(g), WS[:, s, column:column + 128], XT[:, s // 2, bass.ds(n * NTP, NTP)], start=(s == 0), stop=(s == 2))
                            mm.then_inc(first_done, 1)

                    def second(n):
                        after(pe, second_relu, n * 3)
                        pe.wait_ge(first_relu, n * GROUPS + GROUPS)
                        for q in range(ME // 2):
                            for half in range(2):
                                mm = nc.tensor.matmul(PS[D * half:D * half + D, 3, NTP * q:NTP * q + NTP], MW2[:, 2 * q + half, :], H1[:, 1 + 2 * q + half, :], start=True, stop=True)
                        mm.then_inc(second_done, 1)
                        nc.tensor.matmul(PS[:, 4, 0:NTP], SW2[:], H1[:, 0, :], start=True, stop=True).then_inc(second_done, 1)

                    def third(n):
                        pe.wait_ge(second_relu, n * 3 + 3)
                        after(pe, weighted, n)
                        for j in range(2):
                            tokens = slice(TP * j, TP * j + TP)
                            for q in range(ME // 2):
                                nc.tensor.matmul(PS[:, 5 + j, 128 * q:128 * q + 128], H2[:, q, tokens], EW3[:, q, :], start=True, stop=True)
                            mm = nc.tensor.matmul(PS[:, 5 + j, ME * D:GROUPS * D], H2[:, 2, tokens], SW3[:], start=True, stop=True)
                        mm.then_inc(third_done, 1)

                    first(0)
                    second(0)
                    first(1)
                    third(0)
                    with pe.Fori(0, B - 2) as i:
                        second(i + 1)
                        first(i + 2)
                        third(i + 1)
                    second(B - 1)
                    third(B - 1)

                @blk.scalar
                def _(act):
                    def first(n):
                        for g in range(GROUPS):
                            act.wait_ge(first_done, n * GROUPS + (min(g // 2 * 2 + 2, GROUPS)))
                            if g == 0:
                                after(act, second_done, n * 2)
                            nc.scalar.activation(H1[:, g, :], PS[:, g // 2, NTP * (g % 2):NTP * (g % 2) + NTP], ACT.Relu, bias=MB1[:, g:g + 1]).then_inc(first_relu, 1)

                    def second(n):
                        after(act, third_done, n)
                        for q in range(3):
                            act.wait_ge(second_done, n * 2 + (1 if q < 2 else 2))
                            src = PS[:, 3, NTP * q:NTP * q + NTP] if q < 2 else PS[:, 4, 0:NTP]
                            nc.scalar.activation(H2[:, q, :], src, ACT.Relu, bias=MB2[:, q:q + 1]).then_inc(second_relu, 1)

                    first(0)
                    second(0)
                    first(1)
                    with act.Fori(0, B - 2) as i:
                        second(i + 1)
                        first(i + 2)
                    second(B - 1)

                @blk.vector
                def _(vec):
                    def combine(n):
                        vec.wait_ge(third_done, n + 1)
                        after(vec, sum_chain, n)
                        y = PS[:, 5:7, 0:GROUPS * D].rearrange("p j (e f) -> p j e f", f=D)
                        nc.vector.tensor_tensor(WM[:], y, G5[:, bass.ds(n * 2, 2), :].unsqueeze(3).broadcast_to([128, 2, GROUPS, D]), ALU.mult).then_inc(weighted, 1)
                        vec.wait_ge(weighted, n + 1)
                        nc.vector.tensor_reduce(MO[:], WM[:].rearrange("p j e f -> p j f e"), AX.X, ALU.add).then_inc(sum_chain, 1)
                        vec.wait_ge(sum_chain, n + 1)
                        hb = HB[:, bass.ds(n * 2, 2), :]
                        nc.vector.tensor_tensor(hb, hb, MO[:], ALU.add).then_inc(token_ready, 1)

                    combine(0)
                    with vec.Fori(0, B - 1) as i:
                        combine(i + 1)

                @blk.sync
                def _(sp):
                    with sp.Fori(0, B) as i:
                        wait_apart(sp, token_ready, i + 1, sp_passed)
                        for j, lo, hi in ((0, 0, TP), (1, 0, 112), (1, 112, LAST)):
                            dst = bass.AP(tensor=out.tensor, offset=i * (NT * D) + D * (TP * j + lo), ap=[[D, hi - lo], [1, D]])
                            sp.dma_start(dst, HB[lo:hi, bass.ds(i * 2 + j, 1), :].rearrange("p a f -> p (a f)")).then_inc(out_written, 16)
                    sp.wait_ge(out_written, 16 * 3 * B)


def kernel(**inputs):
    import concourse.bacc as bacc
    from concourse.bass_utils import run_bass_kernel_spmd

    def given(name):
        return np.ascontiguousarray(np.asarray(inputs[name]))

    def head_rows(w):
        return w.reshape(D, 2, 8, DH).transpose(0, 1, 3, 2).reshape(D, 2 * 8 * DH)

    def beside(w):
        return w.transpose(1, 0, 2).reshape(D, -1)

    kv = given("L0_attn_Wkv")
    half = kv.shape[1] // 2
    arrays = {"x": given("x")}
    arrays["k64"] = np.ascontiguousarray(np.concatenate([
        head_rows(given("L0_attn_Wq")), head_rows(kv[:, :half]), kv[:, half:], given("L0_attn_Wg"),
        beside(given("L0_ffn_W1")), given("L1_ffn_sW1"), beside(given("L1_ffn_eW1")), given("L1_ffn_gW")], axis=1))
    for to, name in (("wout", "Wout"), ("bout", "bout"), ("bg", "bg"), ("lq1", "lq1"), ("lk1", "lk1"), ("lq2", "lq2"),
                     ("lk2", "lk2"), ("ln_gamma", "ln_gamma"), ("ln_beta", "ln_beta")):
        arrays[to] = given("L0_attn_" + name)
    for name in ("Wr", "br", "b1", "W2", "b2", "gamma", "beta"):
        arrays["f_" + name.lower()] = given("L0_ffn_" + name)
    for name in ("Wk", "bk", "Wq", "bq", "Wv", "bv", "Wr", "br"):
        arrays["a_" + name.lower()] = np.ascontiguousarray(given("L1_attn_" + name).T)
    for name in ("sb1", "sW2", "sb2", "sW3", "sb3", "eb1", "eW2", "eb2", "eW3", "eb3", "gb"):
        arrays["m_" + name.lower()] = given("L1_ffn_" + name)
    arrays.update(shape_constants())

    nc = bacc.Bacc("TRN2", target_bir_lowering=False, num_devices=1)
    names = {name: nc.dram_tensor(name, a.shape, mybir.dt.from_np(a.dtype), kind="ExternalInput").ap() for name, a in arrays.items()}
    out = nc.dram_tensor("out", (B, NT, D), F32, kind="ExternalOutput").ap()
    build_tower(nc, out=out, **names)
    return run_bass_kernel_spmd(nc, [arrays], core_ids=[0]).results[0]["out"]
```

```python
import math
from contextlib import ExitStack

import numpy as np

import concourse.bass as bass
from concourse import mybir

F32 = mybir.dt.float32
BF16 = mybir.dt.bfloat16
ALU = mybir.AluOpType
ACT = mybir.ActivationFunctionType
AX = mybir.AxisListType

B = 16
L = 4096
D = 64
UP = 4
NT = (L - 1) * UP // D
TP = 128
TILES = 2 * B
NTP = 2 * TP
LAST = NT - TP
HOP = D // UP
TAPS = HOP + 3
BINS = D // 2 + 1
EPS = 1e-5
SH = 16
DH = 16
VH = 32
LAMBDA_INIT = 0.8 - 0.6 * math.exp(-0.3)
NE = 8
FH = 128
CAPACITY = float(math.ceil(B * NT * 1.25 / NE))
PAIRS = B // 2
LK = 8
ME = 4
MH = 128
STACK = 6 * DH
EARLIER = 2 * B - 1
NUMBERS = EARLIER + NE * NE
HEADS = NUMBERS + NE
SELECT = HEADS + 128
EARLIER4 = SELECT + TILES
ROUTE_COLUMNS = EARLIER4 + ME * ME
MAXROWS = 3


def after(eng, sem, value):
    if isinstance(value, int) and value <= 0:
        return
    eng.wait_ge(sem, value)


def wait_apart(eng, sem, value, passed):
    if isinstance(value, int):
        after(eng, sem, value)
    else:
        eng.wait_ge(sem, value)
        eng.sem_inc(passed, 1)


class Chain:

    def __init__(self, eng, sem, at=0):
        self.eng, self.sem, self.at = eng, sem, at

    def step(self, instruction):
        instruction.then_inc(self.sem, 1)
        self.at = self.at + 1

    def wait(self):
        self.eng.wait_ge(self.sem, self.at)

    def link(self, instruction):
        self.step(instruction)
        self.wait()


def shape_constants():
    A = -0.75

    def near(t):
        return ((A + 2) * t - (A + 3)) * t * t + 1

    def far(t):
        return ((A * t - 5 * A) * t + 8 * A) * t - 4 * A

    def near_slope(t):
        return (3 * (A + 2) * t - 2 * (A + 3)) * t

    def far_slope(t):
        return (3 * A * t - 10 * A) * t + 8 * A

    taps = np.zeros((2, TAPS, D))
    for p in range(D):
        f = (p % UP) / UP
        for off, value, slope in ((-1, far(1 + f), far_slope(1 + f)), (0, near(f), near_slope(f)),
                                  (1, near(1 - f), -near_slope(1 - f)), (2, far(2 - f), -far_slope(2 - f))):
            taps[0, p // UP + off + 1, p] += value
            taps[1, p // UP + off + 1, p] += slope
    quad = np.zeros((128, 4, 128), np.float32)
    for kind in range(2):
        for tile in range(4):
            u, i = divmod(tile, 2)
            quad[32 * tile:32 * tile + TAPS, 2 * kind + u, 64 * i:64 * i + 64] = taps[kind]
    n = (L - 1) * UP + 1
    steps = np.arange(n - 1, dtype=np.float32) * (np.float32(1) / np.float32(n - 1))
    at = np.concatenate([steps, np.ones(1, np.float32)]) * np.float32(L - 1)
    shift = np.zeros((128, TP), np.float32)
    for i in range(2):
        for t in range(TP if i == 0 else LAST):
            p = D * (TP * i + t) + np.arange(D)
            shift[64 * i:64 * i + 64, t] = at[p].astype(np.float64) - p / UP
    dft = np.zeros((128, 128), np.float32)
    angle = 2 * np.pi * np.outer(np.arange(D), np.arange(BINS)) / D
    one = 0.5 * np.concatenate([np.cos(angle), np.sin(angle[:, 1:BINS - 1])], axis=1)
    dft[:64, :64] = dft[64:, 64:] = one
    average = np.kron(np.eye(128 // VH), np.full((VH, VH), 1.0 / VH)).astype(np.float32)
    route = np.zeros((128, ROUTE_COLUMNS), np.float32)
    route[:, B - 1] = 1.0 / NT
    route[:, EARLIER:EARLIER + NE * NE] = np.tril(np.ones((NE, NE)), -1).ravel()
    route[:, NUMBERS:NUMBERS + NE] = np.arange(NE)
    route[:, HEADS:HEADS + 128] = np.kron(np.eye(128 // LK), np.ones((LK, LK)))
    route[:, SELECT:SELECT + TILES] = np.kron(np.eye(TILES), np.ones((ME, 1)))
    route[:, EARLIER4:EARLIER4 + ME * ME] = np.tril(np.ones((ME, ME)), -1).ravel()
    return {"c_route": route, "c_ident": np.eye(128, dtype=np.float32), "c_taps": quad, "c_shift": shift, "c_dft": dft, "c_average": average}


def build_tower(nc, x, k64, wout, bout, bg, lq1, lk1, lq2, lk2, ln_gamma, ln_beta,
                f_wr, f_br, f_b1, f_w2, f_b2, f_gamma, f_beta,
                a_wk, a_bk, a_wq, a_bq, a_wv, a_bv, a_wr, a_br,
                m_sb1, m_sw2, m_sb2, m_sw3, m_sb3, m_eb1, m_ew2, m_eb2, m_ew3, m_eb3, m_gb,
                c_ident, c_taps, c_shift, c_dft, c_average, c_route, out):
    NQKVG = 4 * 256
    NW1 = NE * FH
    NM1 = D + ME * MH + ME
    NK64 = NQKVG + NW1 + NM1
    KQ = TILES // 4

    with ExitStack() as ctx:
        def sb(name, shape, dt=F32):
            return ctx.enter_context(nc.sbuf_tensor(name, shape, dt))

        signals = []

        def sem(name):
            signals.append(nc.alloc_semaphore(name=name))
            return signals[-1]

        def end_stages():
            nc.clear_and_free_semaphores(signals)
            signals.clear()
            nc.all_engine_barrier()

        PS = ctx.enter_context(nc.psum_tensor("PS", [128, 8, 512], F32))

        def bank_bf16(k):
            return PS[:, k, :].bitcast(BF16)

        H = sb("H", [128, TILES, D])
        XT = sb("XT", [128, 2, B * NTP], BF16)
        SG = sb("SG", [128, 2, B * NTP])
        ident = sb("ident", [128, 128])
        identb = sb("identb", [128, 128], BF16)
        taps = sb("taps", [128, 4, 128])
        shift = sb("shift", [128, TP])
        dft = sb("dft", [128, 128])
        average = sb("average", [128, 128])
        bias = sb("bias", [128, 8])
        WS = sb("WS", [128, 3, NK64], BF16)
        WO = sb("WO", [128, 2, D])
        BO = sb("BO", [128, D])
        BG = sb("BG", [128, 2])
        LV = sb("LV", [128, 4, DH])
        LS = sb("LS", [128, 8])
        GB = sb("GB", [128, 4])
        st = sb("st", [128, 6, TILES])

        scratch = nc.dram_tensor("parts_scratch", (2, 2, 3, 2, DH, 8, NTP), BF16).ap()

        consts_in = sem("consts_in"); ident_in = sem("ident_in"); windows_in = sem("windows_in"); weights_in = sem("weights_in")
        small_in = sem("small_in")
        windows_zeroed = sem("windows_zeroed"); consts_made = sem("consts_made")
        windows_turned = sem("windows_turned"); windows_copied = sem("windows_copied")
        interpolated = sem("interpolated"); points_ready = sem("points_ready")
        terms_ready = sem("terms_ready"); kernels_ready = sem("kernels_ready")
        spectrum_done = sem("spectrum_done"); squares_ready = sem("squares_ready")
        power_ready = sem("power_ready"); magnitude_ready = sem("magnitude_ready")
        excess_ready = sem("excess_ready"); mask_ready = sem("mask_ready")
        gap_ready = sem("gap_ready"); log_ready = sem("log_ready")
        centered = sem("centered"); csq_ready = sem("csq_ready"); var_ready = sem("var_ready")
        rstd_ready = sem("rstd_ready"); normed = sem("normed"); x1_ready = sem("x1_ready")
        rest_ready = sem("rest_ready"); x2_ready = sem("x2_ready"); x_split = sem("x_split")
        x_turned = sem("x_turned"); xt0_copied = sem("xt0_copied"); xt1_copied = sem("xt1_copied")
        weights_split = sem("weights_split"); gates_done = sem("gates_done"); gates_used = sem("gates_used")
        lam_products = sem("lam_products"); lam_exps = sem("lam_exps"); bout_added = sem("bout_added")
        vec_chain = sem("vec_chain"); act_chain = sem("act_chain"); pool_chain = sem("pool_chain")
        q_done = sem("q_done"); k_done = sem("k_done"); v_done = sem("v_done")
        q1_ready = sem("q1_ready"); k1_ready = sem("k1_ready")
        q_rest = sem("q_rest"); k_rest = sem("k_rest"); v_copied = sem("v_copied")
        q_parts = sem("q_parts"); k_parts = sem("k_parts")
        q_written = sem("q_written"); k_written = sem("k_written")
        stacks_in = [sem("stacks_in_even"), sem("stacks_in_odd")]
        scores_done = sem("scores_done"); maxes_taken = sem("maxes_taken")
        max_parts = sem("max_parts"); max_turned = sem("max_turned"); max_copied = sem("max_copied")
        max_rows_in = sem("max_rows_in")
        scoresT_done = sem("scoresT_done"); exps_ready = sem("exps_ready")
        quad_done = sem("quad_done"); inv_ready = sem("inv_ready"); quad_scaled = sem("quad_scaled")
        heads_out = sem("heads_out"); 
        squares_taken = sem("squares_taken"); var_done = sem("var_done"); hrstd_ready = sem("hrstd_ready")
        head_normed = sem("head_normed"); gated = sem("gated"); wout_done = sem("wout_done")
        h_updated = sem("h_updated"); act_chain2 = sem("act_chain2"); act_logs = sem("act_logs")
        max_chain = sem("max_chain"); part_chain = sem("part_chain"); ones_made = sem("ones_made")

        one = ExitStack()
        with one:
            def sa(name, shape, dt=F32):
                return one.enter_context(nc.sbuf_tensor(name, shape, dt))
            W = sa("W", [128, TILES, 32])
            SW = sa("SW", [128, KQ, TP])
            TX = sa("TX", [128, 2, KQ, TP])
            TP2 = sa("TP2", [128, 2, KQ, TP])
            TG = sa("TG", [128, 2, KQ, TP])
            SQ = sa("SQ", [128, TILES, D])
            MG = sa("MG", [128, TILES, BINS])
            MZ = sa("MZ", [128, TILES, BINS])
            ML = sa("ML", [128, TILES, BINS])
            XC = sa("XC", [128, TILES, D])
            XS = sa("XS", [128, TILES, 3 * D], BF16)
            WF = sa("WF", [128, NK64])
            WR = sa("WR", [128, NK64])
            WM8 = sa("WM8", [128, 8])
            values_centered = sem("values_centered")

            block = one.enter_context(nc.Block("front"))

            @block.sync
            def _(sp):
                sp.wait_ge(windows_zeroed, 1)
                def src(offset, n, width):
                    return bass.AP(tensor=x.tensor, offset=offset, ap=[[HOP, n], [L, B], [1, width]])
                tiles = W[:].rearrange("p (b j) s -> p j b s", j=2)
                for lo, hi in ((0, 112), (112, LAST)):
                    sp.dma_start(tiles[1 + lo:1 + hi, 0, :, 0:TAPS], src(HOP * (1 + lo) - 1, hi - lo, TAPS)).then_inc(windows_in, 16)
                    sp.dma_start(tiles[lo:hi, 1, :, 0:TAPS], src(HOP * (TP + lo) - 1, hi - lo, TAPS)).then_inc(windows_in, 16)
                sp.dma_start(tiles[0:1, 0, :, 1:TAPS], src(0, 1, TAPS - 1)).then_inc(windows_in, 16)
                sp.dma_start(tiles[0:1, 0, :, 0:1], src(0, 1, 1), allow_slow_non_contiguous=True).then_inc(windows_in, 16)
                for half in (0, 64):
                    sp.dma_start(WF[half:half + 64, :], k64).then_inc(weights_in, 16)
                sp.dma_start(WO[:], wout.rearrange("(g p) n -> p g n", g=2)).then_inc(small_in, 16)
                sp.dma_start(BO[:], bass.AP(tensor=bout.tensor, offset=0, ap=[[0, 128], [1, D]])).then_inc(small_in, 16)
                for n, v in enumerate((lq1, lk1, lq2, lk2)):
                    sp.dma_start(LV[:, n, :], bass.AP(tensor=v.tensor, offset=0, ap=[[0, 128], [1, DH]])).then_inc(small_in, 16)

            @block.scalar
            def _(act):
                nc.scalar.preload_act_table_set("natural_log_exp_and_others")
                act.dma_start(ident[:], c_ident).then_inc(ident_in, 16)
                act.dma_start(taps[:], c_taps).then_inc(consts_in, 16)
                act.dma_start(shift[:], c_shift).then_inc(consts_in, 16)
                act.dma_start(dft[:], c_dft).then_inc(consts_in, 16)
                act.dma_start(average[:], c_average).then_inc(consts_in, 16)
                act.dma_start(BG[:], bg.rearrange("(g p) -> p g", g=2), allow_slow_non_contiguous=True).then_inc(small_in, 16)
                for n, v in enumerate((ln_gamma, ln_beta)):
                    act.dma_start(GB[:, n:n + 1], bass.AP(tensor=v.tensor, offset=0, ap=[[0, 4], [1, VH], [1, 1]]), allow_slow_non_contiguous=True).then_inc(small_in, 16)
                chain = Chain(act, act_chain)
                for k in range(2):
                    act.wait_ge(windows_turned, k + 1)
                    nc.scalar.copy(SW[:, 4 * k:4 * k + 4, :], PS[:, k, :].rearrange("p (q t) -> p q t", q=4)).then_inc(windows_copied, 1)
                act.wait_ge(consts_made, 1)
                for s, (n, u) in enumerate(((0, 0), (0, 1), (1, 0), (1, 1))):
                    act.wait_ge(points_ready, s + 1)
                    part = (slice(None), u, slice(4 * n, 4 * n + 4), slice(None))
                    chain.step(nc.scalar.activation(TG[part], TX[part], ACT.Square, bias=bias[:, 0:1]))
                    chain.step(nc.scalar.activation(TP2[part], TX[part], ACT.Square, bias=bias[:, 1:2]))
                    chain.wait()
                    nc.scalar.activation(TG[part], TG[part], ACT.Exp, scale=-0.5).then_inc(terms_ready, 1)
                for k in range(4):
                    act.wait_ge(spectrum_done, k + 1)
                    nc.scalar.activation(SQ[:, 8 * k:8 * k + 8, :], PS[:, 2 + k, :].rearrange("p (t f) -> p t f", t=8), ACT.Square).then_inc(squares_ready, 1)
                halves = [slice(0, B), slice(B, TILES)]
                for n in range(2):
                    act.wait_ge(power_ready, n + 1)
                    nc.scalar.activation(MG[:, halves[n], :], SQ[:, halves[n], 0:BINS], ACT.Sqrt).then_inc(magnitude_ready, 1)
                for n in range(2):
                    act.wait_ge(excess_ready, n + 1)
                    nc.scalar.activation(MZ[:, halves[n], :], MZ[:, halves[n], :], ACT.Sigmoid).then_inc(mask_ready, 1)
                nc.scalar.preload_act_table_set("natural_log_exp_and_others")
                for n in range(2):
                    part = (slice(None), halves[n], slice(None))
                    act.wait_ge(gap_ready, n + 1)
                    chain.link(nc.scalar.activation(ML[part], ML[part], ACT.Abs))
                    chain.link(nc.scalar.activation(ML[part], ML[part], ACT.Exp, scale=-1.0))
                    nc.scalar.activation(ML[part], ML[part], ACT.Ln, bias=bias[:, 3:4]).then_inc(log_ready, 1)
                act.wait_ge(lam_products, 2)
                nc.scalar.activation(LS[:, 2:4], LS[:, 0:2], ACT.Exp).then_inc(lam_exps, 1)
                for n in range(2):
                    part = (slice(None), halves[n], slice(None))
                    act.wait_ge(centered, n + 1)
                    nc.scalar.activation(SQ[part], XC[part], ACT.Square).then_inc(csq_ready, 1)
                    act.wait_ge(var_ready, n + 1)
                    chain.link(nc.scalar.activation(st[:, 2, halves[n]], st[:, 1, halves[n]], ACT.Ln, scale=1.0 / D, bias=bias[:, 2:3]))
                    nc.scalar.activation(st[:, 3, halves[n]], st[:, 2, halves[n]], ACT.Exp, scale=-0.5).then_inc(rstd_ready, 1)
                for n in range(2):
                    act.wait_ge(normed, n + 1)
                    nc.scalar.copy(XS[:, halves[n], D:2 * D], XC[:, halves[n], :]).then_inc(x1_ready, 1)
                    act.wait_ge(rest_ready, n + 1)
                    nc.scalar.copy(XS[:, halves[n], 0:D], XC[:, halves[n], :]).then_inc(x2_ready, 1)
                for k in range(4):
                    act.wait_ge(x_turned, 2 * k + 1)
                    nc.scalar.copy(XT[:, 0, 1024 * k:1024 * k + 1024], bank_bf16(k)).then_inc(xt0_copied, 1)
                for n in range(8):
                    for m in range(2):
                        act.wait_ge(gates_done, 2 * n + m + 1)
                        nc.scalar.activation(SG[:, m, 512 * n:512 * n + 512], PS[:, (2 * n + m) % 8, :], ACT.Sigmoid, bias=BG[:, m:m + 1]).then_inc(gates_used, 1)

            @block.gpsimd
            def _(pool):
                nc.gpsimd.memset(W[:], 0.0).then_inc(windows_zeroed, 1)
                for n, value in enumerate((-0.7, 1.3, EPS, 1.0)):
                    m = nc.gpsimd.memset(bias[:, n:n + 1], value)
                m.then_inc(consts_made, 1)
                pool.wait_ge(ident_in, 16)
                nc.gpsimd.tensor_copy(identb[:], ident[:]).then_inc(consts_made, 1)
                chain = Chain(pool, pool_chain)
                pool.wait_ge(weights_in, 32)
                pool.wait_ge(values_centered, 1)
                for n, (lo, hi) in enumerate(((0, NQKVG), (NQKVG, NK64))):
                    chain.link(nc.gpsimd.tensor_copy(WS[:, 0, lo:hi], WF[:, lo:hi]))
                    chain.link(nc.gpsimd.tensor_tensor(WR[:, lo:hi], WF[:, lo:hi], WS[:, 0, lo:hi], ALU.subtract))
                    chain.link(nc.gpsimd.tensor_copy(WS[:, 1, lo:hi], WR[:, lo:hi]))
                    chain.link(nc.gpsimd.tensor_tensor(WS[0:64, 2, lo:hi], WR[0:64, lo:hi], WS[0:64, 1, lo:hi], ALU.subtract))
                    nc.gpsimd.tensor_copy(WS[64:128, 2, lo:hi], WS[64:128, 0, lo:hi]).then_inc(weights_split, 1)
                    pool.wait_ge(weights_split, n + 1)
                pool.wait_ge(small_in, 16 * 9)
                pool.wait_ge(centered, 2)
                chain.step(nc.gpsimd.tensor_scalar(GB[:, 2:4], GB[:, 0:2], 1.0 - LAMBDA_INIT, None, ALU.mult))
                nc.gpsimd.tensor_tensor(H[:], H[:], BO[:].unsqueeze(1).broadcast_to([128, TILES, D]), ALU.add).then_inc(bout_added, 1)

            @block.tensor
            def _(pe):
                pe.wait_ge(ident_in, 16); pe.wait_ge(consts_in, 64)
                pe.wait_ge(windows_in, 16 * 6)
                for q in range(KQ):
                    t = nc.tensor.transpose(PS[:, q // 4, 128 * (q % 4):128 * (q % 4) + 128], W[:, 4 * q:4 * q + 4, :], ident[:])
                    if q % 4 == 3:
                        t.then_inc(windows_turned, 1)
                for n in range(2):
                    pe.wait_ge(windows_copied, 2 if n else 1)
                    for u in range(2):
                        value, slope = ((2 + u, 4 + u), (6 + u, u))[n]
                        rhs = SW[:, 4 * n:4 * n + 4, :]
                        nc.tensor.matmul(PS[:, value, :], taps[:, u, :], rhs, start=True, stop=True)
                        nc.tensor.matmul(PS[:, slope, :], taps[:, 2 + u, :], rhs, start=True, stop=True).then_inc(interpolated, 1)
                for q in range(KQ):
                    for u in range(2):
                        pe.wait_ge(kernels_ready, 2 * (q // 4) + u + 1)
                        t = nc.tensor.matmul(PS[:, 2 + q // 2, 128 * (2 * (q % 2) + u):128 * (2 * (q % 2) + u) + 128],
                                             TX[:, u, q, :], dft[:], start=True, stop=True)
                    if q % 2:
                        t.then_inc(spectrum_done, 1)
                pe.wait_ge(consts_made, 2)
                for k in range(4):
                    if k % 2 == 0:
                        pe.wait_ge(x_split, k // 2 + 1)
                    for kind in range(2):
                        for t in range(8):
                            m = nc.tensor.transpose(bank_bf16(4 * kind + k)[:, 128 * t:128 * t + 128],
                                                    XS[:, 8 * k + t, D * kind:D * kind + 128], identb[:])
                        m.then_inc(x_turned, 1)
                pe.wait_ge(weights_split, 1)
                for n in range(8):
                    for m in range(2):
                        use = 2 * n + m
                        if use < 8:
                            pe.wait_ge(xt0_copied, 4)
                            pe.wait_ge(xt1_copied, 4)
                        else:
                            pe.wait_ge(gates_used, use - 7)
                        cols = slice(768 + 128 * m, 896 + 128 * m)
                        for s in range(3):
                            mm = nc.tensor.matmul(PS[:, use % 8, :], WS[:, s, cols], XT[:, s // 2, 512 * n:512 * n + 512], start=(s == 0), stop=(s == 2))
                        mm.then_inc(gates_done, 1)

            @block.vector
            def _(vec):
                chain = Chain(vec, vec_chain)
                vec.wait_ge(consts_in, 64)
                sh = shift[:].unsqueeze(1).broadcast_to([128, 4, TP])
                for s, (n, u) in enumerate(((0, 0), (0, 1), (1, 0), (1, 1))):
                    value, slope = ((2 + u, 4 + u), (6 + u, u))[n]
                    part = (slice(None), u, slice(4 * n, 4 * n + 4), slice(None))
                    vec.wait_ge(interpolated, s + 1)
                    chain.link(nc.vector.tensor_tensor(TP2[part], PS[:, slope, :].rearrange("p (q t) -> p q t", q=4), sh, ALU.mult))
                    nc.vector.tensor_tensor(TX[part], PS[:, value, :].rearrange("p (q t) -> p q t", q=4), TP2[part], ALU.add).then_inc(points_ready, 1)
                vec.wait_ge(weights_in, 32)
                heads = WF[:, 2 * 256:3 * 256].rearrange("p (h v) -> p h v", v=VH)
                chain.link(nc.vector.tensor_reduce(WM8[:], heads, AX.X, ALU.add))
                nc.vector.scalar_tensor_tensor(out=heads, in0=WM8[:].unsqueeze(2).broadcast_to([128, 8, VH]), scalar=-1.0 / VH,
                                               in1=heads, op0=ALU.mult, op1=ALU.add).then_inc(values_centered, 1)
                for s, (n, u) in enumerate(((0, 0), (0, 1), (1, 0), (1, 1))):
                    part = (slice(None), u, slice(4 * n, 4 * n + 4), slice(None))
                    vec.wait_ge(terms_ready, s + 1)
                    nc.vector.tensor_tensor(TX[part], TP2[part], TG[part], ALU.add).then_inc(kernels_ready, 1)
                vec.wait_ge(small_in, 16 * 9)
                for n in range(2):
                    chain.link(nc.vector.tensor_tensor(LV[:, 2 * n, :], LV[:, 2 * n, :], LV[:, 2 * n + 1, :], ALU.mult))
                    nc.vector.tensor_reduce(LS[:, n:n + 1], LV[:, 2 * n, :], AX.X, ALU.add).then_inc(lam_products, 1)
                halves = [slice(0, B), slice(B, TILES)]
                for n in range(2):
                    vec.wait_ge(squares_ready, 2 * n + 2)
                    nc.vector.tensor_tensor(SQ[:, halves[n], 1:BINS - 1], SQ[:, halves[n], 1:BINS - 1], SQ[:, halves[n], BINS:D], ALU.add).then_inc(power_ready, 1)

                def peak(n):
                    return st[:, 0, halves[n]].unsqueeze(2).broadcast_to([128, B, BINS])

                for n in range(2):
                    vec.wait_ge(magnitude_ready, n + 1)
                    chain.link(nc.vector.tensor_reduce(st[:, 0, halves[n]], MG[:, halves[n], :], AX.X, ALU.max))
                    nc.vector.scalar_tensor_tensor(out=MZ[:, halves[n], :], in0=peak(n), scalar=-0.12, in1=MG[:, halves[n], :], op0=ALU.mult, op1=ALU.add).then_inc(excess_ready, 1)
                for n in range(2):
                    part = (slice(None), halves[n], slice(None))
                    vec.wait_ge(mask_ready, n + 1)
                    chain.link(nc.vector.tensor_tensor(MG[part], MG[part], MZ[part], ALU.mult))
                    nc.vector.scalar_tensor_tensor(out=ML[part], in0=peak(n), scalar=-0.9, in1=MG[part], op0=ALU.mult, op1=ALU.add).then_inc(gap_ready, 1)
                    chain.step(nc.vector.scalar_tensor_tensor(out=MZ[part], in0=peak(n), scalar=0.9, in1=MG[part], op0=ALU.mult, op1=ALU.min))
                chain.wait()
                for n in range(2):
                    vec.wait_ge(log_ready, n + 1)
                    chain.step(nc.vector.tensor_tensor(H[:, halves[n], 0:BINS], MZ[:, halves[n], :], ML[:, halves[n], :], ALU.subtract))
                    chain.link(nc.vector.tensor_tensor(H[:, halves[n], BINS:D], MZ[:, halves[n], BINS - 2:0:-1], ML[:, halves[n], BINS - 2:0:-1], ALU.subtract))
                    chain.link(nc.vector.tensor_reduce(st[:, 0, halves[n]], H[:, halves[n], :], AX.X, ALU.add))
                    nc.vector.scalar_tensor_tensor(out=XC[:, halves[n], :], in0=st[:, 0, halves[n]].unsqueeze(2).broadcast_to([128, B, D]), scalar=-1.0 / D,
                                                   in1=H[:, halves[n], :], op0=ALU.mult, op1=ALU.add).then_inc(centered, 1)
                for n in range(2):
                    vec.wait_ge(csq_ready, n + 1)
                    nc.vector.tensor_reduce(st[:, 1, halves[n]], SQ[:, halves[n], :], AX.X, ALU.add).then_inc(var_ready, 1)
                for n in range(2):
                    vec.wait_ge(rstd_ready, n + 1)
                    nc.vector.tensor_tensor(XC[:, halves[n], :], XC[:, halves[n], :], st[:, 3, halves[n]].unsqueeze(2).broadcast_to([128, B, D]), ALU.mult).then_inc(normed, 1)
                for n in range(2):
                    part = (slice(None), halves[n], slice(None))
                    vec.wait_ge(x1_ready, n + 1)
                    nc.vector.tensor_tensor(XC[part], XC[part], XS[:, halves[n], D:2 * D], ALU.subtract).then_inc(rest_ready, 1)
                    vec.wait_ge(x2_ready, n + 1)
                    nc.vector.tensor_tensor(XS[:, halves[n], 2 * D:3 * D], XC[part], XS[:, halves[n], 0:D], ALU.subtract).then_inc(x_split, 1)
                vec.wait_ge(lam_exps, 1)
                chain.link(nc.vector.tensor_tensor(LS[:, 4:5], LS[:, 3:4], LS[:, 2:3], ALU.subtract))
                chain.link(nc.vector.tensor_scalar(LS[:, 5:6], LS[:, 4:5], -LAMBDA_INIT, None, ALU.add))
                for k in range(4):
                    vec.wait_ge(x_turned, 2 * k + 2)
                    nc.vector.tensor_copy(XT[:, 1, 1024 * k:1024 * k + 1024], bank_bf16(4 + k)).then_inc(xt1_copied, 1)


        with ExitStack() as two:
            def sa(name, shape, dt=F32):
                return two.enter_context(nc.sbuf_tensor(name, shape, dt))
            QP = [sa(f"QP{p}", [128, 2, 3, 2, NTP], BF16) for p in range(2)]
            QR = sa("QR", [128, 2, 2, NTP])
            QS = [sa(f"QS{p}", [STACK + MAXROWS, SH, NTP], BF16) for p in range(2)]
            KS = [sa(f"KS{p}", [STACK + MAXROWS, SH, NTP], BF16) for p in range(2)]
            NM = sa("NM", [128, SH, 2])
            NP = sa("NP", [128, 2, 3, SH], BF16)
            NR = sa("NR", [128, 2, SH])
            MT = sa("MT", [3 * SH, 2, TP], BF16)
            EX = [sa(f"EX{p}", [128, 4, 2, NTP]) for p in range(2)]
            V = [sa(f"V{p}", [128, 2, 8 * VH]) for p in range(2)]
            ones = sa("ones", [128, VH])
            IN = [sa(f"IN{p}", [128, NTP]) for p in range(2)]
            AH = sa("AH", [128, 4, NTP])
            O = sa("O", [128, 2, NTP])
            OQ = sa("OQ", [128, 2, NTP])
            RS = sa("RS", [128, 2, NTP])
            Y = sa("Y", [128, 2, NTP])
            U = sa("U", [128, 2, NTP])

            pe_passed = sem("pe_passed"); pool_passed = sem("pool_passed"); sp_passed = sem("sp_passed")
            stack_in = [[sem(f"stack_in_{p}{h}") for h in range(2)] for p in range(2)]
            ORDER = [2 * (4 * g + j) + odd for g in range(2) for odd in range(2) for j in range(4)]

            TWICE = (0, 1, 3, 5, 8, 9)
            NEXT_SLOTS = SH - len(TWICE)
            SLOT = {"queries": 0, "keys": 1, "values": 5, "variances": 10, "turn maxima": 11, "output": 14,
                    "inverse 2": 0, "queries copied": 0, "keys copied": 2, "inverse 3": 3, "values copied": 6,
                    "squares": 8, "inverse 0": 8, "rstd": 10, "maxima copied": 11, "inverse 1": 12,
                    "scale 2": 0, "queries left": 0, "keys left": 2, "scale 3": 6, "scale 0": 10,
                    "head norm": 11, "scale 1": 13, "residual": 15}

            def coming(s):
                first = s + sum(s > t for t in TWICE)
                return range(first, first + (2 if s in TWICE else 1)) if s < NEXT_SLOTS else ()

            class Signal:

                def __init__(self, i, c):
                    self.n = i * 2 + c if not isinstance(i, int) or i else c
                    self.p = c % 2
                    self.pair = i + c // 2 if not isinstance(i, int) or i or c >= 2 else 0
                    self.i, self.c = i, c

                def next(self, k):
                    return Signal(self.i, self.c + k)

            def upto(value, most=B):
                return min(value, most) if isinstance(value, int) else value

            def schedule(eng, prologue, step, epilogue):
                prologue()
                step(Signal(0, 0), True, True, False)
                step(Signal(0, 1), True, True, True)
                with eng.Fori(0, B // 2 - 2) as i:
                    step(Signal(i, 2), True, True, True)
                    step(Signal(i, 3), True, True, True)
                step(Signal(0, B - 2), False, True, True)
                step(Signal(0, B - 1), False, False, True)
                epilogue()

            block = two.enter_context(nc.Block("attention"))

            @block.sync
            def _(sp):
                part = 2 * DH * 8 * NTP
                rows = 8 * NTP

                def park(t):
                    q_sc, k_sc = scratch[t.p, 0], scratch[t.p, 1]
                    for h in range(2):
                        wait_apart(sp, stack_in[t.p][h], t.pair * 96, sp_passed)
                    sp.wait_ge(q_parts, t.n + 1)
                    sp.dma_start(q_sc.rearrange("s g d h t -> (d h) (s g) t"), QP[t.p][:, 0].rearrange("p s g t -> p (s g) t")).then_inc(q_written, 16)
                    sp.wait_ge(k_parts, t.n + 1)
                    sp.dma_start(k_sc.rearrange("s g d h t -> (d h) (s g) t"), QP[t.p][:, 1].rearrange("p s g t -> p (s g) t")).then_inc(k_written, 16)

                def stack(t, g):
                    wait_apart(sp, q_written, (t.n + 1) * 16, sp_passed)
                    wait_apart(sp, k_written, (t.n + 1) * 16, sp_passed)
                    wait_apart(sp, scoresT_done, (t.n - 2) * 16 + 8 * (g + 1), sp_passed)
                    heads = slice(8 * g, 8 * g + 8)
                    q0, k0 = scratch[t.p, 0, 0, g].offset, scratch[t.p, 1, 0, g].offset
                    for dst, base, first, reps, pstep, at in ((QS, q0, 0, 3, 0, 0), (QS, q0, 1, 2, 0, 3), (QS, q0, 2, 1, 0, 5),
                                                              (KS, k0, 0, 3, part, 0), (KS, k0, 0, 2, part, 3), (KS, k0, 0, 1, part, 5)):
                        src = bass.AP(tensor=scratch.tensor, offset=base + first * part, ap=[[pstep, reps], [rows, DH], [1, rows]])
                        sp.dma_start(dst[t.p][DH * at:DH * (at + reps), heads, :], src).then_inc(stack_in[t.p][g], 16)

                def max_rows(t):
                    sp.wait_ge(max_copied, t.n + 1)
                    for s in range(3):
                        sp.dma_start(QS[t.p][STACK + s:STACK + s + 1, :, :], MT[SH * s:SH * s + SH, :, :].rearrange("h j t -> h (j t)")).then_inc(max_rows_in, 16)

                def prologue():
                    for c in range(2):
                        park(Signal(0, c))
                        for g in range(2):
                            stack(Signal(0, c), g)
                    max_rows(Signal(0, 0))

                def step(b, front, nxt, tail):
                    if front:
                        park(b.next(2))
                        stack(b.next(2), 0)
                    if nxt:
                        max_rows(b.next(1))
                    if front:
                        stack(b.next(2), 1)

                schedule(sp, prologue, step, lambda: None)

            @block.tensor
            def _(pe):
                pe.wait_ge(ones_made, 2)

                def project_q(t):
                    after(pe, max_copied, t.n - 1)
                    after(pe, q_rest, t.n)
                    for m in range(2):
                        for s in range(3):
                            mm = nc.tensor.matmul(PS[:, 7, NTP * m:NTP * m + NTP], WS[:, s, 128 * m:128 * m + 128],
                                                  XT[:, s // 2, bass.ds(t.n * NTP, NTP)], start=(s == 0), stop=(s == 2))
                    mm.then_inc(q_done, 1)

                def project_k(t):
                    after(pe, h_updated, t.n - 3)
                    after(pe, k_rest, t.n)
                    for m in range(2):
                        for s in range(3):
                            mm = nc.tensor.matmul(PS[:, 6, NTP * m:NTP * m + NTP], WS[:, s, 256 + 128 * m:384 + 128 * m],
                                                  XT[:, s // 2, bass.ds(t.n * NTP, NTP)], start=(s == 0), stop=(s == 2))
                    mm.then_inc(k_done, 1)

                def project_v(t):
                    pe.wait_ge(q_rest, upto(t.n + 2))
                    after(pe, max_copied, t.n)
                    for j in range(2):
                        for s in range(3):
                            mm = nc.tensor.matmul(PS[:, 7, 256 * j:256 * j + 256], XT[:, s // 2, bass.ds(t.n * NTP + TP * j, TP)],
                                                  WS[:, s, 512:768], start=(s == 0), stop=(s == 2))
                    mm.then_inc(v_done, 1)

                def turn_maxes(t):
                    pe.wait_ge(v_copied, t.n + 1)
                    wait_apart(pe, max_parts, t.n + 1, pe_passed)
                    for j in range(2):
                        tr = nc.tensor.transpose(bank_bf16(7)[0:3 * SH, TP * j:TP * j + TP], NP[:, j].rearrange("p s h -> p (s h)"), identb[:])
                    tr.then_inc(max_turned, 1)

                def head_variance(t):
                    pe.wait_ge(k_rest, upto(t.n + 4))
                    after(pe, h_updated, t.n)
                    pe.wait_ge(squares_taken, t.n + 1)
                    for g in range(2):
                        mm = nc.tensor.matmul(PS[:, 6, NTP * g:NTP * g + NTP], average[:], OQ[:, g, :], start=True, stop=True)
                    mm.then_inc(var_done, 1)

                def project_out(t):
                    pe.wait_ge(hrstd_ready, t.n + 1)
                    pe.wait_ge(gated, t.n + 1)
                    for j in range(2):
                        for g in range(2):
                            mm = nc.tensor.matmul(PS[:, 6, D * j:D * j + D], U[:, g, TP * j:TP * j + TP], WO[:, g, :], start=(g == 0), stop=(g == 1))
                    mm.then_inc(wout_done, 1)

                def scores(t, s):
                    if s % 8 == 0:
                        pe.wait_ge(stack_in[t.p][s // 8], t.pair * 96 + 96)
                    after(pe, maxes_taken, t.n * 16 + (s - 1))
                    for j in range(2):
                        mm = nc.tensor.matmul(PS[:, s % 2, NTP * j:NTP * j + NT], QS[t.p][0:STACK, s, TP * j:TP * j + TP], KS[t.p][0:STACK, s, 0:NT], start=True, stop=True)
                    mm.then_inc(scores_done, 1)

                def scores_turned(t, s):
                    if s == 0:
                        pe.wait_ge(max_rows_in, t.n * 48 + 48)
                    after(pe, exps_ready, t.n * 16 + (s - 1))
                    for j in range(2):
                        mm = nc.tensor.matmul(PS[:, 2 + s % 2, NTP * j:NTP * j + NTP], KS[t.p][:, ORDER[s], TP * j:TP * j + TP], QS[t.p][:, ORDER[s], :], start=True, stop=True)
                    mm.then_inc(scoresT_done, 1)

                def values(t, q, piece):
                    half, j = divmod(piece, 2)
                    if piece == 0:
                        pe.wait_ge(exps_ready, t.n * 16 + (4 * q + 4))
                        if q == 0:
                            pe.wait_ge(v_copied, t.n + 1)
                        after(pe, quad_scaled, t.n * 4 + (q - 1))
                    rows = TP if j == 0 else LAST
                    for c in range(4):
                        head = 4 * (q // 2) + c
                        w = V[t.p][0:rows, j, VH * head:VH * head + VH] if half == 0 else ones[0:rows, :]
                        mm = nc.tensor.matmul(PS[32 * c:32 * c + 32, 4 + q % 2, NTP * half:NTP * half + NTP], w, EX[q % 2][0:rows, c, j, :], start=(j == 0), stop=(j == 1))
                    if piece == 3:
                        mm.then_inc(quad_done, 1)

                def prologue():
                    for c in range(2):
                        project_q(Signal(0, c))
                        project_k(Signal(0, c))
                    project_v(Signal(0, 0))
                    for s in range(SH):
                        scores(Signal(0, 0), s)
                    turn_maxes(Signal(0, 0))

                def step(b, front, nxt, tail):
                    for s in range(SH):
                        scores_turned(b, s)
                        if nxt:
                            for head in coming(s)[0:1]:
                                scores(b.next(1), head)
                        if s == SLOT["queries"] and front:
                            project_q(b.next(2))
                        if s == SLOT["keys"] and front:
                            project_k(b.next(2))
                        if s == SLOT["values"] and nxt:
                            project_v(b.next(1))
                        if s == SLOT["variances"] and tail:
                            head_variance(b.next(-1))
                        if s == SLOT["turn maxima"] and nxt:
                            turn_maxes(b.next(1))
                        if s == SLOT["output"] and tail:
                            project_out(b.next(-1))
                        if s >= 4:
                            values(b, s // 4 - 1, s % 4)
                        elif tail:
                            values(b.next(-1), 3, s)
                        if nxt:
                            for head in coming(s)[1:]:
                                scores(b.next(1), head)

                def epilogue():
                    last = Signal(0, B - 1)
                    for piece in range(4):
                        values(last, 3, piece)
                    head_variance(last)
                    project_out(last)

                schedule(pe, prologue, step, epilogue)

            @block.scalar
            def _(act):
                nc.scalar.preload_act_table_set("natural_log_exp_and_others")
                chain = Chain(act, act_chain2)

                def q_first(t):
                    act.wait_ge(q_done, t.n + 1)
                    after(act, q_written, (t.n - 1) * 16)
                    nc.scalar.activation(QP[t.p][:, 0, 0].rearrange("p g t -> p (g t)"), PS[:, 7, :], ACT.Copy, scale=DH ** -0.5).then_inc(q1_ready, 1)

                def k_first(t):
                    act.wait_ge(k_done, t.n + 1)
                    after(act, k_written, (t.n - 1) * 16)
                    nc.scalar.activation(QP[t.p][:, 1, 0].rearrange("p g t -> p (g t)"), PS[:, 6, :], ACT.Copy).then_inc(k1_ready, 1)

                def v_copy(t):
                    act.wait_ge(v_done, t.n + 1)
                    after(act, quad_done, t.n * 4 - 4)
                    nc.scalar.activation(V[t.p][:].rearrange("p j f -> p (j f)"), PS[:, 7, :], ACT.Copy).then_inc(v_copied, 1)

                def max_copy(t):
                    act.wait_ge(max_turned, t.n + 1)
                    after(act, max_rows_in, t.n * 48)
                    nc.scalar.activation(MT[:].rearrange("h j t -> h (j t)"), bank_bf16(7)[0:3 * SH, 0:NTP], ACT.Copy).then_inc(max_copied, 1)

                def head_squares(t):
                    act.wait_ge(heads_out, t.n * 2 + 2)
                    after(act, var_done, t.n)
                    nc.scalar.activation(OQ[:], O[:], ACT.Square).then_inc(squares_taken, 1)

                def head_rstd(t):
                    act.wait_ge(var_done, t.n + 1)
                    after(act, head_normed, t.n)
                    chain.at = t.n
                    chain.link(nc.scalar.activation(RS[:].rearrange("p g t -> p (g t)"), PS[:, 6, :], ACT.Ln, bias=bias[:, 2:3]))
                    nc.scalar.activation(RS[:], RS[:], ACT.Exp, scale=-0.5).then_inc(hrstd_ready, 1)

                def exps(t, s):
                    act.wait_ge(scoresT_done, t.n * 16 + (s + 1))
                    if s % 4 == 0:
                        after(act, quad_done, t.n * 4 + (s // 4 - 1))
                    nc.scalar.activation(EX[s // 4 % 2][:, s % 4].rearrange("p j t -> p (j t)"), PS[:, 2 + s % 2, :], ACT.Exp).then_inc(exps_ready, 1)

                def inverse(t, q):
                    act.wait_ge(quad_done, t.n * 4 + (q + 1))
                    after(act, quad_scaled, t.n * 4 + (q - 1))
                    chain2.at = t.n * 4 + q
                    chain2.link(nc.scalar.activation(IN[q % 2][:], PS[:, 4 + q % 2, NTP:2 * NTP], ACT.Ln))
                    nc.scalar.activation(IN[q % 2][:], IN[q % 2][:], ACT.Exp, scale=-1.0).then_inc(inv_ready, 1)

                chain2 = Chain(act, act_logs)

                def prologue():
                    for c in range(2):
                        q_first(Signal(0, c))
                        k_first(Signal(0, c))
                    v_copy(Signal(0, 0))
                    max_copy(Signal(0, 0))

                def step(b, front, nxt, tail):
                    for s in range(SH):
                        exps(b, s)
                        if s == SLOT["inverse 2"] and tail:
                            inverse(b.next(-1), 2)
                        if s == SLOT["queries copied"] and front:
                            q_first(b.next(2))
                        if s == SLOT["keys copied"] and front:
                            k_first(b.next(2))
                        if s == SLOT["inverse 3"] and tail:
                            inverse(b.next(-1), 3)
                        if s == SLOT["values copied"] and nxt:
                            v_copy(b.next(1))
                        if s == SLOT["inverse 0"]:
                            inverse(b, 0)
                        if s == SLOT["squares"] and tail:
                            head_squares(b.next(-1))
                        if s == SLOT["rstd"] and tail:
                            head_rstd(b.next(-1))
                        if s == SLOT["maxima copied"] and nxt:
                            max_copy(b.next(1))
                        if s == SLOT["inverse 1"]:
                            inverse(b, 1)

                def epilogue():
                    last = Signal(0, B - 1)
                    inverse(last, 2)
                    inverse(last, 3)
                    head_squares(last)
                    head_rstd(last)

                schedule(act, prologue, step, epilogue)

            @block.vector
            def _(vec):
                chain = Chain(vec, max_chain)

                def flat(a):
                    return a[:].rearrange("p g t -> p (g t)")

                def q_left(t):
                    vec.wait_ge(q1_ready, t.n + 1)
                    after(vec, q_parts, t.n)
                    nc.vector.scalar_tensor_tensor(out=QR[:, 0].rearrange("p g t -> p (g t)"), in0=PS[:, 7, :], scalar=DH ** -0.5,
                                                   in1=QP[t.p][:, 0, 0].rearrange("p g t -> p (g t)"), op0=ALU.mult, op1=ALU.subtract).then_inc(q_rest, 1)

                def k_left(t):
                    vec.wait_ge(k1_ready, t.n + 1)
                    after(vec, k_parts, t.n)
                    nc.vector.tensor_tensor(QR[:, 1].rearrange("p g t -> p (g t)"), PS[:, 6, :], QP[t.p][:, 1, 0].rearrange("p g t -> p (g t)"), ALU.subtract).then_inc(k_rest, 1)

                def head_norm(t):
                    vec.wait_ge(heads_out, t.n * 2 + 2)
                    vec.wait_ge(hrstd_ready, t.n + 1)
                    nc.vector.scalar_tensor_tensor(out=Y[:], in0=O[:], scalar=GB[:, 2:3], in1=RS[:], op0=ALU.mult, op1=ALU.mult).then_inc(head_normed, 1)
                    vec.wait_ge(head_normed, t.n + 1)
                    after(vec, wout_done, t.n)
                    nc.vector.scalar_tensor_tensor(out=U[:], in0=Y[:], scalar=GB[:, 3:4], in1=SG[:, :, bass.ds(t.n * NTP, NTP)], op0=ALU.add, op1=ALU.mult).then_inc(gated, 1)

                def take_max(t, s):
                    vec.wait_ge(scores_done, t.n * 16 + (s + 1))
                    nc.vector.tensor_reduce(NM[:, s, :], PS[:, s % 2, :].rearrange("p (j k) -> p j k", j=2)[:, :, 0:NT], AX.X, ALU.max, negate=True).then_inc(maxes_taken, 1)

                def split_max(t):
                    vec.wait_ge(maxes_taken, t.n * 16 + 16)
                    after(vec, max_turned, t.n)
                    nm = NM[:].rearrange("p h j -> p j h")
                    chain.at = t.n * 3
                    chain.link(nc.vector.tensor_copy(NP[:, :, 0, :], nm))
                    chain.link(nc.vector.tensor_tensor(NR[:], nm, NP[:, :, 0, :], ALU.subtract))
                    chain.link(nc.vector.tensor_copy(NP[:, :, 1, :], NR[:]))
                    nc.vector.tensor_tensor(NP[:, :, 2, :], NR[:], NP[:, :, 1, :], ALU.subtract).then_inc(max_parts, 1)

                def scale_quad(t, q):
                    vec.wait_ge(inv_ready, t.n * 4 + (q + 1))
                    after(vec, heads_out, t.n * 2 + (q // 2 - 1))
                    av = PS[:, 4 + q % 2, 0:NTP]
                    if q % 2 == 0:
                        ins = nc.vector.tensor_tensor(AH[:, q, :], av, IN[q % 2][:], ALU.mult)
                    else:
                        ins = nc.vector.scalar_tensor_tensor(out=AH[:, q, :], in0=av, scalar=LS[:, 5:6], in1=IN[q % 2][:], op0=ALU.mult, op1=ALU.mult)
                    ins.then_inc(quad_scaled, 1)

                def update(t):
                    vec.wait_ge(wout_done, t.n + 1)
                    h = H[:, bass.ds(t.n * 2, 2), :]
                    nc.vector.tensor_tensor(h, PS[:, 6, 0:2 * D].rearrange("p (j f) -> p j f", j=2), h, ALU.add).then_inc(h_updated, 1)

                def prologue():
                    for c in range(2):
                        q_left(Signal(0, c))
                        k_left(Signal(0, c))
                    for s in range(SH):
                        take_max(Signal(0, 0), s)
                    split_max(Signal(0, 0))

                def step(b, front, nxt, tail):
                    for s in range(SH):
                        if nxt:
                            for head in coming(s):
                                take_max(b.next(1), head)
                        if s == SLOT["scale 2"] and tail:
                            scale_quad(b.next(-1), 2)
                        if s == SLOT["queries left"] and front:
                            q_left(b.next(2))
                        if s == SLOT["keys left"] and front:
                            k_left(b.next(2))
                        if s == SLOT["scale 3"] and tail:
                            scale_quad(b.next(-1), 3)
                        if s == NEXT_SLOTS - 1 and nxt:
                            split_max(b.next(1))
                        if s == SLOT["scale 0"]:
                            scale_quad(b, 0)
                        if s == SLOT["head norm"] and tail:
                            head_norm(b.next(-1))
                        if s == SLOT["scale 1"]:
                            scale_quad(b, 1)
                        if s == SLOT["residual"] and tail:
                            update(b.next(-1))

                def epilogue():
                    last = Signal(0, B - 1)
                    scale_quad(last, 2)
                    scale_quad(last, 3)
                    head_norm(last)
                    update(last)

                schedule(vec, prologue, step, epilogue)

            @block.gpsimd
            def _(pool):
                nc.gpsimd.memset(ones[:], 1.0).then_inc(ones_made, 1)
                pool.wait_ge(ones_made, 1)
                for p in range(2):
                    m = nc.gpsimd.memset(KS[p][STACK:STACK + MAXROWS, :, :], 1.0)
                m.then_inc(ones_made, 1)
                pool.wait_ge(ones_made, 2)
                chain = Chain(pool, part_chain)

                def parts(t, which, rest, ready):
                    wait_apart(pool, rest, t.n + 1, pool_passed)
                    src = QR[:, which]
                    dst = QP[t.p][:, which]
                    chain.at = t.n * 2 + which
                    chain.link(nc.gpsimd.tensor_copy(dst[:, 1], src))
                    nc.gpsimd.tensor_tensor(dst[:, 2], src, dst[:, 1], ALU.subtract).then_inc(ready, 1)

                def join(t, g):
                    pool.wait_ge(quad_scaled, t.n * 4 + (2 * g + 2))
                    after(pool, head_normed, t.n)
                    nc.gpsimd.tensor_tensor(O[:, g, :], AH[:, 2 * g, :], AH[:, 2 * g + 1, :], ALU.add).then_inc(heads_out, 1)

                def prologue():
                    for c in range(2):
                        parts(Signal(0, c), 0, q_rest, q_parts)
                        parts(Signal(0, c), 1, k_rest, k_parts)

                def step(b, front, nxt, tail):
                    if front:
                        parts(b.next(2), 0, q_rest, q_parts)
                        parts(b.next(2), 1, k_rest, k_parts)
                    if tail:
                        join(b.next(-1), 1)
                    join(b, 0)

                schedule(pool, prologue, step, lambda: join(Signal(0, B - 1), 1))

        end_stages()
        late = ctx.enter_context(ExitStack())

        def sl(name, shape, dt=F32):
            return late.enter_context(nc.sbuf_tensor(name, shape, dt))

        XN = sl("XN", [128, TILES, D])
        XR = sl("XR", [128, TILES, D])
        SQ2 = sl("SQ2", [128, TILES, D])
        XS2 = sl("XS2", [128, TILES, 3 * D], BF16)
        W2 = sl("W2", [128, NE, D])
        RT = sl("RT", [128, ROUTE_COLUMNS])
        WR8 = sl("WR8", [D, NE])
        BR8 = sl("BR8", [B, NE])
        B1 = sl("B1", [NE, FH])
        B2 = sl("B2", [NE, D])
        GA = sl("GA", [128, 2, D])
        route_in = sem("route_in")
        QUARTERS = 4
        QT = TILES // QUARTERS

        def quarter(n):
            return slice(QT * n, QT * n + QT)

        def across(column, width):
            return column.unsqueeze(2).broadcast_to([128, QT, width])

        class Norm:

            def __init__(self, name, src, dst):
                self.src, self.dst = src, dst
                self.centered, self.squared, self.summed = sem(name + "_centered"), sem(name + "_squared"), sem(name + "_summed")
                self.rstd, self.done, self.chain = sem(name + "_rstd"), sem(name + "_done"), sem(name + "_chain")
                self.logs = sem(name + "_logs")

            def vector(self, ready=None):
                src, dst = self.src, self.dst
                chain = Chain(nc.vector, self.chain)
                for n in range(QUARTERS):
                    if ready is not None:
                        nc.vector.wait_ge(ready, n + 1)
                    chain.link(nc.vector.tensor_reduce(st[:, 0, quarter(n)], src[:, quarter(n), :], AX.X, ALU.add))
                    nc.vector.scalar_tensor_tensor(out=dst[:, quarter(n), :], in0=across(st[:, 0, quarter(n)], D), scalar=-1.0 / D,
                                                   in1=src[:, quarter(n), :], op0=ALU.mult, op1=ALU.add).then_inc(self.centered, 1)
                for n in range(QUARTERS):
                    nc.vector.wait_ge(self.squared, n + 1)
                    nc.vector.tensor_reduce(st[:, 1, quarter(n)], SQ2[:, quarter(n), :], AX.X, ALU.add).then_inc(self.summed, 1)
                for n in range(QUARTERS):
                    nc.vector.wait_ge(self.rstd, n + 1)
                    nc.vector.tensor_tensor(dst[:, quarter(n), :], dst[:, quarter(n), :], across(st[:, 3, quarter(n)], D), ALU.mult).then_inc(self.done, 1)

            def scalar(self):
                chain = Chain(nc.scalar, self.logs)
                for n in range(QUARTERS):
                    nc.scalar.wait_ge(self.centered, n + 1)
                    nc.scalar.activation(SQ2[:, quarter(n), :], self.dst[:, quarter(n), :], ACT.Square).then_inc(self.squared, 1)
                for n in range(QUARTERS):
                    nc.scalar.wait_ge(self.summed, n + 1)
                    chain.link(nc.scalar.activation(st[:, 2, quarter(n)], st[:, 1, quarter(n)], ACT.Ln, scale=1.0 / D, bias=bias[:, 2:3]))
                    nc.scalar.activation(st[:, 3, quarter(n)], st[:, 2, quarter(n)], ACT.Exp, scale=-0.5).then_inc(self.rstd, 1)

        class Turn:

            def __init__(self, name, src, rest):
                self.src, self.rest = src, rest
                self.first, self.left, self.second, self.third = sem(name + "_first"), sem(name + "_left"), sem(name + "_second"), sem(name + "_third")
                self.turned, self.copied0, self.copied1 = sem(name + "_turned"), sem(name + "_copied0"), sem(name + "_copied1")

            def vector(self):
                for n in range(QUARTERS):
                    nc.vector.wait_ge(self.first, n + 1)
                    nc.vector.tensor_tensor(self.rest[:, quarter(n), :], self.src[:, quarter(n), :], XS2[:, quarter(n), D:2 * D], ALU.subtract).then_inc(self.left, 1)

            def vector_copies(self):
                for n in range(QUARTERS):
                    nc.vector.wait_ge(self.turned, 2 * n + 2)
                    nc.vector.tensor_copy(XT[:, 1, 1024 * n:1024 * n + 1024], bank_bf16(4 + n)).then_inc(self.copied1, 1)

            def pool(self):
                for n in range(QUARTERS):
                    nc.gpsimd.wait_ge(self.second, n + 1)
                    nc.gpsimd.tensor_tensor(XS2[:, quarter(n), 2 * D:3 * D], self.rest[:, quarter(n), :], XS2[:, quarter(n), 0:D], ALU.subtract).then_inc(self.third, 1)

            def scalar(self, normed):
                for n in range(QUARTERS):
                    nc.scalar.wait_ge(normed, n + 1)
                    nc.scalar.copy(XS2[:, quarter(n), D:2 * D], self.src[:, quarter(n), :]).then_inc(self.first, 1)
                for n in range(QUARTERS):
                    nc.scalar.wait_ge(self.left, n + 1)
                    nc.scalar.copy(XS2[:, quarter(n), 0:D], self.rest[:, quarter(n), :]).then_inc(self.second, 1)
                for n in range(QUARTERS):
                    nc.scalar.wait_ge(self.turned, 2 * n + 1)
                    nc.scalar.copy(XT[:, 0, 1024 * n:1024 * n + 1024], bank_bf16(n)).then_inc(self.copied0, 1)

            def tensor(self):
                for n in range(QUARTERS):
                    nc.tensor.wait_ge(self.third, n + 1)
                    for kind in range(2):
                        for t in range(8):
                            m = nc.tensor.transpose(bank_bf16(4 * kind + n)[:, 128 * t:128 * t + 128], XS2[:, 8 * n + t, D * kind:D * kind + 128], identb[:])
                        m.then_inc(self.turned, 1)

        WB = sl("WB", [128, B, 4])
        WI = sl("WI", [1, B, 2], mybir.dt.int32)
        B1S = sl("B1S", [FH, 2 * B])
        XM = sl("XM", [D, B])
        R = sl("R", [B, 16, NE])
        RQ = sl("RQ", [B, 2, NE, NE])
        RC = sl("RC", [B, 16])
        R4 = sl("R4", [B, B, 4])
        OT = sl("OT", [NE, 3, B])
        BE = sl("BE", [NE, B, D])
        ones8 = sl("ones8", [B, 128])
        fnorm = Norm("fnorm", H, XN)
        fturn = Turn("fturn", XN, SQ2)
        vec_small = sem("vec_small"); rstep = sem("rstep"); r_pe = sem("r_pe"); r_act = sem("r_act"); residual_ready = sem("residual_ready")
        ones8_made = sem("ones8_made")
        with nc.Block("routing") as blk:
            @blk.sync
            def _(sp):
                sp.dma_start(RT[:], c_route).then_inc(route_in, 16)
                sp.dma_start(WR8[:], f_wr).then_inc(route_in, 16)
                sp.dma_start(BR8[:], bass.AP(tensor=f_br.tensor, offset=0, ap=[[0, B], [1, NE]])).then_inc(route_in, 16)
                sp.dma_start(B1[:], f_b1).then_inc(route_in, 16)
                sp.dma_start(B2[:], f_b2).then_inc(route_in, 16)
                sp.dma_start(W2[:], f_w2.rearrange("e f d -> f e d")).then_inc(route_in, 16)
                for n, v in enumerate((f_gamma, f_beta)):
                    sp.dma_start(GA[:, n, :], bass.AP(tensor=v.tensor, offset=0, ap=[[0, 128], [1, D]])).then_inc(route_in, 16)

            @blk.gpsimd
            def _(pool):
                nc.gpsimd.memset(ones8[:], 1.0).then_inc(ones8_made, 1)
                fturn.pool()

            @blk.scalar
            def _(act):
                nc.scalar.preload_act_table_set("natural_log_exp_and_others")
                fnorm.scalar()
                fturn.scalar(fnorm.done)
                act.wait_ge(rstep, 3)
                nc.scalar.activation(R[:, 2, :], R[:, 1, :], ACT.Exp).then_inc(r_act, 1)
                act.wait_ge(rstep, 13)
                nc.scalar.activation(R[:, 5, :], R[:, 4, :], ACT.Exp).then_inc(r_act, 1)
                act.wait_ge(rstep, 30)
                nc.scalar.activation(RC[:, 9:10], RC[:, 8:9], ACT.Exp).then_inc(r_act, 1)

            @blk.tensor
            def _(pe):
                pe.wait_ge(route_in, 16 * 8)
                for t in range(TILES):
                    rows = TP if t % 2 == 0 else LAST
                    b = t // 2
                    if t % QT == 0:
                        pe.wait_ge(fnorm.done, t // QT + 1)
                    mm = nc.tensor.matmul(PS[0:D, 7, 0:B], XN[0:rows, t, :], RT[0:rows, B - 1 - b:2 * B - 1 - b], start=(t == 0), stop=(t == TILES - 1))
                mm.then_inc(r_pe, 1)
                pe.wait_ge(rstep, 1)
                fturn.tensor()
                pe.wait_ge(fturn.copied0, QUARTERS)
                nc.tensor.matmul(PS[0:B, 1, 0:NE], XM[:], WR8[:], start=True, stop=True).then_inc(r_pe, 1)
                pe.wait_ge(ones8_made, 1)
                pe.wait_ge(rstep, 7)
                nc.tensor.matmul(PS[0:B, 2, 0:NE], ones8[:, 0:B], R[:, 3, :], start=True, stop=True).then_inc(r_pe, 1)
                pe.wait_ge(rstep, 36)
                for n, row in enumerate((10, 11, 12)):
                    tr = nc.tensor.transpose(PS[0:NE, 3, B * n:B * n + B], R[:, row, :], ident[0:B, 0:B])
                tr.then_inc(r_pe, 1)
                nc.tensor.matmul(PS[:, 0, 0:4 * B], ones8[:], R4[:].rearrange("p b f -> p (b f)"), start=True, stop=True).then_inc(r_pe, 1)
                pe.wait_ge(rstep, 38)
                nc.tensor.matmul(PS[:, 1, 0:2 * B], B1[:], OT[:, 0:2, :].rearrange("e s b -> e (s b)"), start=True, stop=True).then_inc(r_pe, 1)
                for n in range(2):
                    mm = nc.tensor.matmul(PS[:, 4 + n, :], ones8[0:NE, :], BE[:, 8 * n:8 * n + 8, :].rearrange("e b f -> e (b f)"), start=True, stop=True)
                mm.then_inc(r_pe, 1)

            @blk.vector
            def _(vec):
                fnorm.vector()
                fturn.vector()
                v = nc.vector
                c = Chain(vec, rstep)
                vec.wait_ge(r_pe, 1)
                c.link(v.tensor_copy(XM[:], PS[0:D, 7, 0:B]))
                fturn.vector_copies()
                vec.wait_ge(r_pe, 2)
                c.link(v.tensor_tensor(R[:, 0, :], PS[0:B, 1, 0:NE], BR8[:], ALU.add))
                nc.vector.tensor_reduce(RC[:, 0:1], R[:, 0, :], AX.X, ALU.max).then_inc(vec_small, 1)
                vec.wait_ge(vec_small, 1)
                c.link(v.tensor_scalar(R[:, 1, :], R[:, 0, :], RC[:, 0:1], None, ALU.subtract))
                vec.wait_ge(r_act, 1)
                c.link(v.tensor_reduce(RC[:, 1:2], R[:, 2, :], AX.X, ALU.add))
                c.link(v.reciprocal(RC[:, 2:3], RC[:, 1:2]))
                c.link(v.memset(RC[:, 3:4], 1.0))
                c.link(v.tensor_scalar(R[:, 3, :], R[:, 2, :], RC[:, 2:3], None, ALU.mult))
                vec.wait_ge(r_pe, 3)
                c.link(v.tensor_scalar(R[:, 6, :], PS[0:B, 2, 0:NE], float(NT), None, ALU.mult))
                c.link(v.reciprocal(R[:, 7, :], R[:, 6, :]))
                c.link(v.tensor_scalar(R[:, 8, :], R[:, 7, :], CAPACITY, 1.0, ALU.mult, ALU.min))
                c.link(v.tensor_tensor(R[:, 9, :], R[:, 3, :], R[:, 8, :], ALU.mult))
                c.link(v.tensor_reduce(RC[:, 4:5], R[:, 9, :], AX.X, ALU.max))
                c.link(v.tensor_scalar(R[:, 4, :], R[:, 9, :], RC[:, 4:5], None, ALU.subtract))
                vec.wait_ge(r_act, 2)
                c.link(v.tensor_reduce(RC[:, 5:6], R[:, 5, :], AX.X, ALU.add))
                c.link(v.reciprocal(RC[:, 6:7], RC[:, 5:6]))
                c.link(v.tensor_scalar(R[:, 13, :], R[:, 5, :], RC[:, 6:7], None, ALU.mult))
                w = R[:, 13, :]
                others = w.unsqueeze(1).broadcast_to([B, NE, NE])
                own = w.unsqueeze(2).broadcast_to([B, NE, NE])
                earlier = RT[0:B, EARLIER:EARLIER + NE * NE].rearrange("p (e j) -> p e j", e=NE)
                c.link(v.tensor_tensor(RQ[:, 0], others, own, ALU.is_gt))
                c.link(v.tensor_tensor(RQ[:, 1], others, own, ALU.is_equal))
                c.link(v.tensor_tensor(RQ[:, 1], RQ[:, 1], earlier, ALU.mult))
                c.link(v.tensor_tensor(RQ[:, 0], RQ[:, 0], RQ[:, 1], ALU.add))
                c.link(v.tensor_reduce(R[:, 14, :], RQ[:, 0], AX.X, ALU.add))
                c.link(v.tensor_scalar(R[:, 10, :], R[:, 14, :], 0.0, None, ALU.is_equal))
                c.link(v.tensor_scalar(R[:, 11, :], R[:, 14, :], 1.0, None, ALU.is_equal))
                numbers = RT[0:B, NUMBERS:NUMBERS + NE]
                for s in range(2):
                    c.link(v.tensor_tensor(R[:, 15, :], R[:, 10 + s, :], w, ALU.mult))
                    c.link(v.tensor_reduce(RC[:, 6 + s:7 + s], R[:, 15, :], AX.X, ALU.add))
                    if s == 0:
                        c.link(v.memset(RC[:, 15:16], 0.0))
                c.link(v.memset(RC[:, 14:15], 0.0))
                c.link(v.tensor_tensor(RC[:, 8:9], RC[:, 7:8], RC[:, 6:7], ALU.subtract))
                vec.wait_ge(r_act, 3)
                c.link(v.tensor_scalar(RC[:, 13:14], RC[:, 9:10], 1.0, None, ALU.add))
                c.link(v.reciprocal(RC[:, 10:11], RC[:, 13:14]))
                c.link(v.tensor_tensor(RC[:, 11:12], RC[:, 9:10], RC[:, 10:11], ALU.mult))
                c.link(v.tensor_scalar(R[:, 12, :], R[:, 10, :], RC[:, 10:11], None, ALU.mult))
                c.link(v.scalar_tensor_tensor(out=R[:, 12, :], in0=R[:, 11, :], scalar=RC[:, 11:12], in1=R[:, 12, :], op0=ALU.mult, op1=ALU.add))
                diag = ident[0:B, 0:B]
                small = Chain(vec, vec_small, 1)
                for s in range(2):
                    small.link(v.tensor_scalar(R4[:, :, s], diag, RC[:, 10 + s:11 + s], None, ALU.mult))
                    small.link(v.tensor_tensor(R[:, 15, :], R[:, 10 + s, :], numbers, ALU.mult))
                    small.link(v.tensor_reduce(RC[:, 12:13], R[:, 15, :], AX.X, ALU.add))
                    small.link(v.tensor_scalar(R4[:, :, 2 + s], diag, RC[:, 12:13], None, ALU.mult))
                c.link(v.memset(RC[:, 0:1], 0.0))
                vec.wait_ge(r_pe, 4)
                c.link(v.tensor_copy(OT[:].rearrange("e s b -> e (s b)"), PS[0:NE, 3, 0:3 * B]))
                c.link(v.tensor_tensor(BE[:], B2[:].unsqueeze(1).broadcast_to([NE, B, D]), OT[:, 2, :].unsqueeze(2).broadcast_to([NE, B, D]), ALU.mult))
                vec.wait_ge(r_pe, 5)
                c.link(v.tensor_copy(WB[:].rearrange("p b f -> p (b f)"), PS[:, 0, 0:4 * B]))
                c.link(v.tensor_copy(WI[:], WB[0:1, :, 2:4]))
                vec.wait_ge(r_pe, 6)
                c.link(v.tensor_copy(B1S[:], PS[:, 1, 0:2 * B]))
                vec.wait_ge(r_pe, 7)
                for n in range(2):
                    for j in range(2):
                        tiles = slice(B * n, B * n + B)
                        out4 = XR[:, tiles, :].rearrange("p (b j) f -> p j b f", j=2)[:, j]
                        in4 = XN[:, tiles, :].rearrange("p (b j) f -> p j b f", j=2)[:, j]
                        c.link(v.tensor_tensor(out4, PS[:, 4 + n, :].rearrange("p (b f) -> p b f", f=D), in4, ALU.add))

        with ExitStack() as three:
            def sa(name, shape, dt=F32):
                return three.enter_context(nc.sbuf_tensor(name, shape, dt))
            GE = [sa(f"GE{p}", [FH, 2, NTP]) for p in range(2)]
            PICKS = 4
            TA = sa("TA", [128, 2, 2, D])
            P1 = sa("P1", [128, PICKS, 2, 3, FH], BF16)
            P2 = sa("P2", [128, PICKS, 2, D])
            weights_picked = sem("weights_picked"); vec_passed = sem("vec_passed")
            hidden_done = sem("hidden_done"); gelu_ready = sem("gelu_ready"); expert_done = sem("expert_done")
            mix_chain = sem("mix_chain"); mixed = sem("mixed")

            def schedule(eng, step):
                step(0, 0)
                with eng.Fori(0, (B - PICKS) // PICKS) as i:
                    for c in range(1, 1 + PICKS):
                        step(i * PICKS + c, c)
                for n in range(B - PICKS + 1, B - 1):
                    step(n, n)

            with nc.Block("ffn") as blk:
                @blk.tensor
                def _(pe):
                    def hidden(n, p, w):
                        after(pe, gelu_ready, (n - 1) * 2)
                        pe.wait_ge(weights_picked, n + 1)
                        for s in range(2):
                            for k in range(3):
                                mm = nc.tensor.matmul(PS[:, p, NTP * s:NTP * s + NTP], P1[:, w, s, k, :], XT[:, k // 2, bass.ds(n * NTP, NTP)], start=(k == 0), stop=(k == 2))
                        mm.then_inc(hidden_done, 1)

                    def output(n, p, w):
                        after(pe, mixed, n - 1)
                        pe.wait_ge(gelu_ready, n * 2 + 2)
                        for s in range(2):
                            for j in range(2):
                                mm = nc.tensor.matmul(PS[:, 2 + p, D * (2 * j + s):D * (2 * j + s) + D], GE[p][:, s, TP * j:TP * j + TP], P2[:, w, s, :], start=True, stop=True)
                        mm.then_inc(expert_done, 1)

                    def step(n, c):
                        hidden(n + 1, (c + 1) % 2, (c + 1) % PICKS)
                        output(n, c % 2, c % PICKS)

                    hidden(0, 0, 0)
                    schedule(pe, step)
                    output(B - 1, 1, (B - 1) % PICKS)

                @blk.scalar
                def _(act):
                    nc.scalar.preload_act_table(ACT.Gelu)

                    def gelu(n, p):
                        act.wait_ge(hidden_done, n + 1)
                        after(act, expert_done, n - 1)
                        for s in range(2):
                            nc.scalar.activation(GE[p][:, s, :], PS[:, p, NTP * s:NTP * s + NTP], ACT.Gelu, bias=B1S[:, bass.ds(n + B * s, 1)]).then_inc(gelu_ready, 1)

                    gelu(0, 0)
                    gelu(1, 1)
                    with act.Fori(0, 7) as i:
                        gelu(i * 2 + 2, 0)
                        gelu(i * 2 + 3, 1)

                @blk.vector
                def _(vec):
                    chain = Chain(vec, mix_chain)

                    def pick(n, w):
                        after(vec, hidden_done, n - (PICKS - 1))
                        wait_apart(vec, expert_done, n - (PICKS - 1), vec_passed)
                        for s in range(2):
                            e = vec.value_load(WI[0:1, bass.ds(n, 1), s:s + 1], min_val=0, max_val=NE - 1)
                            nc.vector.tensor_copy(P1[:, w, s], WS[:, :, bass.ds(e * FH + NQKVG, FH)])
                            copy = nc.vector.tensor_copy(P2[:, w, s, :], W2[:, bass.ds(e, 1), :].rearrange("p e d -> p (e d)"))
                        copy.then_inc(weights_picked, 1)

                    def mix(n, p):
                        vec.wait_ge(expert_done, n + 1)
                        y = PS[:, 2 + p, 0:4 * D].rearrange("p (j s f) -> p s j f", j=2, s=2)
                        xr = XR[:, bass.ds(n * 2, 2), :]
                        chain.at = n
                        chain.link(nc.vector.scalar_tensor_tensor(out=TA[:, p], in0=y[:, 0], scalar=WB[:, bass.ds(n, 1), 0], in1=xr, op0=ALU.mult, op1=ALU.add))
                        nc.vector.scalar_tensor_tensor(out=xr, in0=y[:, 1], scalar=WB[:, bass.ds(n, 1), 1], in1=TA[:, p], op0=ALU.mult, op1=ALU.add).then_inc(mixed, 1)

                    def step(n, c):
                        if c < B - PICKS + 1:
                            pick(n + PICKS - 1, (c + PICKS - 1) % PICKS)
                        mix(n, c % 2)

                    for n in range(PICKS - 1):
                        pick(n, n)
                    schedule(vec, step)
                    mix(B - 1, 1)

        onorm = Norm("onorm", XR, XR)
        anorm = Norm("anorm", H, XN)
        flat_scratch = nc.dram_tensor("flat_scratch", (B, NTP, D), F32).ap()
        back_scratch = nc.dram_tensor("back_scratch", (B, NTP, D), F32).ap()

        def as_rows(scratch, pair):
            return bass.AP(tensor=scratch.tensor, offset=pair * (2 * NTP * D), ap=[[NTP * D, 2], [NT, D], [1, NT]])

        with ExitStack() as four:
            def sa(name, shape, dt=F32):
                return four.enter_context(nc.sbuf_tensor(name, shape, dt))
            AW = sa("AW", [128, 4, 128])
            AB = sa("AB", [128, 2])
            AR = sa("AR", [128, 2, 128])
            FL = [sa(f"FL{p}", [128, NTP]) for p in range(2)]
            KB = sa("KB", [128, NTP]); KE = [sa(f"KE{p}", [128, NTP]) for p in range(2)]
            KM = sa("KM", [128, 4])
            QB = sa("QB", [128, 2, 128]); QE = [sa(f"QE{p}", [128, 2, 128]) for p in range(2)]
            QM = sa("QM", [128, 4, 32])
            VT = [sa(f"VT{p}", [128, 2, 128]) for p in range(2)]
            KT = sa("KT", [128, 2, 128]); QF = sa("QF", [128, NTP]); CT = sa("CT", [128, 128])
            AG = sa("AG", [128, NTP]); OF = [sa(f"OF{p}", [128, NTP]) for p in range(2)]
            a_weights_in = sem("a_weights_in"); aw_zeroed = sem("aw_zeroed"); residual_added = sem("residual_added")
            gamma_chain = sem("gamma_chain"); beta_added = sem("beta_added"); flat_written = [sem(f"flat_written_{n}") for n in range(QUARTERS)]; dummies_written = sem("dummies_written"); fl_zeroed = sem("fl_zeroed")
            flat_in = [sem("flat_in_even"), sem("flat_in_odd")]
            ka_done = sem("ka_done"); qa_done = sem("qa_done"); va_done = sem("va_done"); kb_ready = sem("kb_ready"); kmax_ready = sem("kmax_ready")
            ke_ready = sem("ke_ready"); ka_chain = sem("ka_chain"); qshift_ready = sem("qshift_ready"); qexp_ready = sem("qexp_ready")
            qa_chain = sem("qa_chain"); qsoft_ready = sem("qsoft_ready"); vt_ready = sem("vt_ready")
            kt_turned = sem("kt_turned"); qf_turned = sem("qf_turned"); kt_copied = sem("kt_copied"); qf_copied = sem("qf_copied")
            context_done = sem("context_done"); context_ready = sem("context_ready"); agg_done = sem("agg_done")
            agg_copied = sem("agg_copied"); proj_done = sem("proj_done"); of_ready = sem("of_ready"); of_written = [sem("of_written_even"), sem("of_written_odd")]
            back_in = [sem(f"back_in_{n}") for n in range(QUARTERS)]

            with nc.Block("residual") as blk:
                @blk.gpsimd
                def _(pool):
                    nc.gpsimd.memset(AW[:], 0.0).then_inc(aw_zeroed, 1)
                    for p in range(2):
                        m = nc.gpsimd.memset(FL[p][:], 0.0)
                    m.then_inc(fl_zeroed, 1)
                    nc.gpsimd.tensor_tensor(H[:], H[:], GA[:, 1, :].unsqueeze(1).broadcast_to([128, TILES, D]), ALU.add).then_inc(beta_added, 1)

                @blk.sync
                def _(sp):
                    sp.wait_ge(aw_zeroed, 1)
                    for n, w in enumerate((a_wk, a_wq, a_wv, a_wr)):
                        for half in (0, 64):
                            sp.dma_start(AW[half:half + 64, n, half:half + 64], w).then_inc(a_weights_in, 16)
                    for half in (0, 64):
                        for n, w in enumerate((a_bk, a_br)):
                            sp.dma_start(AB[half:half + 64, n:n + 1], w.rearrange("(p a) -> p a", a=1), allow_slow_non_contiguous=True).then_inc(a_weights_in, 16)
                        for n, w in enumerate((a_bq, a_bv)):
                            sp.dma_start(AR[:, n, half:half + 64], bass.AP(tensor=w.tensor, offset=0, ap=[[0, 128], [1, D]])).then_inc(a_weights_in, 16)
                    for n in range(QUARTERS):
                        sp.wait_ge(anorm.done, n + 1)
                        src = XN[:, quarter(n), :]
                        dst = flat_scratch[4 * n:4 * n + 4].rearrange("b (j t) f -> t (b j) f", j=2)
                        sp.dma_start(dst, src).then_inc(flat_written[n], 16)
                    sp.dma_start(back_scratch[:, NT, :], XN[0:B, 0, :]).then_inc(dummies_written, 16)
                    sp.wait_ge(a_weights_in, 16 * 16)

                @blk.scalar
                def _(act):
                    nc.scalar.preload_act_table_set("natural_log_exp_and_others")
                    onorm.scalar()
                    anorm.scalar()

                @blk.vector
                def _(vec):
                    onorm.vector()
                    chain = Chain(vec, gamma_chain)
                    for n in range(QUARTERS):
                        xr = XR[:, quarter(n), :]
                        if n == 0:
                            vec.wait_ge(onorm.done, QUARTERS)
                            vec.wait_ge(beta_added, 1)
                        chain.link(nc.vector.tensor_tensor(xr, xr, GA[:, 0, :].unsqueeze(1).broadcast_to([128, QT, D]), ALU.mult))
                        nc.vector.tensor_tensor(H[:, quarter(n), :], H[:, quarter(n), :], xr, ALU.add).then_inc(residual_added, 1)
                    anorm.vector(residual_added)

            def schedule(eng, step):
                def at(n):
                    return n, n % 2, n // 2

                step(None, at(0))
                step(at(0), at(1))
                step(at(1), at(2))
                with eng.Fori(0, PAIRS // 2 - 2) as i:
                    step((i * 2 + 2, 0, i + 1), (i * 2 + 3, 1, i + 1))
                    step((i * 2 + 3, 1, i + 1), (i * 2 + 4, 0, i + 2))
                step(at(PAIRS - 2), at(PAIRS - 1))
                step(at(PAIRS - 1), None)

            with nc.Block("linear_attention") as blk:
                @blk.sync
                def _(sp):
                    def load(n):
                        p = n % 2
                        sp.wait_ge(flat_written[n // 2], 16)
                        after(sp, va_done, n - 1)
                        sp.dma_start(FL[p][:, 0:NT], as_rows(flat_scratch, n)).then_inc(flat_in[p], 16)

                    def store(n):
                        sp.wait_ge(of_ready, n + 1)
                        sp.dma_start(as_rows(back_scratch, n), OF[n % 2][:, 0:NT]).then_inc(of_written[n % 2], 16)

                    def back(q):
                        for p in range(2):
                            sp.wait_ge(of_written[p], 16 * (q + 1))
                        sp.dma_start(XR[:, quarter(q), :], back_scratch[4 * q:4 * q + 4].rearrange("b (j t) f -> t (b j) f", j=2)).then_inc(back_in[q], 16)

                    sp.wait_ge(dummies_written, 16)
                    load(0)
                    load(1)
                    for n in range(PAIRS):
                        if n + 2 < PAIRS:
                            load(n + 2)
                        store(n)
                        if n > 2 and n % 2:
                            back((n - 3) // 2)
                    back(QUARTERS - 1)

                @blk.tensor
                def _(pe):
                    def project_queries(n, p, turn):
                        pe.wait_ge(flat_in[p], turn * 16 + 16)
                        after(pe, qshift_ready, n - 1)
                        after(pe, vt_ready, n - 1)
                        for j in range(2):
                            mm = nc.tensor.matmul(PS[:, 2 + p, 128 * j:128 * j + 128], FL[p][:, TP * j:TP * j + TP], AW[:, 1, :], start=True, stop=True)
                        mm.then_inc(qa_done, 1)

                    def project_keys(n, p):
                        after(pe, kb_ready, n - 1)
                        nc.tensor.matmul(PS[:, p, 0:NTP], AW[:, 0, :], FL[p][:], start=True, stop=True).then_inc(ka_done, 1)

                    def project_values(n, p):
                        pe.wait_ge(qshift_ready, n + 1)
                        for j in range(2):
                            mm = nc.tensor.matmul(PS[:, 2 + p, 256 + 128 * j:384 + 128 * j], FL[p][:, TP * j:TP * j + TP], AW[:, 2, :], start=True, stop=True)
                        mm.then_inc(va_done, 1)

                    def turn_both(n, p):
                        after(pe, kt_copied, n)
                        pe.wait_ge(ke_ready, n + 1)
                        for j in range(2):
                            rows = TP if j == 0 else LAST
                            tr = nc.tensor.transpose(PS[0:rows, 4, 128 * j:128 * j + 128], KE[p][:, TP * j:TP * j + rows], ident[:])
                        tr.then_inc(kt_turned, 1)
                        after(pe, qf_copied, n)
                        pe.wait_ge(qsoft_ready, n + 1)
                        for j in range(2):
                            tr = nc.tensor.transpose(PS[:, 5, 128 * j:128 * j + 128], QE[p][:, j, :], ident[:])
                        tr.then_inc(qf_turned, 1)

                    def contexts(n, p):
                        pe.wait_ge(kt_copied, n + 1)
                        pe.wait_ge(vt_ready, n + 1)
                        after(pe, agg_copied, n)
                        for j in range(2):
                            rows = TP if j == 0 else LAST
                            mm = nc.tensor.matmul(PS[:, 6, 0:128], KT[0:rows, j, :], VT[p][0:rows, j, :], start=(j == 0), stop=(j == 1))
                        mm.then_inc(context_done, 1)

                    def attend(n):
                        pe.wait_ge(context_ready, n + 1)
                        pe.wait_ge(qf_copied, n + 1)
                        nc.tensor.matmul(PS[:, 6, 0:NTP], CT[:], QF[:], start=True, stop=True).then_inc(agg_done, 1)

                    def project_out(n):
                        pe.wait_ge(agg_copied, n + 1)
                        after(pe, of_ready, n)
                        nc.tensor.matmul(PS[:, 7, 0:NTP], AW[:, 3, :], AG[:], start=True, stop=True).then_inc(proj_done, 1)

                    def step(now, coming):
                        if now:
                            turn_both(now[0], now[1])
                        if coming:
                            project_queries(*coming)
                        if now:
                            contexts(now[0], now[1])
                        if coming:
                            project_keys(coming[0], coming[1])
                        if now:
                            attend(now[0])
                        if coming:
                            project_values(coming[0], coming[1])
                        if now:
                            project_out(now[0])

                    schedule(pe, step)

                @blk.scalar
                def _(act):
                    def soft_keys(n, p):
                        after(act, kt_turned, n - 1)
                        act.wait_ge(kmax_ready, n + 1)
                        nc.scalar.activation(KE[p][:, 0:NT], KB[:, 0:NT], ACT.Exp, bias=KM[:, 0:1], accum_out=KM[:, 2 + p:3 + p]).then_inc(ke_ready, 1)

                    def soft_queries(n, p):
                        after(act, qf_turned, n - 1)
                        act.wait_ge(qshift_ready, n + 1)
                        nc.scalar.activation(QE[p][:], QB[:], ACT.Exp).then_inc(qexp_ready, 1)

                    def copy_turned(n):
                        act.wait_ge(kt_turned, n + 1)
                        after(act, context_done, n)
                        nc.scalar.copy(KT[:, 0, :], PS[:, 4, 0:128])
                        nc.scalar.copy(KT[0:LAST, 1, :], PS[0:LAST, 4, 128:256]).then_inc(kt_copied, 1)
                        act.wait_ge(qf_turned, n + 1)
                        after(act, agg_done, n)
                        nc.scalar.copy(QF[:], PS[:, 5, 0:NTP]).then_inc(qf_copied, 1)

                    def copy_attended(n):
                        act.wait_ge(agg_done, n + 1)
                        after(act, proj_done, n)
                        nc.scalar.copy(AG[:], PS[:, 6, 0:NTP]).then_inc(agg_copied, 1)

                    def add_bias(n, p, turn):
                        act.wait_ge(proj_done, n + 1)
                        after(act, of_written[p], turn * 16)
                        nc.scalar.activation(OF[p][:], PS[:, 7, 0:NTP], ACT.Identity, bias=AB[:, 1:2]).then_inc(of_ready, 1)

                    def step(now, coming):
                        if now:
                            copy_turned(now[0])
                        if coming:
                            soft_queries(coming[0], coming[1])
                        if now:
                            copy_attended(now[0])
                        if coming:
                            soft_keys(coming[0], coming[1])
                        if now:
                            add_bias(*now)

                    schedule(act, step)

                @blk.vector
                def _(vec):
                    kchain = Chain(vec, ka_chain)
                    qchain = Chain(vec, qa_chain)

                    def queries(n, p):
                        qchain.at = n * 4
                        vec.wait_ge(qa_done, n + 1)
                        after(vec, qexp_ready, n)
                        half = PS[:, 2 + p, 0:256].rearrange("p (j c) -> p j c", j=2)
                        qchain.link(nc.vector.tensor_tensor(QB[:], half, AR[:, 0, :].unsqueeze(1).broadcast_to([128, 2, 128]), ALU.add))
                        groups = QB[:].rearrange("p j (g k) -> p (j g) k", k=LK)
                        qchain.link(nc.vector.tensor_reduce(QM[:, 0, :], groups, AX.X, ALU.max))
                        nc.vector.tensor_tensor(groups, groups, QM[:, 0, :].unsqueeze(2).broadcast_to([128, 32, LK]), ALU.subtract).then_inc(qshift_ready, 1)

                    def divide_queries(n, p):
                        vec.wait_ge(qexp_ready, n + 1)
                        egroups = QE[p][:].rearrange("p j (g k) -> p (j g) k", k=LK)
                        qchain.link(nc.vector.tensor_reduce(QM[:, 1, :], egroups, AX.X, ALU.add))
                        qchain.link(nc.vector.reciprocal(QM[:, 2, :], QM[:, 1, :]))
                        nc.vector.tensor_tensor(egroups, egroups, QM[:, 2, :].unsqueeze(2).broadcast_to([128, 32, LK]), ALU.mult).then_inc(qsoft_ready, 1)

                    def keys(n, p):
                        vec.wait_ge(ka_done, n + 1)
                        after(vec, ke_ready, n)
                        nc.vector.tensor_scalar(KB[:, 0:NT], PS[:, p, 0:NT], AB[:, 0:1], None, ALU.add).then_inc(kb_ready, 1)
                        vec.wait_ge(kb_ready, n + 1)
                        nc.vector.tensor_reduce(KM[:, 0:1], KB[:, 0:NT], AX.X, ALU.max, negate=True).then_inc(kmax_ready, 1)

                    def values(n, p):
                        vec.wait_ge(va_done, n + 1)
                        after(vec, context_done, n - 1)
                        half = PS[:, 2 + p, 256:512].rearrange("p (j c) -> p j c", j=2)
                        nc.vector.tensor_tensor(VT[p][:], half, AR[:, 1, :].unsqueeze(1).broadcast_to([128, 2, 128]), ALU.add).then_inc(vt_ready, 1)

                    def context(n, p):
                        vec.wait_ge(ke_ready, n + 1)
                        after(vec, context_ready, n)
                        kchain.at = n
                        kchain.link(nc.vector.reciprocal(KM[:, 1:2], KM[:, 2 + p:3 + p]))
                        vec.wait_ge(context_done, n + 1)
                        after(vec, agg_done, n)
                        nc.vector.scalar_tensor_tensor(out=CT[:], in0=PS[:, 6, 0:128], scalar=KM[:, 1:2], in1=RT[:, HEADS:HEADS + 128],
                                                       op0=ALU.mult, op1=ALU.mult).then_inc(context_ready, 1)

                    def step(now, coming):
                        if now:
                            context(now[0], now[1])
                        if coming:
                            n, p, _ = coming
                            queries(n, p)
                            keys(n, p)
                            divide_queries(n, p)
                            values(n, p)

                    schedule(vec, step)

        mnorm = Norm("mnorm", H, XN)
        mturn = Turn("mturn", XN, SQ2)
        HB = XR
        M1 = NQKVG + NW1
        GATE = M1 + D + ME * MH
        GROUPS = 1 + ME
        with ExitStack() as five:
            def sa(name, shape, dt=F32):
                return five.enter_context(nc.sbuf_tensor(name, shape, dt))
            MW2 = sa("MW2", [MH, ME, D])
            SW2 = sa("SW2", [128, 128])
            EW3 = sa("EW3", [128, ME // 2, 128])
            SW3 = sa("SW3", [128, D])
            MB1 = sa("MB1", [128, GROUPS])
            MB2 = sa("MB2", [128, 1 + ME // 2])
            SB3 = sa("SB3", [128, D])
            EB3 = sa("EB3", [128, D])
            GBB = sa("GBB", [128, ME])
            BD = sa("BD", [128, TILES, D])
            ZL = sa("ZL", [128, TILES, ME])
            G1 = sa("G1", [128, TILES, ME])
            G2 = sa("G2", [128, TILES, ME])
            GQ = sa("GQ", [128, 2, TILES, ME, ME])
            GS = sa("GS", [128, 6, TILES])
            G5 = sa("G5", [128, TILES, GROUPS])
            GT = sa("GT", [128, TP])
            H1 = sa("H1", [128, GROUPS, NTP])
            H2 = sa("H2", [128, 1 + ME // 2, NTP])
            WM = sa("WM", [128, 2, GROUPS, D])
            MO = sa("MO", [128, 2, D])
            sp_passed = sem("sp_passed_experts")
            attention_added = sem("attention_added")
            m_zeroed = sem("m_zeroed"); m_weights_in = sem("m_weights_in"); biases_spread = sem("biases_spread")
            logits_done = sem("logits_done"); gate_steps = sem("gate_steps"); gate_exps = sem("gate_exps")
            weights_ready = sem("weights_ready"); weights_turned = sem("weights_turned"); turned_copied = sem("turned_copied")
            bias_done = sem("bias_done"); sums_ready = sem("sums_ready")
            first_done = sem("first_done"); first_relu = sem("first_relu"); second_done = sem("second_done")
            second_relu = sem("second_relu"); third_done = sem("third_done"); weighted = sem("weighted")
            sum_chain = sem("sum_chain"); token_ready = sem("token_ready"); out_written = sem("out_written")

            with nc.Block("gates") as blk:
                @blk.sync
                def _(sp):
                    sp.dma_start(GBB[:], bass.AP(tensor=m_gb.tensor, offset=0, ap=[[0, 128], [1, ME]])).then_inc(m_weights_in, 16)
                    sp.dma_start(SB3[:], bass.AP(tensor=m_sb3.tensor, offset=0, ap=[[0, 128], [1, D]])).then_inc(m_weights_in, 16)
                    sp.dma_start(EB3[:], bass.AP(tensor=m_eb3.tensor, offset=0, ap=[[0, TILES], [D, ME], [1, D]])).then_inc(m_weights_in, 16)
                    sp.dma_start(MW2[:], m_ew2.rearrange("e h g -> h e g")).then_inc(m_weights_in, 16)
                    sp.dma_start(SW3[:], m_sw3).then_inc(m_weights_in, 16)
                    sp.dma_start(MB1[:, 1:GROUPS], m_eb1.rearrange("e h -> h e"), allow_slow_non_contiguous=True).then_inc(m_weights_in, 16)
                    for half in range(2):
                        sp.dma_start(MB2[D * half:D * half + D, 0:2], m_eb2.rearrange("(q r) g -> g r q", r=2)[:, half], allow_slow_non_contiguous=True).then_inc(m_weights_in, 16)
                    sp.dma_start(MB2[:, 2:3], m_sb2.rearrange("(p a) -> p a", a=1), allow_slow_non_contiguous=True).then_inc(m_weights_in, 16)
                    sp.wait_ge(m_zeroed, 1)
                    sp.dma_start(MB1[0:D, 0:1], m_sb1.rearrange("(p a) -> p a", a=1), allow_slow_non_contiguous=True).then_inc(m_weights_in, 16)
                    sp.dma_start(SW2[0:D, :], m_sw2).then_inc(m_weights_in, 16)
                    for half in range(2):
                        sp.dma_start(EW3[D * half:D * half + D, :, D * half:D * half + D], m_ew3.rearrange("(q r) g f -> r g q f", r=2)[half]).then_inc(m_weights_in, 16)
                    sp.wait_ge(m_weights_in, 16 * 13)

                @blk.gpsimd
                def _(pool):
                    nc.gpsimd.memset(MB1[:, 0:1], 0.0)
                    nc.gpsimd.memset(SW2[:], 0.0)
                    nc.gpsimd.memset(G5[:, :, ME:GROUPS], 1.0)
                    nc.gpsimd.memset(EW3[:], 0.0).then_inc(m_zeroed, 1)
                    mturn.pool()
                    pool.wait_ge(m_weights_in, 16 * 13)
                    select = RT[:, SELECT:SELECT + TILES].unsqueeze(2).broadcast_to([128, TILES, D])
                    nc.gpsimd.tensor_tensor(BD[:], EB3[:].unsqueeze(1).broadcast_to([128, TILES, D]), select, ALU.mult).then_inc(biases_spread, 1)

                @blk.scalar
                def _(act):
                    nc.scalar.preload_act_table_set("natural_log_exp_and_others")
                    mnorm.scalar()
                    mturn.scalar(mnorm.done)
                    act.wait_ge(gate_steps, 3)
                    nc.scalar.activation(G1[:], ZL[:], ACT.Exp).then_inc(gate_exps, 1)
                    act.wait_ge(gate_steps, 17)
                    nc.scalar.activation(GS[:, 4, :], GS[:, 3, :], ACT.Exp).then_inc(gate_exps, 1)

                @blk.tensor
                def _(pe):
                    mturn.tensor()
                    pe.wait_ge(mturn.copied0, QUARTERS)
                    pe.wait_ge(mturn.copied1, QUARTERS)
                    for t in range(TILES):
                        for s in range(3):
                            mm = nc.tensor.matmul(PS[:, 0, ME * t:ME * t + ME], XT[:, s // 2, TP * t:TP * t + TP], WS[:, s, GATE:GATE + ME], start=(s == 0), stop=(s == 2))
                    mm.then_inc(logits_done, 1)
                    pe.wait_ge(weights_ready, 1)
                    nc.tensor.transpose(PS[:, 1, 0:TP], G1[:].rearrange("p t e -> p (t e)"), ident[:]).then_inc(weights_turned, 1)
                    pe.wait_ge(turned_copied, 1)
                    pe.wait_ge(biases_spread, 1)
                    for n in range(QUARTERS):
                        nc.tensor.matmul(PS[:, 2 + n, :], GT[:], BD[:, quarter(n), :], start=True, stop=True).then_inc(bias_done, 1)

                @blk.vector
                def _(vec):
                    for n in range(QUARTERS):
                        vec.wait_ge(back_in[n], 16)
                        nc.vector.tensor_tensor(H[:, quarter(n), :], H[:, quarter(n), :], XR[:, quarter(n), :], ALU.add).then_inc(attention_added, 1)
                    mnorm.vector(attention_added)
                    mturn.vector()
                    mturn.vector_copies()
                    c = Chain(vec, gate_steps)
                    v = nc.vector

                    def each(column):
                        return column.unsqueeze(2).broadcast_to([128, TILES, ME])

                    vec.wait_ge(logits_done, 1)
                    vec.wait_ge(m_weights_in, 16 * 13)
                    c.link(v.tensor_tensor(ZL[:], PS[:, 0, 0:TILES * ME].rearrange("p (t e) -> p t e", e=ME), GBB[:].unsqueeze(1).broadcast_to([128, TILES, ME]), ALU.add))
                    c.link(v.tensor_reduce(GS[:, 0, :], ZL[:], AX.X, ALU.max))
                    c.link(v.tensor_tensor(ZL[:], ZL[:], each(GS[:, 0, :]), ALU.subtract))
                    vec.wait_ge(gate_exps, 1)
                    c.link(v.tensor_reduce(GS[:, 0, :], G1[:], AX.X, ALU.add))
                    c.link(v.reciprocal(GS[:, 1, :], GS[:, 0, :]))
                    c.link(v.tensor_tensor(G1[:], G1[:], each(GS[:, 1, :]), ALU.mult))
                    others = G1[:].unsqueeze(2).broadcast_to([128, TILES, ME, ME])
                    own = G1[:].unsqueeze(3).broadcast_to([128, TILES, ME, ME])
                    earlier = RT[:, EARLIER4:EARLIER4 + ME * ME].rearrange("p (e j) -> p e j", e=ME).unsqueeze(1).broadcast_to([128, TILES, ME, ME])
                    c.step(v.tensor_tensor(GQ[:, 0], others, own, ALU.is_gt))
                    c.link(v.tensor_tensor(GQ[:, 1], others, own, ALU.is_equal))
                    c.link(v.tensor_tensor(GQ[:, 1], GQ[:, 1], earlier, ALU.mult))
                    c.link(v.tensor_tensor(GQ[:, 0], GQ[:, 0], GQ[:, 1], ALU.add))
                    c.link(v.tensor_reduce(G2[:], GQ[:, 0], AX.X, ALU.add))
                    for s in range(2):
                        c.link(v.scalar_tensor_tensor(out=GQ[:, 0, :, 0, :], in0=G2[:], scalar=float(s), in1=G1[:], op0=ALU.is_equal, op1=ALU.mult))
                        c.link(v.tensor_reduce(GS[:, 1 + s, :], GQ[:, 0, :, 0, :], AX.X, ALU.add))
                    c.link(v.memset(GS[:, 5, :], 1.0))
                    c.link(v.tensor_tensor(GS[:, 3, :], GS[:, 2, :], GS[:, 1, :], ALU.subtract))
                    vec.wait_ge(gate_exps, 2)
                    c.link(v.tensor_tensor(GS[:, 0, :], GS[:, 4, :], GS[:, 5, :], ALU.add))
                    c.link(v.reciprocal(GS[:, 1, :], GS[:, 0, :]))
                    c.link(v.tensor_tensor(GS[:, 2, :], GS[:, 4, :], GS[:, 1, :], ALU.mult))
                    for s in range(2):
                        c.link(v.scalar_tensor_tensor(out=GQ[:, s, :, 0, :], in0=G2[:], scalar=float(s), in1=each(GS[:, 1 + s, :]), op0=ALU.is_equal, op1=ALU.mult))
                    c.link(v.tensor_tensor(G5[:, :, 0:ME], GQ[:, 0, :, 0, :], GQ[:, 1, :, 0, :], ALU.add))
                    v.tensor_copy(G1[:], G5[:, :, 0:ME]).then_inc(weights_ready, 1)
                    c.link(v.tensor_tensor(HB[:], H[:], SB3[:].unsqueeze(1).broadcast_to([128, TILES, D]), ALU.add))
                    vec.wait_ge(weights_turned, 1)
                    v.tensor_copy(GT[:], PS[:, 1, 0:TP]).then_inc(turned_copied, 1)
                    for n in range(QUARTERS):
                        vec.wait_ge(bias_done, n + 1)
                        v.tensor_tensor(HB[:, quarter(n), :], HB[:, quarter(n), :], PS[:, 2 + n, :].rearrange("p (t f) -> p t f", f=D), ALU.add).then_inc(sums_ready, 1)
                    vec.wait_ge(sums_ready, QUARTERS)

            with nc.Block("experts") as blk:
                @blk.tensor
                def _(pe):
                    def place(g):
                        return PS[:, g // 2, NTP * (g % 2):NTP * (g % 2) + NTP]

                    def first(n):
                        for g in range(GROUPS):
                            if g % 2 == 0:
                                after(pe, first_relu, (n - 1) * GROUPS + min(g + 2, GROUPS))
                            column = M1 if g == 0 else M1 + D + MH * (g - 1)
                            for s in range(3):
                                mm = nc.tensor.matmul(place(g), WS[:, s, column:column + 128], XT[:, s // 2, bass.ds(n * NTP, NTP)], start=(s == 0), stop=(s == 2))
                            mm.then_inc(first_done, 1)

                    def second(n):
                        after(pe, second_relu, n * 3)
                        pe.wait_ge(first_relu, n * GROUPS + GROUPS)
                        for q in range(ME // 2):
                            for half in range(2):
                                mm = nc.tensor.matmul(PS[D * half:D * half + D, 3, NTP * q:NTP * q + NTP], MW2[:, 2 * q + half, :], H1[:, 1 + 2 * q + half, :], start=True, stop=True)
                        mm.then_inc(second_done, 1)
                        nc.tensor.matmul(PS[:, 4, 0:NTP], SW2[:], H1[:, 0, :], start=True, stop=True).then_inc(second_done, 1)

                    def third(n):
                        pe.wait_ge(second_relu, n * 3 + 3)
                        after(pe, weighted, n)
                        for j in range(2):
                            tokens = slice(TP * j, TP * j + TP)
                            for q in range(ME // 2):
                                nc.tensor.matmul(PS[:, 5 + j, 128 * q:128 * q + 128], H2[:, q, tokens], EW3[:, q, :], start=True, stop=True)
                            mm = nc.tensor.matmul(PS[:, 5 + j, ME * D:GROUPS * D], H2[:, 2, tokens], SW3[:], start=True, stop=True)
                        mm.then_inc(third_done, 1)

                    first(0)
                    second(0)
                    first(1)
                    third(0)
                    with pe.Fori(0, B - 2) as i:
                        second(i + 1)
                        first(i + 2)
                        third(i + 1)
                    second(B - 1)
                    third(B - 1)

                @blk.scalar
                def _(act):
                    def first(n):
                        for g in range(GROUPS):
                            act.wait_ge(first_done, n * GROUPS + (min(g // 2 * 2 + 2, GROUPS)))
                            if g == 0:
                                after(act, second_done, n * 2)
                            nc.scalar.activation(H1[:, g, :], PS[:, g // 2, NTP * (g % 2):NTP * (g % 2) + NTP], ACT.Relu, bias=MB1[:, g:g + 1]).then_inc(first_relu, 1)

                    def second(n):
                        after(act, third_done, n)
                        for q in range(3):
                            act.wait_ge(second_done, n * 2 + (1 if q < 2 else 2))
                            src = PS[:, 3, NTP * q:NTP * q + NTP] if q < 2 else PS[:, 4, 0:NTP]
                            nc.scalar.activation(H2[:, q, :], src, ACT.Relu, bias=MB2[:, q:q + 1]).then_inc(second_relu, 1)

                    first(0)
                    second(0)
                    first(1)
                    with act.Fori(0, B - 2) as i:
                        second(i + 1)
                        first(i + 2)
                    second(B - 1)

                @blk.vector
                def _(vec):
                    def combine(n):
                        vec.wait_ge(third_done, n + 1)
                        after(vec, sum_chain, n)
                        y = PS[:, 5:7, 0:GROUPS * D].rearrange("p j (e f) -> p j e f", f=D)
                        nc.vector.tensor_tensor(WM[:], y, G5[:, bass.ds(n * 2, 2), :].unsqueeze(3).broadcast_to([128, 2, GROUPS, D]), ALU.mult).then_inc(weighted, 1)
                        vec.wait_ge(weighted, n + 1)
                        nc.vector.tensor_reduce(MO[:], WM[:].rearrange("p j e f -> p j f e"), AX.X, ALU.add).then_inc(sum_chain, 1)
                        vec.wait_ge(sum_chain, n + 1)
                        hb = HB[:, bass.ds(n * 2, 2), :]
                        nc.vector.tensor_tensor(hb, hb, MO[:], ALU.add).then_inc(token_ready, 1)

                    combine(0)
                    with vec.Fori(0, B - 1) as i:
                        combine(i + 1)

                @blk.sync
                def _(sp):
                    with sp.Fori(0, B) as i:
                        wait_apart(sp, token_ready, i + 1, sp_passed)
                        for j, lo, hi in ((0, 0, TP), (1, 0, 112), (1, 112, LAST)):
                            dst = bass.AP(tensor=out.tensor, offset=i * (NT * D) + D * (TP * j + lo), ap=[[D, hi - lo], [1, D]])
                            sp.dma_start(dst, HB[lo:hi, bass.ds(i * 2 + j, 1), :].rearrange("p a f -> p (a f)")).then_inc(out_written, 16)
                    sp.wait_ge(out_written, 16 * 3 * B)


def kernel(**inputs):
    import concourse.bacc as bacc
    from concourse.bass_utils import run_bass_kernel_spmd

    def given(name):
        return np.ascontiguousarray(np.asarray(inputs[name]))

    def head_rows(w):
        return w.reshape(D, 2, 8, DH).transpose(0, 1, 3, 2).reshape(D, 2 * 8 * DH)

    def beside(w):
        return w.transpose(1, 0, 2).reshape(D, -1)

    kv = given("L0_attn_Wkv")
    half = kv.shape[1] // 2
    arrays = {"x": given("x")}
    arrays["k64"] = np.ascontiguousarray(np.concatenate([
        head_rows(given("L0_attn_Wq")), head_rows(kv[:, :half]), kv[:, half:], given("L0_attn_Wg"),
        beside(given("L0_ffn_W1")), given("L1_ffn_sW1"), beside(given("L1_ffn_eW1")), given("L1_ffn_gW")], axis=1))
    for to, name in (("wout", "Wout"), ("bout", "bout"), ("bg", "bg"), ("lq1", "lq1"), ("lk1", "lk1"), ("lq2", "lq2"),
                     ("lk2", "lk2"), ("ln_gamma", "ln_gamma"), ("ln_beta", "ln_beta")):
        arrays[to] = given("L0_attn_" + name)
    for name in ("Wr", "br", "b1", "W2", "b2", "gamma", "beta"):
        arrays["f_" + name.lower()] = given("L0_ffn_" + name)
    for name in ("Wk", "bk", "Wq", "bq", "Wv", "bv", "Wr", "br"):
        arrays["a_" + name.lower()] = np.ascontiguousarray(given("L1_attn_" + name).T)
    for name in ("sb1", "sW2", "sb2", "sW3", "sb3", "eb1", "eW2", "eb2", "eW3", "eb3", "gb"):
        arrays["m_" + name.lower()] = given("L1_ffn_" + name)
    arrays.update(shape_constants())

    nc = bacc.Bacc("TRN2", target_bir_lowering=False, num_devices=1)
    names = {name: nc.dram_tensor(name, a.shape, mybir.dt.from_np(a.dtype), kind="ExternalInput").ap() for name, a in arrays.items()}
    out = nc.dram_tensor("out", (B, NT, D), F32, kind="ExternalOutput").ap()
    build_tower(nc, out=out, **names)
    return run_bass_kernel_spmd(nc, [arrays], core_ids=[0]).results[0]["out"]
```

```python
import math
from contextlib import ExitStack

import numpy as np

import concourse.bass as bass
from concourse import mybir

F32 = mybir.dt.float32
BF16 = mybir.dt.bfloat16
ALU = mybir.AluOpType
ACT = mybir.ActivationFunctionType
AX = mybir.AxisListType

B = 16
L = 4096
D = 64
UP = 4
NT = (L - 1) * UP // D
TP = 128
TILES = 2 * B
NTP = 2 * TP
LAST = NT - TP
HOP = D // UP
TAPS = HOP + 3
BINS = D // 2 + 1
EPS = 1e-5
SH = 16
DH = 16
VH = 32
LAMBDA_INIT = 0.8 - 0.6 * math.exp(-0.3)
NE = 8
FH = 128
CAPACITY = float(math.ceil(B * NT * 1.25 / NE))
PAIRS = B // 2
LK = 8
ME = 4
MH = 128
STACK = 6 * DH
EARLIER = 2 * B - 1
NUMBERS = EARLIER + NE * NE
HEADS = NUMBERS + NE
SELECT = HEADS + 128
EARLIER4 = SELECT + TILES
ROUTE_COLUMNS = EARLIER4 + ME * ME
MAXROWS = 3


def after(eng, sem, value):
    if isinstance(value, int) and value <= 0:
        return
    eng.wait_ge(sem, value)


def wait_apart(eng, sem, value, passed):
    if isinstance(value, int):
        after(eng, sem, value)
    else:
        eng.wait_ge(sem, value)
        eng.sem_inc(passed, 1)


class Chain:

    def __init__(self, eng, sem, at=0):
        self.eng, self.sem, self.at = eng, sem, at

    def step(self, instruction):
        instruction.then_inc(self.sem, 1)
        self.at = self.at + 1

    def wait(self):
        self.eng.wait_ge(self.sem, self.at)

    def link(self, instruction):
        self.step(instruction)
        self.wait()


def shape_constants():
    A = -0.75

    def near(t):
        return ((A + 2) * t - (A + 3)) * t * t + 1

    def far(t):
        return ((A * t - 5 * A) * t + 8 * A) * t - 4 * A

    def near_slope(t):
        return (3 * (A + 2) * t - 2 * (A + 3)) * t

    def far_slope(t):
        return (3 * A * t - 10 * A) * t + 8 * A

    taps = np.zeros((2, TAPS, D))
    for p in range(D):
        f = (p % UP) / UP
        for off, value, slope in ((-1, far(1 + f), far_slope(1 + f)), (0, near(f), near_slope(f)),
                                  (1, near(1 - f), -near_slope(1 - f)), (2, far(2 - f), -far_slope(2 - f))):
            taps[0, p // UP + off + 1, p] += value
            taps[1, p // UP + off + 1, p] += slope
    quad = np.zeros((128, 4, 128), np.float32)
    for kind in range(2):
        for tile in range(4):
            u, i = divmod(tile, 2)
            quad[32 * tile:32 * tile + TAPS, 2 * kind + u, 64 * i:64 * i + 64] = taps[kind]
    n = (L - 1) * UP + 1
    steps = np.arange(n - 1, dtype=np.float32) * (np.float32(1) / np.float32(n - 1))
    at = np.concatenate([steps, np.ones(1, np.float32)]) * np.float32(L - 1)
    shift = np.zeros((128, TP), np.float32)
    for i in range(2):
        for t in range(TP if i == 0 else LAST):
            p = D * (TP * i + t) + np.arange(D)
            shift[64 * i:64 * i + 64, t] = at[p].astype(np.float64) - p / UP
    dft = np.zeros((128, 128), np.float32)
    angle = 2 * np.pi * np.outer(np.arange(D), np.arange(BINS)) / D
    one = 0.5 * np.concatenate([np.cos(angle), np.sin(angle[:, 1:BINS - 1])], axis=1)
    dft[:64, :64] = dft[64:, 64:] = one
    average = np.kron(np.eye(128 // VH), np.full((VH, VH), 1.0 / VH)).astype(np.float32)
    route = np.zeros((128, ROUTE_COLUMNS), np.float32)
    route[:, B - 1] = 1.0 / NT
    route[:, EARLIER:EARLIER + NE * NE] = np.tril(np.ones((NE, NE)), -1).ravel()
    route[:, NUMBERS:NUMBERS + NE] = np.arange(NE)
    route[:, HEADS:HEADS + 128] = np.kron(np.eye(128 // LK), np.ones((LK, LK)))
    route[:, SELECT:SELECT + TILES] = np.kron(np.eye(TILES), np.ones((ME, 1)))
    route[:, EARLIER4:EARLIER4 + ME * ME] = np.tril(np.ones((ME, ME)), -1).ravel()
    return {"c_route": route, "c_ident": np.eye(128, dtype=np.float32), "c_taps": quad, "c_shift": shift, "c_dft": dft, "c_average": average}


def build_tower(nc, x, k64, wout, bout, bg, lq1, lk1, lq2, lk2, ln_gamma, ln_beta,
                f_wr, f_br, f_b1, f_w2, f_b2, f_gamma, f_beta,
                a_wk, a_bk, a_wq, a_bq, a_wv, a_bv, a_wr, a_br,
                m_sb1, m_sw2, m_sb2, m_sw3, m_sb3, m_eb1, m_ew2, m_eb2, m_ew3, m_eb3, m_gb,
                c_ident, c_taps, c_shift, c_dft, c_average, c_route, out):
    NQKVG = 4 * 256
    NW1 = NE * FH
    NM1 = D + ME * MH + ME
    NK64 = NQKVG + NW1 + NM1
    KQ = TILES // 4

    with ExitStack() as ctx:
        def sb(name, shape, dt=F32):
            return ctx.enter_context(nc.sbuf_tensor(name, shape, dt))

        signals = []

        def sem(name):
            signals.append(nc.alloc_semaphore(name=name))
            return signals[-1]

        def end_stages():
            nc.clear_and_free_semaphores(signals)
            signals.clear()
            nc.all_engine_barrier()

        PS = ctx.enter_context(nc.psum_tensor("PS", [128, 8, 512], F32))

        def bank_bf16(k):
            return PS[:, k, :].bitcast(BF16)

        H = sb("H", [128, TILES, D])
        XT = sb("XT", [128, 2, B * NTP], BF16)
        SG = sb("SG", [128, 2, B * NTP])
        ident = sb("ident", [128, 128])
        identb = sb("identb", [128, 128], BF16)
        taps = sb("taps", [128, 4, 128])
        shift = sb("shift", [128, TP])
        dft = sb("dft", [128, 128])
        average = sb("average", [128, 128])
        bias = sb("bias", [128, 8])
        WS = sb("WS", [128, 3, NK64], BF16)
        WO = sb("WO", [128, 2, D])
        BO = sb("BO", [128, D])
        BG = sb("BG", [128, 2])
        LV = sb("LV", [128, 4, DH])
        LS = sb("LS", [128, 8])
        GB = sb("GB", [128, 4])
        st = sb("st", [128, 6, TILES])

        scratch = nc.dram_tensor("parts_scratch", (2, 2, 3, 2, DH, 8, NTP), BF16).ap()

        consts_in = sem("consts_in"); ident_in = sem("ident_in"); windows_in = sem("windows_in"); weights_in = sem("weights_in")
        small_in = sem("small_in")
        windows_zeroed = sem("windows_zeroed"); consts_made = sem("consts_made")
        windows_turned = sem("windows_turned"); windows_copied = sem("windows_copied")
        interpolated = sem("interpolated"); points_ready = sem("points_ready")
        terms_ready = sem("terms_ready"); kernels_ready = sem("kernels_ready")
        spectrum_done = sem("spectrum_done"); squares_ready = sem("squares_ready")
        power_ready = sem("power_ready"); magnitude_ready = sem("magnitude_ready")
        excess_ready = sem("excess_ready"); mask_ready = sem("mask_ready")
        gap_ready = sem("gap_ready"); log_ready = sem("log_ready")
        centered = sem("centered"); csq_ready = sem("csq_ready"); var_ready = sem("var_ready")
        rstd_ready = sem("rstd_ready"); normed = sem("normed"); x1_ready = sem("x1_ready")
        rest_ready = sem("rest_ready"); x2_ready = sem("x2_ready"); x_split = sem("x_split")
        x_turned = sem("x_turned"); xt0_copied = sem("xt0_copied"); xt1_copied = sem("xt1_copied")
        weights_split = sem("weights_split"); gates_done = sem("gates_done"); gates_used = sem("gates_used")
        lam_products = sem("lam_products"); lam_exps = sem("lam_exps"); bout_added = sem("bout_added")
        vec_chain = sem("vec_chain"); act_chain = sem("act_chain"); pool_chain = sem("pool_chain")
        q_done = sem("q_done"); k_done = sem("k_done"); v_done = sem("v_done")
        q_left = sem("q_left"); k_left = sem("k_left")
        q_taken = sem("q_taken"); k_taken = sem("k_taken"); q_second = sem("q_second"); k_second = sem("k_second"); v_copied = sem("v_copied")
        q_parts = sem("q_parts"); k_parts = sem("k_parts")
        q_written = sem("q_written"); k_written = sem("k_written")
        stacks_in = [sem("stacks_in_even"), sem("stacks_in_odd")]
        scores_done = sem("scores_done"); maxes_taken = sem("maxes_taken")
        max_parts = sem("max_parts"); max_turned = sem("max_turned"); max_copied = sem("max_copied")
        max_rows_in = sem("max_rows_in")
        scoresT_done = sem("scoresT_done"); exps_ready = sem("exps_ready")
        quad_done = sem("quad_done"); inv_ready = sem("inv_ready"); quad_scaled = sem("quad_scaled")
        heads_out = sem("heads_out"); 
        squares_taken = sem("squares_taken"); var_done = sem("var_done"); hrstd_ready = sem("hrstd_ready")
        head_normed = sem("head_normed"); gated = sem("gated"); wout_done = sem("wout_done")
        h_updated = sem("h_updated"); act_chain2 = sem("act_chain2"); act_logs = sem("act_logs")
        max_chain = sem("max_chain"); ones_made = sem("ones_made")

        one = ExitStack()
        with one:
            def sa(name, shape, dt=F32):
                return one.enter_context(nc.sbuf_tensor(name, shape, dt))
            W = sa("W", [128, TILES, 32])
            SW = sa("SW", [128, KQ, TP])
            TX = sa("TX", [128, 2, KQ, TP])
            TP2 = sa("TP2", [128, 2, KQ, TP])
            TG = sa("TG", [128, 2, KQ, TP])
            SQ = sa("SQ", [128, TILES, D])
            MG = sa("MG", [128, TILES, BINS])
            MZ = sa("MZ", [128, TILES, BINS])
            ML = sa("ML", [128, TILES, BINS])
            XC = sa("XC", [128, TILES, D])
            XS = sa("XS", [128, TILES, 3 * D], BF16)
            WF = sa("WF", [128, NK64])
            WR = sa("WR", [128, NK64])
            WM8 = sa("WM8", [128, 8])
            values_centered = sem("values_centered"); weights_first = sem("weights_first")

            block = one.enter_context(nc.Block("front"))

            @block.sync
            def _(sp):
                sp.wait_ge(windows_zeroed, 1)
                def src(offset, n, width):
                    return bass.AP(tensor=x.tensor, offset=offset, ap=[[HOP, n], [L, B], [1, width]])
                tiles = W[:].rearrange("p (b j) s -> p j b s", j=2)
                for lo, hi in ((0, 112), (112, LAST)):
                    sp.dma_start(tiles[1 + lo:1 + hi, 0, :, 0:TAPS], src(HOP * (1 + lo) - 1, hi - lo, TAPS)).then_inc(windows_in, 16)
                    sp.dma_start(tiles[lo:hi, 1, :, 0:TAPS], src(HOP * (TP + lo) - 1, hi - lo, TAPS)).then_inc(windows_in, 16)
                sp.dma_start(tiles[0:1, 0, :, 1:TAPS], src(0, 1, TAPS - 1)).then_inc(windows_in, 16)
                sp.dma_start(tiles[0:1, 0, :, 0:1], src(0, 1, 1), allow_slow_non_contiguous=True).then_inc(windows_in, 16)
                for half in (0, 64):
                    sp.dma_start(WF[half:half + 64, :], k64).then_inc(weights_in, 16)
                sp.dma_start(WO[:], wout.rearrange("(g p) n -> p g n", g=2)).then_inc(small_in, 16)
                sp.dma_start(BO[:], bass.AP(tensor=bout.tensor, offset=0, ap=[[0, 128], [1, D]])).then_inc(small_in, 16)
                for n, v in enumerate((lq1, lk1, lq2, lk2)):
                    sp.dma_start(LV[:, n, :], bass.AP(tensor=v.tensor, offset=0, ap=[[0, 128], [1, DH]])).then_inc(small_in, 16)

            @block.scalar
            def _(act):
                nc.scalar.preload_act_table_set("natural_log_exp_and_others")
                act.dma_start(ident[:], c_ident).then_inc(ident_in, 16)
                act.dma_start(taps[:], c_taps).then_inc(consts_in, 16)
                act.dma_start(shift[:], c_shift).then_inc(consts_in, 16)
                act.dma_start(dft[:], c_dft).then_inc(consts_in, 16)
                act.dma_start(average[:], c_average).then_inc(consts_in, 16)
                act.dma_start(BG[:], bg.rearrange("(g p) -> p g", g=2), allow_slow_non_contiguous=True).then_inc(small_in, 16)
                for n, v in enumerate((ln_gamma, ln_beta)):
                    act.dma_start(GB[:, n:n + 1], bass.AP(tensor=v.tensor, offset=0, ap=[[0, 4], [1, VH], [1, 1]]), allow_slow_non_contiguous=True).then_inc(small_in, 16)
                chain = Chain(act, act_chain)
                for k in range(2):
                    act.wait_ge(windows_turned, k + 1)
                    nc.scalar.copy(SW[:, 4 * k:4 * k + 4, :], PS[:, k, :].rearrange("p (q t) -> p q t", q=4)).then_inc(windows_copied, 1)
                act.wait_ge(values_centered, 1)
                nc.scalar.copy(WS[:, 0, :], WF[:]).then_inc(weights_first, 1)
                act.wait_ge(consts_made, 1)
                for s, (n, u) in enumerate(((0, 0), (0, 1), (1, 0), (1, 1))):
                    act.wait_ge(points_ready, s + 1)
                    part = (slice(None), u, slice(4 * n, 4 * n + 4), slice(None))
                    chain.step(nc.scalar.activation(TG[part], TX[part], ACT.Square, bias=bias[:, 0:1]))
                    chain.step(nc.scalar.activation(TP2[part], TX[part], ACT.Square, bias=bias[:, 1:2]))
                    chain.wait()
                    nc.scalar.activation(TG[part], TG[part], ACT.Exp, scale=-0.5).then_inc(terms_ready, 1)
                for k in range(4):
                    act.wait_ge(spectrum_done, k + 1)
                    nc.scalar.activation(SQ[:, 8 * k:8 * k + 8, :], PS[:, 2 + k, :].rearrange("p (t f) -> p t f", t=8), ACT.Square).then_inc(squares_ready, 1)
                halves = [slice(0, B), slice(B, TILES)]
                for n in range(2):
                    act.wait_ge(power_ready, n + 1)
                    nc.scalar.activation(MG[:, halves[n], :], SQ[:, halves[n], 0:BINS], ACT.Sqrt).then_inc(magnitude_ready, 1)
                for n in range(2):
                    act.wait_ge(excess_ready, n + 1)
                    nc.scalar.activation(MZ[:, halves[n], :], MZ[:, halves[n], :], ACT.Sigmoid).then_inc(mask_ready, 1)
                nc.scalar.preload_act_table_set("natural_log_exp_and_others")
                for n in range(2):
                    part = (slice(None), halves[n], slice(None))
                    act.wait_ge(gap_ready, n + 1)
                    chain.link(nc.scalar.activation(ML[part], ML[part], ACT.Abs))
                    chain.link(nc.scalar.activation(ML[part], ML[part], ACT.Exp, scale=-1.0))
                    nc.scalar.activation(ML[part], ML[part], ACT.Ln, bias=bias[:, 3:4]).then_inc(log_ready, 1)
                act.wait_ge(lam_products, 2)
                nc.scalar.activation(LS[:, 2:4], LS[:, 0:2], ACT.Exp).then_inc(lam_exps, 1)
                for n in range(2):
                    part = (slice(None), halves[n], slice(None))
                    act.wait_ge(centered, n + 1)
                    nc.scalar.activation(SQ[part], XC[part], ACT.Square).then_inc(csq_ready, 1)
                for n in range(2):
                    act.wait_ge(var_ready, n + 1)
                    chain.link(nc.scalar.activation(st[:, 2, halves[n]], st[:, 1, halves[n]], ACT.Ln, scale=1.0 / D, bias=bias[:, 2:3]))
                    nc.scalar.activation(st[:, 3, halves[n]], st[:, 2, halves[n]], ACT.Exp, scale=-0.5).then_inc(rstd_ready, 1)
                for n in range(2):
                    act.wait_ge(normed, n + 1)
                    nc.scalar.copy(XS[:, halves[n], D:2 * D], XC[:, halves[n], :]).then_inc(x1_ready, 1)
                for n in range(2):
                    act.wait_ge(rest_ready, n + 1)
                    nc.scalar.copy(XS[:, halves[n], 0:D], XC[:, halves[n], :]).then_inc(x2_ready, 1)
                for k in range(4):
                    act.wait_ge(x_turned, k + 1)
                    nc.scalar.copy(XT[:, 0, 1024 * k:1024 * k + 1024], bank_bf16(k)).then_inc(xt0_copied, 1)

            @block.gpsimd
            def _(pool):
                nc.gpsimd.memset(W[:], 0.0).then_inc(windows_zeroed, 1)
                for n, value in enumerate((-0.7, 1.3, EPS, 1.0)):
                    m = nc.gpsimd.memset(bias[:, n:n + 1], value)
                m.then_inc(consts_made, 1)
                pool.wait_ge(ident_in, 16)
                nc.gpsimd.tensor_copy(identb[:], ident[:]).then_inc(consts_made, 1)
                chain = Chain(pool, pool_chain)
                pool.wait_ge(weights_first, 1)
                chain.link(nc.gpsimd.tensor_tensor(WR[:], WF[:], WS[:, 0, :], ALU.subtract))
                chain.link(nc.gpsimd.tensor_copy(WS[:, 1, :], WR[:]))
                nc.gpsimd.tensor_tensor(WS[0:64, 2, :], WR[0:64, :], WS[0:64, 1, :], ALU.subtract).then_inc(weights_split, 1)
                pool.wait_ge(weights_split, 1)
                nc.gpsimd.tensor_copy(WS[64:128, 2, :], WS[64:128, 0, :]).then_inc(weights_split, 1)
                pool.wait_ge(weights_split, 2)
                pool.wait_ge(small_in, 16 * 9)
                pool.wait_ge(centered, 2)
                chain.step(nc.gpsimd.tensor_scalar(GB[:, 2:4], GB[:, 0:2], 1.0 - LAMBDA_INIT, None, ALU.mult))
                nc.gpsimd.tensor_tensor(H[:], H[:], BO[:].unsqueeze(1).broadcast_to([128, TILES, D]), ALU.add).then_inc(bout_added, 1)

            @block.tensor
            def _(pe):
                pe.wait_ge(ident_in, 16); pe.wait_ge(consts_in, 64)
                pe.wait_ge(windows_in, 16 * 6)
                for q in range(KQ):
                    t = nc.tensor.transpose(PS[:, q // 4, 128 * (q % 4):128 * (q % 4) + 128], W[:, 4 * q:4 * q + 4, :], ident[:])
                    if q % 4 == 3:
                        t.then_inc(windows_turned, 1)
                for n in range(2):
                    pe.wait_ge(windows_copied, 2 if n else 1)
                    for u in range(2):
                        value, slope = ((2 + u, 4 + u), (6 + u, u))[n]
                        rhs = SW[:, 4 * n:4 * n + 4, :]
                        nc.tensor.matmul(PS[:, value, :], taps[:, u, :], rhs, start=True, stop=True)
                        nc.tensor.matmul(PS[:, slope, :], taps[:, 2 + u, :], rhs, start=True, stop=True).then_inc(interpolated, 1)
                for q in range(KQ):
                    for u in range(2):
                        pe.wait_ge(kernels_ready, 2 * (q // 4) + u + 1)
                        t = nc.tensor.matmul(PS[:, 2 + q // 2, 128 * (2 * (q % 2) + u):128 * (2 * (q % 2) + u) + 128],
                                             TX[:, u, q, :], dft[:], start=True, stop=True)
                    if q % 2:
                        t.then_inc(spectrum_done, 1)
                pe.wait_ge(consts_made, 2)
                for kind in range(2):
                    for k in range(4):
                        if k % 2 == 0:
                            pe.wait_ge((x2_ready, x_split)[kind], k // 2 + 1)
                        for t in range(8):
                            m = nc.tensor.transpose(bank_bf16(4 * kind + k)[:, 128 * t:128 * t + 128],
                                                    XS[:, 8 * k + t, D * kind:D * kind + 128], identb[:])
                        m.then_inc(x_turned, 1)

            @block.vector
            def _(vec):
                chain = Chain(vec, vec_chain)
                vec.wait_ge(weights_in, 32)
                heads = WF[:, 2 * 256:3 * 256].rearrange("p (h v) -> p h v", v=VH)
                chain.link(nc.vector.tensor_reduce(WM8[:], heads, AX.X, ALU.add))
                nc.vector.scalar_tensor_tensor(out=heads, in0=WM8[:].unsqueeze(2).broadcast_to([128, 8, VH]), scalar=-1.0 / VH,
                                               in1=heads, op0=ALU.mult, op1=ALU.add).then_inc(values_centered, 1)
                vec.wait_ge(consts_in, 64)
                sh = shift[:].unsqueeze(1).broadcast_to([128, 4, TP])
                for s, (n, u) in enumerate(((0, 0), (0, 1), (1, 0), (1, 1))):
                    value, slope = ((2 + u, 4 + u), (6 + u, u))[n]
                    part = (slice(None), u, slice(4 * n, 4 * n + 4), slice(None))
                    vec.wait_ge(interpolated, s + 1)
                    chain.link(nc.vector.tensor_tensor(TP2[part], PS[:, slope, :].rearrange("p (q t) -> p q t", q=4), sh, ALU.mult))
                    nc.vector.tensor_tensor(TX[part], PS[:, value, :].rearrange("p (q t) -> p q t", q=4), TP2[part], ALU.add).then_inc(points_ready, 1)
                for s, (n, u) in enumerate(((0, 0), (0, 1), (1, 0), (1, 1))):
                    part = (slice(None), u, slice(4 * n, 4 * n + 4), slice(None))
                    vec.wait_ge(terms_ready, s + 1)
                    nc.vector.tensor_tensor(TX[part], TP2[part], TG[part], ALU.add).then_inc(kernels_ready, 1)
                vec.wait_ge(small_in, 16 * 9)
                for n in range(2):
                    chain.link(nc.vector.tensor_tensor(LV[:, 2 * n, :], LV[:, 2 * n, :], LV[:, 2 * n + 1, :], ALU.mult))
                    nc.vector.tensor_reduce(LS[:, n:n + 1], LV[:, 2 * n, :], AX.X, ALU.add).then_inc(lam_products, 1)
                halves = [slice(0, B), slice(B, TILES)]
                for n in range(2):
                    vec.wait_ge(squares_ready, 2 * n + 2)
                    nc.vector.tensor_tensor(SQ[:, halves[n], 1:BINS - 1], SQ[:, halves[n], 1:BINS - 1], SQ[:, halves[n], BINS:D], ALU.add).then_inc(power_ready, 1)

                def peak(n):
                    return st[:, 0, halves[n]].unsqueeze(2).broadcast_to([128, B, BINS])

                for n in range(2):
                    vec.wait_ge(magnitude_ready, n + 1)
                    chain.link(nc.vector.tensor_reduce(st[:, 0, halves[n]], MG[:, halves[n], :], AX.X, ALU.max))
                    nc.vector.scalar_tensor_tensor(out=MZ[:, halves[n], :], in0=peak(n), scalar=-0.12, in1=MG[:, halves[n], :], op0=ALU.mult, op1=ALU.add).then_inc(excess_ready, 1)
                for n in range(2):
                    part = (slice(None), halves[n], slice(None))
                    vec.wait_ge(mask_ready, n + 1)
                    chain.link(nc.vector.tensor_tensor(MG[part], MG[part], MZ[part], ALU.mult))
                    nc.vector.scalar_tensor_tensor(out=ML[part], in0=peak(n), scalar=-0.9, in1=MG[part], op0=ALU.mult, op1=ALU.add).then_inc(gap_ready, 1)
                    chain.step(nc.vector.scalar_tensor_tensor(out=MZ[part], in0=peak(n), scalar=0.9, in1=MG[part], op0=ALU.mult, op1=ALU.min))
                chain.wait()
                for n in range(2):
                    vec.wait_ge(log_ready, n + 1)
                    chain.step(nc.vector.tensor_tensor(H[:, halves[n], 0:BINS], MZ[:, halves[n], :], ML[:, halves[n], :], ALU.subtract))
                    chain.link(nc.vector.tensor_tensor(H[:, halves[n], BINS:D], MZ[:, halves[n], BINS - 2:0:-1], ML[:, halves[n], BINS - 2:0:-1], ALU.subtract))
                    chain.link(nc.vector.tensor_reduce(st[:, 0, halves[n]], H[:, halves[n], :], AX.X, ALU.add))
                    nc.vector.scalar_tensor_tensor(out=XC[:, halves[n], :], in0=st[:, 0, halves[n]].unsqueeze(2).broadcast_to([128, B, D]), scalar=-1.0 / D,
                                                   in1=H[:, halves[n], :], op0=ALU.mult, op1=ALU.add).then_inc(centered, 1)
                for n in range(2):
                    vec.wait_ge(csq_ready, n + 1)
                    nc.vector.tensor_reduce(st[:, 1, halves[n]], SQ[:, halves[n], :], AX.X, ALU.add).then_inc(var_ready, 1)
                for n in range(2):
                    vec.wait_ge(rstd_ready, n + 1)
                    nc.vector.tensor_tensor(XC[:, halves[n], :], XC[:, halves[n], :], st[:, 3, halves[n]].unsqueeze(2).broadcast_to([128, B, D]), ALU.mult).then_inc(normed, 1)
                for n in range(2):
                    part = (slice(None), halves[n], slice(None))
                    vec.wait_ge(x1_ready, n + 1)
                    nc.vector.tensor_tensor(XC[part], XC[part], XS[:, halves[n], D:2 * D], ALU.subtract).then_inc(rest_ready, 1)
                for n in range(2):
                    part = (slice(None), halves[n], slice(None))
                    vec.wait_ge(x2_ready, n + 1)
                    nc.vector.tensor_tensor(XS[:, halves[n], 2 * D:3 * D], XC[part], XS[:, halves[n], 0:D], ALU.subtract).then_inc(x_split, 1)
                vec.wait_ge(lam_exps, 1)
                chain.link(nc.vector.tensor_tensor(LS[:, 4:5], LS[:, 3:4], LS[:, 2:3], ALU.subtract))
                chain.link(nc.vector.tensor_scalar(LS[:, 5:6], LS[:, 4:5], -LAMBDA_INIT, None, ALU.add))
                for k in range(4):
                    vec.wait_ge(x_turned, 4 + k + 1)
                    nc.vector.tensor_copy(XT[:, 1, 1024 * k:1024 * k + 1024], bank_bf16(4 + k)).then_inc(xt1_copied, 1)


        with ExitStack() as two:
            def sa(name, shape, dt=F32):
                return two.enter_context(nc.sbuf_tensor(name, shape, dt))
            QP = [sa(f"QP{p}", [128, 2, 3, 2, NTP], BF16) for p in range(2)]
            QR = sa("QR", [128, 2, 2, NTP])
            QS = [sa(f"QS{p}", [STACK + MAXROWS, SH, NTP], BF16) for p in range(2)]
            KS = [sa(f"KS{p}", [STACK + MAXROWS, SH, NTP], BF16) for p in range(2)]
            NM = sa("NM", [128, SH, 2])
            NP = sa("NP", [128, 2, 3, SH], BF16)
            NR = sa("NR", [128, 2, SH])
            MT = sa("MT", [3 * SH, 2, TP], BF16)
            EX = [sa(f"EX{p}", [128, 4, 2, NTP]) for p in range(2)]
            V = [sa(f"V{p}", [128, 2, 8 * VH]) for p in range(2)]
            ones = sa("ones", [128, VH])
            IN = [sa(f"IN{p}", [128, NTP]) for p in range(2)]
            AH = sa("AH", [128, 4, NTP])
            O = sa("O", [128, 2, NTP])
            OQ = sa("OQ", [128, 2, NTP])
            RS = sa("RS", [128, 2, NTP])
            Y = sa("Y", [128, 2, NTP])
            U = sa("U", [128, 2, NTP])

            pe_passed = sem("pe_passed"); pool_passed = sem("pool_passed"); sp_passed = sem("sp_passed")
            stack_in = [[sem(f"stack_in_{p}{h}") for h in range(2)] for p in range(2)]
            ORDER = [2 * (4 * g + j) + odd for g in range(2) for odd in range(2) for j in range(4)]

            TWICE = (0, 1, 3, 5, 8, 9)
            NEXT_SLOTS = SH - len(TWICE)
            SLOT = {"queries": 0, "keys": 1, "values": 6, "variances": 10, "turn maxima": 11,
                    "output": 15, "inverse 2": 0, "queries copied": 1, "keys copied": 1, "inverse 3": 3,
                    "values copied": 6, "squares": 7, "inverse 0": 7, "rstd": 10, "maxima copied": 11,
                    "inverse 1": 11, "scale 2": 2, "queries second": 3, "keys second": 3, "scale 3": 6,
                    "scale 0": 8, "head norm": 10, "scale 1": 14, "residual": 15}

            def coming(s):
                first = s + sum(s > t for t in TWICE)
                return range(first, first + (2 if s in TWICE else 1)) if s < NEXT_SLOTS else ()

            class Signal:

                def __init__(self, i, c):
                    self.n = i * 2 + c if not isinstance(i, int) or i else c
                    self.p = c % 2
                    self.pair = i + c // 2 if not isinstance(i, int) or i or c >= 2 else 0
                    self.i, self.c = i, c

                def next(self, k):
                    return Signal(self.i, self.c + k)

            GATES, GATE_BANKS, GATES_AHEAD = 2 * B * NTP // 512, 4, 8

            def gate_place(n):
                return n % 2, slice(512 * (n // 2), 512 * (n // 2) + 512), PS[:, 2 + n % GATE_BANKS, :]

            def upto(value, most=B):
                return min(value, most) if isinstance(value, int) else value

            def schedule(eng, prologue, step, epilogue):
                prologue()
                step(Signal(0, 0), True, True, False)
                step(Signal(0, 1), True, True, True)
                with eng.Fori(0, B // 2 - 2) as i:
                    step(Signal(i, 2), True, True, True)
                    step(Signal(i, 3), True, True, True)
                step(Signal(0, B - 2), False, True, True)
                step(Signal(0, B - 1), False, False, True)
                epilogue()

            def left(eng, ops, t, which, taken, ready):
                eng.wait_ge(taken, t.n + 1)
                ops.tensor_tensor(QR[:, which], QR[:, which], QP[t.p][:, which, 0], ALU.subtract).then_inc(ready, 1)

            def third(eng, ops, t, which, second, ready):
                eng.wait_ge(second, t.n + 1)
                ops.tensor_tensor(QP[t.p][:, which, 2], QR[:, which], QP[t.p][:, which, 1], ALU.subtract).then_inc(ready, 1)

            def split(eng, ops, t):
                left(eng, ops, t, 0, q_taken, q_left)
                left(eng, ops, t, 1, k_taken, k_left)
                third(eng, ops, t, 0, q_second, q_parts)
                third(eng, ops, t, 1, k_second, k_parts)

            block = two.enter_context(nc.Block("attention"))

            @block.sync
            def _(sp):
                part = 2 * DH * 8 * NTP
                rows = 8 * NTP

                def park(t):
                    q_sc, k_sc = scratch[t.p, 0], scratch[t.p, 1]
                    for h in range(2):
                        wait_apart(sp, stack_in[t.p][h], t.pair * 96, sp_passed)
                    sp.wait_ge(q_parts, t.n + 1)
                    sp.dma_start(q_sc.rearrange("s g d h t -> (d h) (s g) t"), QP[t.p][:, 0].rearrange("p s g t -> p (s g) t")).then_inc(q_written, 16)
                    sp.wait_ge(k_parts, t.n + 1)
                    sp.dma_start(k_sc.rearrange("s g d h t -> (d h) (s g) t"), QP[t.p][:, 1].rearrange("p s g t -> p (s g) t")).then_inc(k_written, 16)

                def stack(t, g):
                    wait_apart(sp, q_written, (t.n + 1) * 16, sp_passed)
                    wait_apart(sp, k_written, (t.n + 1) * 16, sp_passed)
                    wait_apart(sp, scoresT_done, (t.n - 2) * 16 + 8 * (g + 1), sp_passed)
                    heads = slice(8 * g, 8 * g + 8)
                    q0, k0 = scratch[t.p, 0, 0, g].offset, scratch[t.p, 1, 0, g].offset
                    for dst, base, first, reps, pstep, at in ((QS, q0, 0, 3, 0, 0), (QS, q0, 1, 2, 0, 3), (QS, q0, 2, 1, 0, 5),
                                                              (KS, k0, 0, 3, part, 0), (KS, k0, 0, 2, part, 3), (KS, k0, 0, 1, part, 5)):
                        src = bass.AP(tensor=scratch.tensor, offset=base + first * part, ap=[[pstep, reps], [rows, DH], [1, rows]])
                        sp.dma_start(dst[t.p][DH * at:DH * (at + reps), heads, :], src).then_inc(stack_in[t.p][g], 16)

                def max_rows(t):
                    sp.wait_ge(max_copied, t.n + 1)
                    for s in range(3):
                        sp.dma_start(QS[t.p][STACK + s:STACK + s + 1, :, :], MT[SH * s:SH * s + SH, :, :].rearrange("h j t -> h (j t)")).then_inc(max_rows_in, 16)

                def prologue():
                    for c in range(2):
                        park(Signal(0, c))
                        for g in range(2):
                            stack(Signal(0, c), g)
                    max_rows(Signal(0, 0))

                def step(b, front, nxt, tail):
                    if front:
                        park(b.next(2))
                        stack(b.next(2), 0)
                    if nxt:
                        max_rows(b.next(1))
                    if front:
                        stack(b.next(2), 1)

                schedule(sp, prologue, step, lambda: None)

            @block.tensor
            def _(pe):
                def project_q(t):
                    after(pe, max_copied, t.n - 1)
                    after(pe, q_taken, t.n)
                    for m in range(2):
                        for s in range(3):
                            mm = nc.tensor.matmul(PS[:, 7, NTP * m:NTP * m + NTP], WS[:, s, 128 * m:128 * m + 128],
                                                  XT[:, s // 2, bass.ds(t.n * NTP, NTP)], start=(s == 0), stop=(s == 2))
                    mm.then_inc(q_done, 1)

                def project_k(t):
                    after(pe, h_updated, t.n - 3)
                    after(pe, k_taken, t.n)
                    for m in range(2):
                        for s in range(3):
                            mm = nc.tensor.matmul(PS[:, 6, NTP * m:NTP * m + NTP], WS[:, s, 256 + 128 * m:384 + 128 * m],
                                                  XT[:, s // 2, bass.ds(t.n * NTP, NTP)], start=(s == 0), stop=(s == 2))
                    mm.then_inc(k_done, 1)

                def project_v(t):
                    pe.wait_ge(q_taken, upto(t.n + 2))
                    after(pe, max_copied, t.n)
                    for j in range(2):
                        for s in range(3):
                            mm = nc.tensor.matmul(PS[:, 7, 256 * j:256 * j + 256], XT[:, s // 2, bass.ds(t.n * NTP + TP * j, TP)],
                                                  WS[:, s, 512:768], start=(s == 0), stop=(s == 2))
                    mm.then_inc(v_done, 1)

                def turn_maxes(t):
                    pe.wait_ge(v_copied, t.n + 1)
                    wait_apart(pe, max_parts, t.n + 1, pe_passed)
                    for j in range(2):
                        tr = nc.tensor.transpose(bank_bf16(7)[0:3 * SH, TP * j:TP * j + TP], NP[:, j].rearrange("p s h -> p (s h)"), identb[:])
                    tr.then_inc(max_turned, 1)

                def head_variance(t):
                    pe.wait_ge(k_taken, upto(t.n + 4))
                    after(pe, h_updated, t.n)
                    pe.wait_ge(squares_taken, t.n + 1)
                    for g in range(2):
                        mm = nc.tensor.matmul(PS[:, 6, NTP * g:NTP * g + NTP], average[:], OQ[:, g, :], start=True, stop=True)
                    mm.then_inc(var_done, 1)

                def project_out(t):
                    pe.wait_ge(hrstd_ready, t.n + 1)
                    pe.wait_ge(gated, t.n + 1)
                    for j in range(2):
                        for g in range(2):
                            mm = nc.tensor.matmul(PS[:, 6, D * j:D * j + D], U[:, g, TP * j:TP * j + TP], WO[:, g, :], start=(g == 0), stop=(g == 1))
                    mm.then_inc(wout_done, 1)

                def scores(t, s):
                    if s % 8 == 0:
                        pe.wait_ge(stack_in[t.p][s // 8], t.pair * 96 + 96)
                    after(pe, maxes_taken, t.n * 16 + (s - 1))
                    for j in range(2):
                        mm = nc.tensor.matmul(PS[:, s % 2, NTP * j:NTP * j + NT], QS[t.p][0:STACK, s, TP * j:TP * j + TP], KS[t.p][0:STACK, s, 0:NT], start=True, stop=True)
                    mm.then_inc(scores_done, 1)

                def scores_turned(t, s):
                    if s == 0:
                        pe.wait_ge(max_rows_in, t.n * 48 + 48)
                    after(pe, exps_ready, t.n * 16 + (s - 1))
                    for j in range(2):
                        mm = nc.tensor.matmul(PS[:, 2 + s % 2, NTP * j:NTP * j + NTP], KS[t.p][:, ORDER[s], TP * j:TP * j + TP], QS[t.p][:, ORDER[s], :], start=True, stop=True)
                    mm.then_inc(scoresT_done, 1)

                def values(t, q, piece):
                    half, j = divmod(piece, 2)
                    if piece == 0:
                        pe.wait_ge(exps_ready, t.n * 16 + (4 * q + 4))
                        if q == 0:
                            pe.wait_ge(v_copied, t.n + 1)
                        after(pe, quad_scaled, t.n * 4 + (q - 1))
                    rows = TP if j == 0 else LAST
                    for c in range(4):
                        head = 4 * (q // 2) + c
                        w = V[t.p][0:rows, j, VH * head:VH * head + VH] if half == 0 else ones[0:rows, :]
                        mm = nc.tensor.matmul(PS[32 * c:32 * c + 32, 4 + q % 2, NTP * half:NTP * half + NTP], w, EX[q % 2][0:rows, c, j, :], start=(j == 0), stop=(j == 1))
                    if piece == 3:
                        mm.then_inc(quad_done, 1)

                def prologue():
                    for c in range(2):
                        project_q(Signal(0, c))
                        project_k(Signal(0, c))
                    for n in range(GATES):
                        if n >= GATES_AHEAD:
                            for s in range(2 * (n - GATES_AHEAD), 2 * (n - GATES_AHEAD) + 2):
                                scores(Signal(0, 0), s)
                        after(pe, gates_used, n + 1 - GATE_BANKS)
                        half, part, bank = gate_place(n)
                        for s in range(3):
                            mm = nc.tensor.matmul(bank, WS[:, s, 768 + 128 * half:896 + 128 * half], XT[:, s // 2, part], start=(s == 0), stop=(s == 2))
                        mm.then_inc(gates_done, 1)
                    project_v(Signal(0, 0))
                    pe.wait_ge(gates_used, GATES)
                    pe.wait_ge(ones_made, 3)
                    turn_maxes(Signal(0, 0))

                def step(b, front, nxt, tail):
                    for s in range(SH):
                        scores_turned(b, s)
                        if nxt:
                            for head in coming(s)[0:1]:
                                scores(b.next(1), head)
                        if s == SLOT["queries"] and front:
                            project_q(b.next(2))
                        if s == SLOT["keys"] and front:
                            project_k(b.next(2))
                        if s == SLOT["values"] and nxt:
                            project_v(b.next(1))
                        if s == SLOT["variances"] and tail:
                            head_variance(b.next(-1))
                        if s == SLOT["turn maxima"] and nxt:
                            turn_maxes(b.next(1))
                        if s == SLOT["output"] and tail:
                            project_out(b.next(-1))
                        if s >= 4:
                            values(b, s // 4 - 1, s % 4)
                        elif tail:
                            values(b.next(-1), 3, s)
                        if nxt:
                            for head in coming(s)[1:]:
                                scores(b.next(1), head)

                def epilogue():
                    last = Signal(0, B - 1)
                    for piece in range(4):
                        values(last, 3, piece)
                    head_variance(last)
                    project_out(last)

                schedule(pe, prologue, step, epilogue)

            @block.scalar
            def _(act):
                chain = Chain(act, act_chain2)

                def take(t, which, bank, done, written, parts, taken):
                    scale = (DH ** -0.5, 1.0)[which]
                    act.wait_ge(done, t.n + 1)
                    after(act, written, (t.n - 1) * 16)
                    nc.scalar.activation(QP[t.p][:, which, 0].rearrange("p g t -> p (g t)"), PS[:, bank, :], ACT.Copy, scale=scale)
                    after(act, parts, t.n)
                    nc.scalar.activation(QR[:, which].rearrange("p g t -> p (g t)"), PS[:, bank, :], ACT.Copy, scale=scale).then_inc(taken, 1)

                def q_take(t):
                    take(t, 0, 7, q_done, q_written, q_parts, q_taken)

                def k_take(t):
                    take(t, 1, 6, k_done, k_written, k_parts, k_taken)

                def second(t, which, left, ready):
                    act.wait_ge(left, t.n + 1)
                    nc.scalar.activation(QP[t.p][:, which, 1], QR[:, which], ACT.Copy).then_inc(ready, 1)

                def v_copy(t):
                    act.wait_ge(v_done, t.n + 1)
                    after(act, quad_done, t.n * 4 - 4)
                    nc.scalar.activation(V[t.p][:].rearrange("p j f -> p (j f)"), PS[:, 7, :], ACT.Copy).then_inc(v_copied, 1)

                def max_copy(t):
                    act.wait_ge(max_turned, t.n + 1)
                    after(act, max_rows_in, t.n * 48)
                    nc.scalar.activation(MT[:].rearrange("h j t -> h (j t)"), bank_bf16(7)[0:3 * SH, 0:NTP], ACT.Copy).then_inc(max_copied, 1)

                def head_squares(t):
                    act.wait_ge(heads_out, t.n * 2 + 2)
                    after(act, var_done, t.n)
                    nc.scalar.activation(OQ[:], O[:], ACT.Square).then_inc(squares_taken, 1)

                def head_rstd(t):
                    act.wait_ge(var_done, t.n + 1)
                    after(act, head_normed, t.n)
                    chain.at = t.n
                    chain.link(nc.scalar.activation(RS[:].rearrange("p g t -> p (g t)"), PS[:, 6, :], ACT.Ln, bias=bias[:, 2:3]))
                    nc.scalar.activation(RS[:], RS[:], ACT.Exp, scale=-0.5).then_inc(hrstd_ready, 1)

                def exps(t, s):
                    act.wait_ge(scoresT_done, t.n * 16 + (s + 1))
                    if s % 4 == 0:
                        after(act, quad_done, t.n * 4 + (s // 4 - 1))
                    nc.scalar.activation(EX[s // 4 % 2][:, s % 4].rearrange("p j t -> p (j t)"), PS[:, 2 + s % 2, :], ACT.Exp).then_inc(exps_ready, 1)

                def inverse(t, q):
                    act.wait_ge(quad_done, t.n * 4 + (q + 1))
                    after(act, quad_scaled, t.n * 4 + (q - 1))
                    chain2.at = t.n * 4 + q
                    chain2.link(nc.scalar.activation(IN[q % 2][:], PS[:, 4 + q % 2, NTP:2 * NTP], ACT.Ln))
                    nc.scalar.activation(IN[q % 2][:], IN[q % 2][:], ACT.Exp, scale=-1.0).then_inc(inv_ready, 1)

                chain2 = Chain(act, act_logs)

                def prologue():
                    for c in range(2):
                        q_take(Signal(0, c))
                        k_take(Signal(0, c))
                        second(Signal(0, c), 0, q_left, q_second)
                        second(Signal(0, c), 1, k_left, k_second)
                    for n in range(GATES):
                        half, part, bank = gate_place(n)
                        act.wait_ge(gates_done, n + 1)
                        nc.scalar.activation(SG[:, half, part], bank, ACT.Sigmoid, bias=BG[:, half:half + 1]).then_inc(gates_used, 1)
                    nc.scalar.preload_act_table_set("natural_log_exp_and_others")
                    v_copy(Signal(0, 0))
                    max_copy(Signal(0, 0))

                def step(b, front, nxt, tail):
                    for s in range(SH):
                        exps(b, s)
                        if s == SLOT["inverse 2"] and tail:
                            inverse(b.next(-1), 2)
                        if s == SLOT["queries copied"] and front:
                            q_take(b.next(2))
                        if s == SLOT["keys copied"] and front:
                            k_take(b.next(2))
                        if s == SLOT["queries second"] and front:
                            second(b.next(2), 0, q_left, q_second)
                        if s == SLOT["keys second"] and front:
                            second(b.next(2), 1, k_left, k_second)
                        if s == SLOT["inverse 3"] and tail:
                            inverse(b.next(-1), 3)
                        if s == SLOT["values copied"] and nxt:
                            v_copy(b.next(1))
                        if s == SLOT["inverse 0"]:
                            inverse(b, 0)
                        if s == SLOT["squares"] and tail:
                            head_squares(b.next(-1))
                        if s == SLOT["rstd"] and tail:
                            head_rstd(b.next(-1))
                        if s == SLOT["maxima copied"] and nxt:
                            max_copy(b.next(1))
                        if s == SLOT["inverse 1"]:
                            inverse(b, 1)

                def epilogue():
                    last = Signal(0, B - 1)
                    inverse(last, 2)
                    inverse(last, 3)
                    head_squares(last)
                    head_rstd(last)

                schedule(act, prologue, step, epilogue)

            @block.vector
            def _(vec):
                chain = Chain(vec, max_chain)

                def flat(a):
                    return a[:].rearrange("p g t -> p (g t)")

                def head_norm(t):
                    vec.wait_ge(heads_out, t.n * 2 + 2)
                    vec.wait_ge(hrstd_ready, t.n + 1)
                    nc.vector.scalar_tensor_tensor(out=Y[:], in0=O[:], scalar=GB[:, 2:3], in1=RS[:], op0=ALU.mult, op1=ALU.mult).then_inc(head_normed, 1)
                    vec.wait_ge(head_normed, t.n + 1)
                    after(vec, wout_done, t.n)
                    if isinstance(t.n, int) and t.n == 0:
                        vec.wait_ge(gates_used, GATES)
                    nc.vector.scalar_tensor_tensor(out=U[:], in0=Y[:], scalar=GB[:, 3:4], in1=SG[:, :, bass.ds(t.n * NTP, NTP)], op0=ALU.add, op1=ALU.mult).then_inc(gated, 1)

                def take_max(t, s):
                    vec.wait_ge(scores_done, t.n * 16 + (s + 1))
                    nc.vector.tensor_reduce(NM[:, s, :], PS[:, s % 2, :].rearrange("p (j k) -> p j k", j=2)[:, :, 0:NT], AX.X, ALU.max, negate=True).then_inc(maxes_taken, 1)

                def split_max(t):
                    vec.wait_ge(maxes_taken, t.n * 16 + 16)
                    after(vec, max_turned, t.n)
                    nm = NM[:].rearrange("p h j -> p j h")
                    chain.at = t.n * 3
                    chain.link(nc.vector.tensor_copy(NP[:, :, 0, :], nm))
                    chain.link(nc.vector.tensor_tensor(NR[:], nm, NP[:, :, 0, :], ALU.subtract))
                    chain.link(nc.vector.tensor_copy(NP[:, :, 1, :], NR[:]))
                    nc.vector.tensor_tensor(NP[:, :, 2, :], NR[:], NP[:, :, 1, :], ALU.subtract).then_inc(max_parts, 1)

                def scale_quad(t, q):
                    vec.wait_ge(inv_ready, t.n * 4 + (q + 1))
                    after(vec, heads_out, t.n * 2 + (q // 2 - 1))
                    av = PS[:, 4 + q % 2, 0:NTP]
                    if q % 2 == 0:
                        ins = nc.vector.tensor_tensor(AH[:, q, :], av, IN[q % 2][:], ALU.mult)
                    else:
                        ins = nc.vector.scalar_tensor_tensor(out=AH[:, q, :], in0=av, scalar=LS[:, 5:6], in1=IN[q % 2][:], op0=ALU.mult, op1=ALU.mult)
                    ins.then_inc(quad_scaled, 1)

                def update(t):
                    vec.wait_ge(wout_done, t.n + 1)
                    h = H[:, bass.ds(t.n * 2, 2), :]
                    nc.vector.tensor_tensor(h, PS[:, 6, 0:2 * D].rearrange("p (j f) -> p j f", j=2), h, ALU.add).then_inc(h_updated, 1)

                def prologue():
                    split(vec, nc.vector, Signal(0, 0))
                    split(vec, nc.vector, Signal(0, 1))
                    for s in range(SH):
                        take_max(Signal(0, 0), s)
                    split_max(Signal(0, 0))

                def step(b, front, nxt, tail):
                    for s in range(SH):
                        if nxt:
                            for head in coming(s):
                                take_max(b.next(1), head)
                        if s == SLOT["scale 2"] and tail:
                            scale_quad(b.next(-1), 2)
                        if s == SLOT["scale 3"] and tail:
                            scale_quad(b.next(-1), 3)
                        if s == NEXT_SLOTS - 1 and nxt:
                            split_max(b.next(1))
                        if s == SLOT["scale 0"]:
                            scale_quad(b, 0)
                        if s == SLOT["head norm"] and tail:
                            head_norm(b.next(-1))
                        if s == SLOT["scale 1"]:
                            scale_quad(b, 1)
                        if s == SLOT["residual"] and tail:
                            update(b.next(-1))

                def epilogue():
                    last = Signal(0, B - 1)
                    scale_quad(last, 2)
                    scale_quad(last, 3)
                    head_norm(last)
                    update(last)

                schedule(vec, prologue, step, epilogue)

            @block.gpsimd
            def _(pool):
                def prologue():
                    for n, where in enumerate((ones[:], *(KS[p][STACK:STACK + MAXROWS, :, :] for p in range(2)))):
                        nc.gpsimd.memset(where, 1.0).then_inc(ones_made, 1)
                        pool.wait_ge(ones_made, n + 1)

                def join(t, g):
                    pool.wait_ge(quad_scaled, t.n * 4 + (2 * g + 2))
                    after(pool, head_normed, t.n)
                    nc.gpsimd.tensor_tensor(O[:, g, :], AH[:, 2 * g, :], AH[:, 2 * g + 1, :], ALU.add).then_inc(heads_out, 1)

                def step(b, front, nxt, tail):
                    if front:
                        split(pool, nc.gpsimd, b.next(2))
                    if tail:
                        join(b.next(-1), 1)
                    join(b, 0)

                schedule(pool, prologue, step, lambda: join(Signal(0, B - 1), 1))

        end_stages()
        late = ctx.enter_context(ExitStack())

        def sl(name, shape, dt=F32):
            return late.enter_context(nc.sbuf_tensor(name, shape, dt))

        XN = sl("XN", [128, TILES, D])
        XR = sl("XR", [128, TILES, D])
        SQ2 = sl("SQ2", [128, TILES, D])
        XS2 = sl("XS2", [128, TILES, 3 * D], BF16)
        W2 = sl("W2", [128, NE, D])
        RT = sl("RT", [128, ROUTE_COLUMNS])
        WR8 = sl("WR8", [D, NE])
        BR8 = sl("BR8", [B, NE])
        B1 = sl("B1", [NE, FH])
        B2 = sl("B2", [NE, D])
        GA = sl("GA", [128, 2, D])
        route_in = sem("route_in")
        QUARTERS = 4
        QT = TILES // QUARTERS

        def quarter(n):
            return slice(QT * n, QT * n + QT)

        def across(column, width):
            return column.unsqueeze(2).broadcast_to([128, QT, width])

        class Norm:

            def __init__(self, name, src, dst):
                self.src, self.dst = src, dst
                self.centered, self.squared, self.summed = sem(name + "_centered"), sem(name + "_squared"), sem(name + "_summed")
                self.rstd, self.done, self.chain = sem(name + "_rstd"), sem(name + "_done"), sem(name + "_chain")
                self.logs = sem(name + "_logs")

            def vector(self, before=None):
                src, dst = self.src, self.dst
                chain = Chain(nc.vector, self.chain)
                for n in range(QUARTERS):
                    if before is not None:
                        before(n)
                    chain.link(nc.vector.tensor_reduce(st[:, 0, quarter(n)], src[:, quarter(n), :], AX.X, ALU.add))
                    nc.vector.scalar_tensor_tensor(out=dst[:, quarter(n), :], in0=across(st[:, 0, quarter(n)], D), scalar=-1.0 / D,
                                                   in1=src[:, quarter(n), :], op0=ALU.mult, op1=ALU.add).then_inc(self.centered, 1)
                for n in range(QUARTERS):
                    nc.vector.wait_ge(self.squared, n + 1)
                    nc.vector.tensor_reduce(st[:, 1, quarter(n)], SQ2[:, quarter(n), :], AX.X, ALU.add).then_inc(self.summed, 1)
                for n in range(QUARTERS):
                    nc.vector.wait_ge(self.rstd, n + 1)
                    nc.vector.tensor_tensor(dst[:, quarter(n), :], dst[:, quarter(n), :], across(st[:, 3, quarter(n)], D), ALU.mult).then_inc(self.done, 1)

            def scalar(self):
                chain = Chain(nc.scalar, self.logs)
                for n in range(QUARTERS):
                    nc.scalar.wait_ge(self.centered, n + 1)
                    nc.scalar.activation(SQ2[:, quarter(n), :], self.dst[:, quarter(n), :], ACT.Square).then_inc(self.squared, 1)
                for n in range(QUARTERS):
                    nc.scalar.wait_ge(self.summed, n + 1)
                    chain.link(nc.scalar.activation(st[:, 2, quarter(n)], st[:, 1, quarter(n)], ACT.Ln, scale=1.0 / D, bias=bias[:, 2:3]))
                    nc.scalar.activation(st[:, 3, quarter(n)], st[:, 2, quarter(n)], ACT.Exp, scale=-0.5).then_inc(self.rstd, 1)

        class Turn:

            def __init__(self, name, src, rest):
                self.src, self.rest = src, rest
                self.first, self.left, self.second, self.third = sem(name + "_first"), sem(name + "_left"), sem(name + "_second"), sem(name + "_third")
                self.turned = sem(name + "_turned0"), sem(name + "_turned1")
                self.copied0, self.copied1 = sem(name + "_copied0"), sem(name + "_copied1")

            def vector(self):
                for n in range(QUARTERS):
                    nc.vector.wait_ge(self.first, n + 1)
                    nc.vector.tensor_tensor(self.rest[:, quarter(n), :], self.src[:, quarter(n), :], XS2[:, quarter(n), D:2 * D], ALU.subtract).then_inc(self.left, 1)

            def vector_copies(self, quarters=range(QUARTERS)):
                for n in quarters:
                    nc.vector.wait_ge(self.turned[1], n + 1)
                    nc.vector.tensor_copy(XT[:, 1, 1024 * n:1024 * n + 1024], bank_bf16(4 + n)).then_inc(self.copied1, 1)

            def pool(self):
                for n in range(QUARTERS):
                    nc.gpsimd.wait_ge(self.second, n + 1)
                    nc.gpsimd.tensor_tensor(XS2[:, quarter(n), 2 * D:3 * D], self.rest[:, quarter(n), :], XS2[:, quarter(n), 0:D], ALU.subtract).then_inc(self.third, 1)

            def scalar(self, normed):
                for n in range(QUARTERS):
                    nc.scalar.wait_ge(normed, n + 1)
                    nc.scalar.copy(XS2[:, quarter(n), D:2 * D], self.src[:, quarter(n), :]).then_inc(self.first, 1)
                for n in range(QUARTERS):
                    nc.scalar.wait_ge(self.left, n + 1)
                    nc.scalar.copy(XS2[:, quarter(n), 0:D], self.rest[:, quarter(n), :]).then_inc(self.second, 1)

            def scalar_copies(self, quarters=range(QUARTERS)):
                for n in quarters:
                    nc.scalar.wait_ge(self.turned[0], n + 1)
                    nc.scalar.copy(XT[:, 0, 1024 * n:1024 * n + 1024], bank_bf16(n)).then_inc(self.copied0, 1)

            def tensor(self, kind, quarters=range(QUARTERS)):
                for n in quarters:
                    nc.tensor.wait_ge((self.second, self.third)[kind], n + 1)
                    for t in range(8):
                        m = nc.tensor.transpose(bank_bf16(4 * kind + n)[:, 128 * t:128 * t + 128], XS2[:, 8 * n + t, D * kind:D * kind + 128], identb[:])
                    m.then_inc(self.turned[kind], 1)

        WB = sl("WB", [128, B, 4])
        WI = sl("WI", [1, B, 2], mybir.dt.int32)
        B1S = sl("B1S", [FH, 2 * B])
        XM = sl("XM", [D, B])
        R = sl("R", [B, 16, NE])
        RQ = sl("RQ", [B, 2, NE, NE])
        RC = sl("RC", [B, 16])
        R4 = sl("R4", [B, B, 4])
        OT = sl("OT", [NE, 3, B])
        BE = sl("BE", [NE, B, D])
        ones8 = sl("ones8", [B, 128])
        fnorm = Norm("fnorm", H, XN)
        fturn = Turn("fturn", XN, SQ2)
        route_steps = sem("route_steps")
        means_done = sem("means_done"); mean_copied = sem("mean_copied"); logits_done = sem("route_logits_done")
        logits_shifted = sem("logits_shifted"); weights_exp = sem("weights_exp"); weights_ready = sem("weights_ready")
        loads_done = sem("loads_done"); weights_shifted = sem("weights_shifted"); second_exp = sem("second_exp")
        top_gap = sem("top_gap"); top_exp = sem("top_exp"); choice_ready = sem("choice_ready"); choice_turned = sem("choice_turned")
        choice_spread = sem("choice_spread"); one_hots_copied = sem("one_hots_copied"); b1_done = sem("b1_done"); b2_done = sem("b2_done")
        ones8_made = sem("ones8_made")
        LOGITS, LOADS = D, 2 * D
        with nc.Block("routing") as blk:
            @blk.sync
            def _(sp):
                sp.dma_start(RT[:], c_route).then_inc(route_in, 16)
                sp.dma_start(WR8[:], f_wr).then_inc(route_in, 16)
                sp.dma_start(BR8[:], bass.AP(tensor=f_br.tensor, offset=0, ap=[[0, B], [1, NE]])).then_inc(route_in, 16)
                sp.dma_start(B1[:], f_b1).then_inc(route_in, 16)
                sp.dma_start(B2[:], f_b2).then_inc(route_in, 16)
                sp.dma_start(W2[:], f_w2.rearrange("e f d -> f e d")).then_inc(route_in, 16)
                for n, v in enumerate((f_gamma, f_beta)):
                    sp.dma_start(GA[:, n, :], bass.AP(tensor=v.tensor, offset=0, ap=[[0, 128], [1, D]])).then_inc(route_in, 16)

            @blk.gpsimd
            def _(pool):
                nc.gpsimd.memset(ones8[:], 1.0).then_inc(ones8_made, 1)
                fturn.pool()

            @blk.scalar
            def _(act):
                nc.scalar.preload_act_table_set("natural_log_exp_and_others")
                fnorm.scalar()
                fturn.scalar(fnorm.done)
                fturn.scalar_copies(range(1))
                act.wait_ge(logits_shifted, 1)
                nc.scalar.activation(R[:, 2, :], R[:, 1, :], ACT.Exp).then_inc(weights_exp, 1)
                fturn.scalar_copies(range(1, QUARTERS))
                act.wait_ge(weights_shifted, 1)
                nc.scalar.activation(R[:, 5, :], R[:, 4, :], ACT.Exp).then_inc(second_exp, 1)
                act.wait_ge(top_gap, 1)
                nc.scalar.activation(RC[:, 9:10], RC[:, 8:9], ACT.Exp).then_inc(top_exp, 1)

            @blk.tensor
            def _(pe):
                pe.wait_ge(route_in, 16 * 8)
                for t in range(TILES):
                    rows = TP if t % 2 == 0 else LAST
                    b = t // 2
                    if t % QT == 0:
                        pe.wait_ge(fnorm.done, t // QT + 1)
                    mm = nc.tensor.matmul(PS[0:D, 7, 0:B], XN[0:rows, t, :], RT[0:rows, B - 1 - b:2 * B - 1 - b], start=(t == 0), stop=(t == TILES - 1))
                mm.then_inc(means_done, 1)
                fturn.tensor(0, range(1))
                pe.wait_ge(mean_copied, 1)
                nc.tensor.matmul(PS[0:B, 7, LOGITS:LOGITS + NE], XM[:], WR8[:], start=True, stop=True).then_inc(logits_done, 1)
                fturn.tensor(0, range(1, QUARTERS))
                fturn.tensor(1, range(1))
                pe.wait_ge(ones8_made, 1)
                pe.wait_ge(weights_ready, 1)
                nc.tensor.matmul(PS[0:B, 7, LOADS:LOADS + NE], ones8[:, 0:B], R[:, 3, :], start=True, stop=True).then_inc(loads_done, 1)
                fturn.tensor(1, range(1, QUARTERS - 1))
                pe.wait_ge(weights_shifted, 1)
                fturn.tensor(1, range(QUARTERS - 1, QUARTERS))
                pe.wait_ge(fturn.copied0, QUARTERS)
                pe.wait_ge(choice_ready, 1)
                for n, row in enumerate((10, 11, 12)):
                    tr = nc.tensor.transpose(PS[0:NE, 3, B * n:B * n + B], R[:, row, :], ident[0:B, 0:B])
                tr.then_inc(choice_turned, 1)
                nc.tensor.matmul(PS[:, 0, 0:4 * B], ones8[:], R4[:].rearrange("p b f -> p (b f)"), start=True, stop=True).then_inc(choice_spread, 1)
                pe.wait_ge(one_hots_copied, 1)
                nc.tensor.matmul(PS[:, 1, 0:2 * B], B1[:], OT[:, 0:2, :].rearrange("e s b -> e (s b)"), start=True, stop=True).then_inc(b1_done, 1)
                pe.wait_ge(fturn.copied1, 2)
                for n in range(2):
                    nc.tensor.matmul(PS[:, 4 + n, :], ones8[0:NE, :], BE[:, 8 * n:8 * n + 8, :].rearrange("e b f -> e (b f)"), start=True, stop=True).then_inc(b2_done, 1)

            @blk.vector
            def _(vec):
                fnorm.vector()
                fturn.vector()
                v = nc.vector
                c = Chain(vec, route_steps)
                vec.wait_ge(means_done, 1)
                v.tensor_copy(XM[:], PS[0:D, 7, 0:B]).then_inc(mean_copied, 1)
                vec.wait_ge(logits_done, 1)
                c.link(v.tensor_tensor(R[:, 0, :], PS[0:B, 7, LOGITS:LOGITS + NE], BR8[:], ALU.add))
                c.link(v.tensor_reduce(RC[:, 0:1], R[:, 0, :], AX.X, ALU.max))
                v.tensor_scalar(R[:, 1, :], R[:, 0, :], RC[:, 0:1], None, ALU.subtract).then_inc(logits_shifted, 1)
                vec.wait_ge(weights_exp, 1)
                c.link(v.tensor_reduce(RC[:, 1:2], R[:, 2, :], AX.X, ALU.add))
                c.link(v.reciprocal(RC[:, 2:3], RC[:, 1:2]))
                v.tensor_scalar(R[:, 3, :], R[:, 2, :], RC[:, 2:3], None, ALU.mult).then_inc(weights_ready, 1)
                vec.wait_ge(loads_done, 1)
                c.link(v.tensor_scalar(R[:, 6, :], PS[0:B, 7, LOADS:LOADS + NE], float(NT), None, ALU.mult))
                c.link(v.reciprocal(R[:, 7, :], R[:, 6, :]))
                c.link(v.tensor_scalar(R[:, 8, :], R[:, 7, :], CAPACITY, 1.0, ALU.mult, ALU.min))
                c.link(v.tensor_tensor(R[:, 9, :], R[:, 3, :], R[:, 8, :], ALU.mult))
                c.link(v.tensor_reduce(RC[:, 4:5], R[:, 9, :], AX.X, ALU.max))
                v.tensor_scalar(R[:, 4, :], R[:, 9, :], RC[:, 4:5], None, ALU.subtract).then_inc(weights_shifted, 1)
                fturn.vector_copies(range(1))
                vec.wait_ge(second_exp, 1)
                c.link(v.tensor_reduce(RC[:, 5:6], R[:, 5, :], AX.X, ALU.add))
                c.link(v.reciprocal(RC[:, 3:4], RC[:, 5:6]))
                w = R[:, 13, :]
                c.link(v.tensor_scalar(w, R[:, 5, :], RC[:, 3:4], None, ALU.mult))
                others = w.unsqueeze(1).broadcast_to([B, NE, NE])
                own = w.unsqueeze(2).broadcast_to([B, NE, NE])
                earlier = RT[0:B, EARLIER:EARLIER + NE * NE].rearrange("p (e j) -> p e j", e=NE)
                c.step(v.tensor_tensor(RQ[:, 0], others, own, ALU.is_gt))
                c.link(v.tensor_tensor(RQ[:, 1], others, own, ALU.is_equal))
                c.link(v.tensor_tensor(RQ[:, 1], RQ[:, 1], earlier, ALU.mult))
                c.link(v.tensor_tensor(RQ[:, 0], RQ[:, 0], RQ[:, 1], ALU.add))
                c.link(v.tensor_reduce(R[:, 14, :], RQ[:, 0], AX.X, ALU.add))
                c.step(v.tensor_scalar(R[:, 10, :], R[:, 14, :], 0.0, None, ALU.is_equal))
                c.link(v.tensor_scalar(R[:, 11, :], R[:, 14, :], 1.0, None, ALU.is_equal))
                for s in range(2):
                    c.link(v.tensor_tensor(R[:, 15, :], R[:, 10 + s, :], w, ALU.mult))
                    c.link(v.tensor_reduce(RC[:, 6 + s:7 + s], R[:, 15, :], AX.X, ALU.add))
                v.tensor_tensor(RC[:, 8:9], RC[:, 7:8], RC[:, 6:7], ALU.subtract).then_inc(top_gap, 1)
                fturn.vector_copies(range(1, 2))
                vec.wait_ge(top_exp, 1)
                c.link(v.tensor_scalar(RC[:, 13:14], RC[:, 9:10], 1.0, None, ALU.add))
                c.link(v.reciprocal(RC[:, 10:11], RC[:, 13:14]))
                c.link(v.tensor_tensor(RC[:, 11:12], RC[:, 9:10], RC[:, 10:11], ALU.mult))
                c.link(v.tensor_scalar(R[:, 12, :], R[:, 10, :], RC[:, 10:11], None, ALU.mult))
                c.link(v.scalar_tensor_tensor(out=R[:, 12, :], in0=R[:, 11, :], scalar=RC[:, 11:12], in1=R[:, 12, :], op0=ALU.mult, op1=ALU.add))
                diag = ident[0:B, 0:B]
                numbers = RT[0:B, NUMBERS:NUMBERS + NE]
                for s in range(2):
                    c.step(v.tensor_scalar(R4[:, :, s], diag, RC[:, 10 + s:11 + s], None, ALU.mult))
                    c.link(v.tensor_tensor(R[:, 15, :], R[:, 10 + s, :], numbers, ALU.mult))
                    c.link(v.tensor_reduce(RC[:, 12:13], R[:, 15, :], AX.X, ALU.add))
                    last = v.tensor_scalar(R4[:, :, 2 + s], diag, RC[:, 12:13], None, ALU.mult)
                    if s == 0:
                        c.link(last)
                    else:
                        last.then_inc(choice_ready, 1)
                vec.wait_ge(choice_turned, 1)
                c.link(v.tensor_copy(OT[:].rearrange("e s b -> e (s b)"), PS[0:NE, 3, 0:3 * B]))
                v.tensor_tensor(BE[:], B2[:].unsqueeze(1).broadcast_to([NE, B, D]), OT[:, 2, :].unsqueeze(2).broadcast_to([NE, B, D]), ALU.mult).then_inc(one_hots_copied, 1)
                fturn.vector_copies(range(2, QUARTERS))
                vec.wait_ge(choice_spread, 1)
                c.link(v.tensor_copy(WB[:].rearrange("p b f -> p (b f)"), PS[:, 0, 0:4 * B]))
                c.step(v.tensor_copy(WI[:], WB[0:1, :, 2:4]))
                vec.wait_ge(b1_done, 1)
                c.step(v.tensor_copy(B1S[:], PS[:, 1, 0:2 * B]))
                for n in range(2):
                    vec.wait_ge(b2_done, n + 1)
                    for j in range(2):
                        tiles = slice(B * n, B * n + B)
                        out4 = XR[:, tiles, :].rearrange("p (b j) f -> p j b f", j=2)[:, j]
                        in4 = XN[:, tiles, :].rearrange("p (b j) f -> p j b f", j=2)[:, j]
                        c.step(v.tensor_tensor(out4, PS[:, 4 + n, :].rearrange("p (b f) -> p b f", f=D), in4, ALU.add))

        with ExitStack() as three:
            def sa(name, shape, dt=F32):
                return three.enter_context(nc.sbuf_tensor(name, shape, dt))
            GE = [sa(f"GE{p}", [FH, 2, NTP]) for p in range(2)]
            PICKS = 4
            TA = sa("TA", [128, 2, 2, D])
            P1 = sa("P1", [128, PICKS, 2, 3, FH], BF16)
            P2 = sa("P2", [128, PICKS, 2, D])
            picked = [sem("first_picked"), sem("second_picked")]
            vec_passed = sem("vec_passed"); act_passed = sem("ffn_act_passed")
            hidden_done = sem("hidden_done"); gelu_ready = sem("gelu_ready"); expert_done = sem("expert_done")
            mix_chain = sem("mix_chain"); mixed = sem("mixed")

            def schedule(eng, step):
                step(0, 0)
                with eng.Fori(0, (B - PICKS) // PICKS) as i:
                    for c in range(1, 1 + PICKS):
                        step(i * PICKS + c, c)
                for n in range(B - PICKS + 1, B - 1):
                    step(n, n)

            def pick(eng, copy, passed, s, n, w):
                after(eng, hidden_done, n - (PICKS - 1))
                wait_apart(eng, expert_done, n - (PICKS - 1), passed)
                e = eng.value_load(WI[0:1, bass.ds(n, 1), s:s + 1], min_val=0, max_val=NE - 1)
                copy(P1[:, w, s], WS[:, :, bass.ds(e * FH + NQKVG, FH)]).then_inc(picked[s], 1)
                copy(P2[:, w, s, :], W2[:, bass.ds(e, 1), :].rearrange("p e d -> p (e d)")).then_inc(picked[s], 1)

            with nc.Block("ffn") as blk:
                @blk.tensor
                def _(pe):
                    def hidden(n, p, w):
                        after(pe, gelu_ready, (n - 1) * 2)
                        for s in range(2):
                            pe.wait_ge(picked[s], n * 2 + 2)
                            for k in range(3):
                                mm = nc.tensor.matmul(PS[:, p, NTP * s:NTP * s + NTP], P1[:, w, s, k, :], XT[:, k // 2, bass.ds(n * NTP, NTP)], start=(k == 0), stop=(k == 2))
                        mm.then_inc(hidden_done, 1)

                    def output(n, p, w):
                        after(pe, mixed, n)
                        pe.wait_ge(gelu_ready, n * 2 + 2)
                        for s in range(2):
                            for j in range(2):
                                mm = nc.tensor.matmul(PS[:, 2 + p, D * (2 * j + s):D * (2 * j + s) + D], GE[p][:, s, TP * j:TP * j + TP], P2[:, w, s, :], start=True, stop=True)
                        mm.then_inc(expert_done, 1)

                    def step(n, c):
                        hidden(n + 1, (c + 1) % 2, (c + 1) % PICKS)
                        output(n, c % 2, c % PICKS)

                    hidden(0, 0, 0)
                    schedule(pe, step)
                    output(B - 1, 1, (B - 1) % PICKS)

                @blk.scalar
                def _(act):
                    nc.scalar.preload_act_table(ACT.Gelu)

                    def gelu(n, p):
                        act.wait_ge(hidden_done, n + 1)
                        after(act, expert_done, n - 1)
                        for s in range(2):
                            nc.scalar.activation(GE[p][:, s, :], PS[:, p, NTP * s:NTP * s + NTP], ACT.Gelu, bias=B1S[:, bass.ds(n + B * s, 1)]).then_inc(gelu_ready, 1)

                    def step(n, c):
                        gelu(n + 1, (c + 1) % 2)
                        if c < B - PICKS + 1:
                            pick(act, nc.scalar.copy, act_passed, 1, n + PICKS - 1, (c + PICKS - 1) % PICKS)

                    for n in range(PICKS - 1):
                        pick(act, nc.scalar.copy, act_passed, 1, n, n)
                    gelu(0, 0)
                    schedule(act, step)

                @blk.vector
                def _(vec):
                    chain = Chain(vec, mix_chain)

                    def mix(n, p):
                        vec.wait_ge(expert_done, n + 1)
                        y = PS[:, 2 + p, 0:4 * D].rearrange("p (j s f) -> p s j f", j=2, s=2)
                        xr = XR[:, bass.ds(n * 2, 2), :]
                        chain.at = n
                        chain.link(nc.vector.scalar_tensor_tensor(out=TA[:, p], in0=y[:, 0], scalar=WB[:, bass.ds(n, 1), 0], in1=xr, op0=ALU.mult, op1=ALU.add))
                        nc.vector.scalar_tensor_tensor(out=xr, in0=y[:, 1], scalar=WB[:, bass.ds(n, 1), 1], in1=TA[:, p], op0=ALU.mult, op1=ALU.add).then_inc(mixed, 1)

                    def step(n, c):
                        if c < B - PICKS + 1:
                            pick(vec, nc.vector.tensor_copy, vec_passed, 0, n + PICKS - 1, (c + PICKS - 1) % PICKS)
                        mix(n, c % 2)

                    vec.sem_inc(mixed, 1)
                    for n in range(PICKS - 1):
                        pick(vec, nc.vector.tensor_copy, vec_passed, 0, n, n)
                    schedule(vec, step)
                    mix(B - 1, 1)


        onorm = Norm("onorm", XR, XR)
        anorm = Norm("anorm", H, XN)
        flat_scratch = nc.dram_tensor("flat_scratch", (B, NTP, D), F32).ap()
        back_scratch = nc.dram_tensor("back_scratch", (B, NTP, D), F32).ap()

        def as_rows(scratch, pair):
            return bass.AP(tensor=scratch.tensor, offset=pair * (2 * NTP * D), ap=[[NTP * D, 2], [NT, D], [1, NT]])

        with ExitStack() as four:
            def sa(name, shape, dt=F32):
                return four.enter_context(nc.sbuf_tensor(name, shape, dt))
            AW = sa("AW", [128, 4, 128])
            AB = sa("AB", [128, 2])
            AR = sa("AR", [128, 2, 128])
            FL = [sa(f"FL{p}", [128, NTP]) for p in range(2)]
            KB = sa("KB", [128, NTP]); KE = [sa(f"KE{p}", [128, NTP]) for p in range(2)]
            KM = sa("KM", [128, 4])
            QB = sa("QB", [128, 2, 128]); QE = [sa(f"QE{p}", [128, 2, 128]) for p in range(2)]
            QM = sa("QM", [128, 4, 32])
            VT = [sa(f"VT{p}", [128, 2, 128]) for p in range(2)]
            KT = sa("KT", [128, 2, 128]); QF = sa("QF", [128, NTP]); CT = sa("CT", [128, 128])
            AG = sa("AG", [128, NTP]); OF = [sa(f"OF{p}", [128, NTP]) for p in range(2)]
            a_weights_in = sem("a_weights_in"); aw_zeroed = sem("aw_zeroed"); residual_added = sem("residual_added")
            beta_added = sem("beta_added"); gamma_times = sem("gamma_times"); flat_written = [sem(f"flat_written_{n}") for n in range(QUARTERS)]; dummies_written = sem("dummies_written"); fl_zeroed = sem("fl_zeroed")
            flat_in = [sem("flat_in_even"), sem("flat_in_odd")]
            ka_done = sem("ka_done"); qa_done = sem("qa_done"); va_done = sem("va_done"); kb_ready = sem("kb_ready"); kmax_ready = sem("kmax_ready")
            ke_ready = sem("ke_ready"); ka_chain = sem("ka_chain"); qshift_ready = sem("qshift_ready"); qexp_ready = sem("qexp_ready")
            qa_chain = sem("qa_chain"); qsoft_ready = sem("qsoft_ready"); vt_ready = sem("vt_ready")
            kt_turned = sem("kt_turned"); qf_turned = sem("qf_turned"); kt_copied = sem("kt_copied"); qf_copied = sem("qf_copied")
            context_done = sem("context_done"); context_ready = sem("context_ready"); agg_done = sem("agg_done")
            agg_copied = sem("agg_copied"); proj_done = sem("proj_done"); of_ready = sem("of_ready"); of_written = [sem("of_written_even"), sem("of_written_odd")]
            back_in = [sem(f"back_in_{n}") for n in range(QUARTERS)]

            def schedule(eng, step):
                def at(n):
                    return n, n % 2, n // 2

                step(None, at(0))
                step(at(0), at(1))
                step(at(1), at(2))
                with eng.Fori(0, PAIRS // 2 - 2) as i:
                    step((i * 2 + 2, 0, i + 1), (i * 2 + 3, 1, i + 1))
                    step((i * 2 + 3, 1, i + 1), (i * 2 + 4, 0, i + 2))
                step(at(PAIRS - 2), at(PAIRS - 1))
                step(at(PAIRS - 1), None)

            with nc.Block("linear_attention") as blk:
                @blk.gpsimd
                def _(pool):
                    nc.gpsimd.memset(AW[:], 0.0).then_inc(aw_zeroed, 1)
                    for p in range(2):
                        m = nc.gpsimd.memset(FL[p][:], 0.0)
                    m.then_inc(fl_zeroed, 1)
                    nc.gpsimd.tensor_tensor(H[:], H[:], GA[:, 1, :].unsqueeze(1).broadcast_to([128, TILES, D]), ALU.add).then_inc(beta_added, 1)
                    for n in range(QUARTERS):
                        pool.wait_ge(onorm.done, n + 1)
                        xr = XR[:, quarter(n), :]
                        nc.gpsimd.tensor_tensor(xr, xr, GA[:, 0, :].unsqueeze(1).broadcast_to([128, QT, D]), ALU.mult).then_inc(gamma_times, 1)

                @blk.sync
                def _(sp):
                    sp.wait_ge(aw_zeroed, 1)
                    for n, w in enumerate((a_wk, a_wq, a_wv, a_wr)):
                        for half in (0, 64):
                            sp.dma_start(AW[half:half + 64, n, half:half + 64], w).then_inc(a_weights_in, 16)
                    for half in (0, 64):
                        for n, w in enumerate((a_bk, a_br)):
                            sp.dma_start(AB[half:half + 64, n:n + 1], w.rearrange("(p a) -> p a", a=1), allow_slow_non_contiguous=True).then_inc(a_weights_in, 16)
                        for n, w in enumerate((a_bq, a_bv)):
                            sp.dma_start(AR[:, n, half:half + 64], bass.AP(tensor=w.tensor, offset=0, ap=[[0, 128], [1, D]])).then_inc(a_weights_in, 16)
                    for n in range(QUARTERS):
                        sp.wait_ge(anorm.done, n + 1)
                        src = XN[:, quarter(n), :]
                        dst = flat_scratch[4 * n:4 * n + 4].rearrange("b (j t) f -> t (b j) f", j=2)
                        sp.dma_start(dst, src).then_inc(flat_written[n], 16)
                    sp.dma_start(back_scratch[:, NT, :], XN[0:B, 0, :]).then_inc(dummies_written, 16)

                    def load(n):
                        p = n % 2
                        sp.wait_ge(flat_written[n // 2], 16)
                        after(sp, va_done, n - 1)
                        sp.dma_start(FL[p][:, 0:NT], as_rows(flat_scratch, n)).then_inc(flat_in[p], 16)

                    def store(n):
                        sp.wait_ge(of_ready, n + 1)
                        sp.dma_start(as_rows(back_scratch, n), OF[n % 2][:, 0:NT]).then_inc(of_written[n % 2], 16)

                    def back(q):
                        for p in range(2):
                            sp.wait_ge(of_written[p], 16 * (q + 1))
                        sp.dma_start(XR[:, quarter(q), :], back_scratch[4 * q:4 * q + 4].rearrange("b (j t) f -> t (b j) f", j=2)).then_inc(back_in[q], 16)

                    sp.wait_ge(dummies_written, 16)
                    load(0)
                    load(1)
                    for n in range(PAIRS):
                        if n + 2 < PAIRS:
                            load(n + 2)
                        store(n)
                        if n > 2 and n % 2:
                            back((n - 3) // 2)
                    back(QUARTERS - 1)

                @blk.tensor
                def _(pe):
                    def project_queries(n, p, turn):
                        pe.wait_ge(flat_in[p], turn * 16 + 16)
                        after(pe, qshift_ready, n - 1)
                        after(pe, vt_ready, n - 1)
                        for j in range(2):
                            mm = nc.tensor.matmul(PS[:, 2 + p, 128 * j:128 * j + 128], FL[p][:, TP * j:TP * j + TP], AW[:, 1, :], start=True, stop=True)
                        mm.then_inc(qa_done, 1)

                    def project_keys(n, p):
                        after(pe, kb_ready, n - 1)
                        nc.tensor.matmul(PS[:, p, 0:NTP], AW[:, 0, :], FL[p][:], start=True, stop=True).then_inc(ka_done, 1)

                    def project_values(n, p):
                        pe.wait_ge(qshift_ready, n + 1)
                        for j in range(2):
                            mm = nc.tensor.matmul(PS[:, 2 + p, 256 + 128 * j:384 + 128 * j], FL[p][:, TP * j:TP * j + TP], AW[:, 2, :], start=True, stop=True)
                        mm.then_inc(va_done, 1)

                    def turn_both(n, p):
                        after(pe, kt_copied, n)
                        pe.wait_ge(ke_ready, n + 1)
                        for j in range(2):
                            rows = TP if j == 0 else LAST
                            tr = nc.tensor.transpose(PS[0:rows, 4, 128 * j:128 * j + 128], KE[p][:, TP * j:TP * j + rows], ident[:])
                        tr.then_inc(kt_turned, 1)
                        after(pe, qf_copied, n)
                        pe.wait_ge(qsoft_ready, n + 1)
                        for j in range(2):
                            tr = nc.tensor.transpose(PS[:, 5, 128 * j:128 * j + 128], QE[p][:, j, :], ident[:])
                        tr.then_inc(qf_turned, 1)

                    def contexts(n, p):
                        pe.wait_ge(kt_copied, n + 1)
                        pe.wait_ge(vt_ready, n + 1)
                        after(pe, agg_copied, n)
                        for j in range(2):
                            rows = TP if j == 0 else LAST
                            mm = nc.tensor.matmul(PS[:, 6, 0:128], KT[0:rows, j, :], VT[p][0:rows, j, :], start=(j == 0), stop=(j == 1))
                        mm.then_inc(context_done, 1)

                    def attend(n):
                        pe.wait_ge(context_ready, n + 1)
                        pe.wait_ge(qf_copied, n + 1)
                        nc.tensor.matmul(PS[:, 6, 0:NTP], CT[:], QF[:], start=True, stop=True).then_inc(agg_done, 1)

                    def project_out(n):
                        pe.wait_ge(agg_copied, n + 1)
                        after(pe, of_ready, n)
                        nc.tensor.matmul(PS[:, 7, 0:NTP], AW[:, 3, :], AG[:], start=True, stop=True).then_inc(proj_done, 1)

                    def step(now, coming):
                        if now:
                            turn_both(now[0], now[1])
                        if coming:
                            project_queries(*coming)
                        if now:
                            contexts(now[0], now[1])
                        if coming:
                            project_keys(coming[0], coming[1])
                        if now:
                            attend(now[0])
                        if coming:
                            project_values(coming[0], coming[1])
                        if now:
                            project_out(now[0])

                    schedule(pe, step)

                @blk.scalar
                def _(act):
                    nc.scalar.preload_act_table_set("natural_log_exp_and_others")
                    onorm.scalar()
                    anorm.scalar()

                    def soft_keys(n, p):
                        after(act, kt_turned, n - 1)
                        act.wait_ge(kmax_ready, n + 1)
                        nc.scalar.activation(KE[p][:, 0:NT], KB[:, 0:NT], ACT.Exp, bias=KM[:, 0:1], accum_out=KM[:, 2 + p:3 + p]).then_inc(ke_ready, 1)

                    def soft_queries(n, p):
                        after(act, qf_turned, n - 1)
                        act.wait_ge(qshift_ready, n + 1)
                        nc.scalar.activation(QE[p][:], QB[:], ACT.Exp).then_inc(qexp_ready, 1)

                    def copy_turned(n):
                        act.wait_ge(kt_turned, n + 1)
                        after(act, context_done, n)
                        nc.scalar.copy(KT[:, 0, :], PS[:, 4, 0:128])
                        nc.scalar.copy(KT[0:LAST, 1, :], PS[0:LAST, 4, 128:256]).then_inc(kt_copied, 1)
                        act.wait_ge(qf_turned, n + 1)
                        after(act, agg_done, n)
                        nc.scalar.copy(QF[:], PS[:, 5, 0:NTP]).then_inc(qf_copied, 1)

                    def copy_attended(n):
                        act.wait_ge(agg_done, n + 1)
                        after(act, proj_done, n)
                        nc.scalar.copy(AG[:], PS[:, 6, 0:NTP]).then_inc(agg_copied, 1)

                    def add_bias(n, p, turn):
                        act.wait_ge(proj_done, n + 1)
                        after(act, of_written[p], turn * 16)
                        nc.scalar.activation(OF[p][:], PS[:, 7, 0:NTP], ACT.Identity, bias=AB[:, 1:2]).then_inc(of_ready, 1)

                    def step(now, coming):
                        if now:
                            copy_turned(now[0])
                        if coming:
                            soft_queries(coming[0], coming[1])
                        if now:
                            copy_attended(now[0])
                        if coming:
                            soft_keys(coming[0], coming[1])
                        if now:
                            add_bias(*now)

                    schedule(act, step)

                @blk.vector
                def _(vec):
                    onorm.vector()
                    def add_ffn(n):
                        vec.wait_ge(beta_added, 1)
                        vec.wait_ge(gamma_times, n + 1)
                        nc.vector.tensor_tensor(H[:, quarter(n), :], H[:, quarter(n), :], XR[:, quarter(n), :], ALU.add).then_inc(residual_added, 1)
                        vec.wait_ge(residual_added, n + 1)

                    anorm.vector(add_ffn)

                    kchain = Chain(vec, ka_chain)
                    qchain = Chain(vec, qa_chain)

                    def queries(n, p):
                        qchain.at = n * 4
                        vec.wait_ge(qa_done, n + 1)
                        after(vec, qexp_ready, n)
                        half = PS[:, 2 + p, 0:256].rearrange("p (j c) -> p j c", j=2)
                        qchain.link(nc.vector.tensor_tensor(QB[:], half, AR[:, 0, :].unsqueeze(1).broadcast_to([128, 2, 128]), ALU.add))
                        groups = QB[:].rearrange("p j (g k) -> p (j g) k", k=LK)
                        qchain.link(nc.vector.tensor_reduce(QM[:, 0, :], groups, AX.X, ALU.max))
                        nc.vector.tensor_tensor(groups, groups, QM[:, 0, :].unsqueeze(2).broadcast_to([128, 32, LK]), ALU.subtract).then_inc(qshift_ready, 1)

                    def divide_queries(n, p):
                        vec.wait_ge(qexp_ready, n + 1)
                        egroups = QE[p][:].rearrange("p j (g k) -> p (j g) k", k=LK)
                        qchain.link(nc.vector.tensor_reduce(QM[:, 1, :], egroups, AX.X, ALU.add))
                        qchain.link(nc.vector.reciprocal(QM[:, 2, :], QM[:, 1, :]))
                        nc.vector.tensor_tensor(egroups, egroups, QM[:, 2, :].unsqueeze(2).broadcast_to([128, 32, LK]), ALU.mult).then_inc(qsoft_ready, 1)

                    def keys(n, p):
                        vec.wait_ge(ka_done, n + 1)
                        after(vec, ke_ready, n)
                        nc.vector.tensor_scalar(KB[:, 0:NT], PS[:, p, 0:NT], AB[:, 0:1], None, ALU.add).then_inc(kb_ready, 1)
                        vec.wait_ge(kb_ready, n + 1)
                        nc.vector.tensor_reduce(KM[:, 0:1], KB[:, 0:NT], AX.X, ALU.max, negate=True).then_inc(kmax_ready, 1)

                    def values(n, p):
                        vec.wait_ge(va_done, n + 1)
                        after(vec, context_done, n - 1)
                        half = PS[:, 2 + p, 256:512].rearrange("p (j c) -> p j c", j=2)
                        nc.vector.tensor_tensor(VT[p][:], half, AR[:, 1, :].unsqueeze(1).broadcast_to([128, 2, 128]), ALU.add).then_inc(vt_ready, 1)

                    def context(n, p):
                        vec.wait_ge(ke_ready, n + 1)
                        after(vec, context_ready, n)
                        kchain.at = n
                        kchain.link(nc.vector.reciprocal(KM[:, 1:2], KM[:, 2 + p:3 + p]))
                        vec.wait_ge(context_done, n + 1)
                        after(vec, agg_done, n)
                        nc.vector.scalar_tensor_tensor(out=CT[:], in0=PS[:, 6, 0:128], scalar=KM[:, 1:2], in1=RT[:, HEADS:HEADS + 128],
                                                       op0=ALU.mult, op1=ALU.mult).then_inc(context_ready, 1)

                    def step(now, coming):
                        if now:
                            context(now[0], now[1])
                        if coming:
                            n, p, _ = coming
                            queries(n, p)
                            keys(n, p)
                            divide_queries(n, p)
                            values(n, p)

                    schedule(vec, step)

        mnorm = Norm("mnorm", H, XN)
        mturn = Turn("mturn", XN, SQ2)
        M1 = NQKVG + NW1
        GATE = M1 + D + ME * MH
        GROUPS = 1 + ME
        with ExitStack() as five:
            def sa(name, shape, dt=F32):
                return five.enter_context(nc.sbuf_tensor(name, shape, dt))
            MW2 = sa("MW2", [MH, ME, D])
            SW2 = sa("SW2", [128, 128])
            EW3 = sa("EW3", [128, ME // 2, 128])
            SW3 = sa("SW3", [128, D])
            MB1 = sa("MB1", [128, GROUPS])
            MB2 = sa("MB2", [128, 1 + ME // 2])
            OB = sa("OB", [3, GROUPS * D])
            OBR = sa("OBR", [3, GROUPS * D])
            OB1 = sa("OB1", [3, GROUPS * D], BF16)
            OB2 = sa("OB2", [3, GROUPS * D], BF16)
            OB3 = sa("OB3", [3, GROUPS * D], BF16)
            ones3 = sa("ones3", [3, TP], BF16)
            GBB = sa("GBB", [128, ME])
            ZL = sa("ZL", [128, TILES, ME])
            G1 = sa("G1", [128, TILES, ME])
            G2 = sa("G2", [128, TILES, ME])
            GQ = sa("GQ", [128, 2, TILES, ME, ME])
            GS = sa("GS", [128, 6, TILES])
            G5 = sa("G5", [128, TILES, GROUPS])
            H1 = sa("H1", [128, GROUPS, NTP])
            H2 = sa("H2", [128, 1 + ME // 2, NTP])
            WM = sa("WM", [128, 2, GROUPS, D])
            MO = sa("MO", [128, 2, D])
            sp_passed = sem("sp_passed_experts")
            attention_added = sem("attention_added")
            m_zeroed = sem("m_zeroed"); m_weights_in = sem("m_weights_in"); biases_spread = sem("biases_spread")
            logits_done = sem("logits_done"); gate_steps = sem("gate_steps"); gate_exps = sem("gate_exps"); gates_shifted = sem("gates_shifted"); gates_gap = sem("gates_gap")
            bias_chain = sem("bias_chain")
            first_done = sem("first_done"); first_relu = sem("first_relu"); second_done = sem("second_done")
            second_relu = sem("second_relu"); third_done = sem("third_done"); weighted = sem("weighted")
            sum_chain = sem("sum_chain"); token_ready = sem("token_ready"); out_written = sem("out_written")

            with nc.Block("experts") as blk:
                @blk.gpsimd
                def _(pool):
                    nc.gpsimd.memset(MB1[:, 0:1], 0.0)
                    nc.gpsimd.memset(SW2[:], 0.0)
                    nc.gpsimd.memset(G5[:, :, ME:GROUPS], 1.0)
                    nc.gpsimd.memset(EW3[:], 0.0).then_inc(m_zeroed, 1)
                    mturn.pool()
                    pool.wait_ge(m_weights_in, 16 * 13)
                    chain = Chain(pool, bias_chain)
                    g = nc.gpsimd
                    chain.step(g.memset(ones3[:], 1.0))
                    chain.link(g.tensor_copy(OB1[:], OB[:]))
                    chain.link(g.tensor_tensor(OBR[:], OB[:], OB1[:], ALU.subtract))
                    chain.link(g.tensor_copy(OB2[:], OBR[:]))
                    chain.link(g.tensor_tensor(OB3[:], OBR[:], OB2[:], ALU.subtract))
                    for part, row in ((OB1, 0), (OB2, 1), (OB3, 2)):
                        chain.link(g.tensor_scalar(part[:], part[:], ident[0:3, row:row + 1], None, ALU.mult))
                    chain.link(g.tensor_tensor(OB1[:], OB1[:], OB2[:], ALU.add))
                    g.tensor_tensor(OB1[:], OB1[:], OB3[:], ALU.add).then_inc(biases_spread, 1)

                @blk.sync
                def _(sp):
                    sp.dma_start(GBB[:], bass.AP(tensor=m_gb.tensor, offset=0, ap=[[0, 128], [1, ME]])).then_inc(m_weights_in, 16)
                    sp.dma_start(OB[:, 0:ME * D], bass.AP(tensor=m_eb3.tensor, offset=0, ap=[[0, 3], [1, ME * D]])).then_inc(m_weights_in, 16)
                    sp.dma_start(OB[:, ME * D:GROUPS * D], bass.AP(tensor=m_sb3.tensor, offset=0, ap=[[0, 3], [1, D]])).then_inc(m_weights_in, 16)
                    sp.dma_start(MW2[:], m_ew2.rearrange("e h g -> h e g")).then_inc(m_weights_in, 16)
                    sp.dma_start(SW3[:], m_sw3).then_inc(m_weights_in, 16)
                    sp.dma_start(MB1[:, 1:GROUPS], m_eb1.rearrange("e h -> h e"), allow_slow_non_contiguous=True).then_inc(m_weights_in, 16)
                    for half in range(2):
                        sp.dma_start(MB2[D * half:D * half + D, 0:2], m_eb2.rearrange("(q r) g -> g r q", r=2)[:, half], allow_slow_non_contiguous=True).then_inc(m_weights_in, 16)
                    sp.dma_start(MB2[:, 2:3], m_sb2.rearrange("(p a) -> p a", a=1), allow_slow_non_contiguous=True).then_inc(m_weights_in, 16)
                    sp.wait_ge(m_zeroed, 1)
                    sp.dma_start(MB1[0:D, 0:1], m_sb1.rearrange("(p a) -> p a", a=1), allow_slow_non_contiguous=True).then_inc(m_weights_in, 16)
                    sp.dma_start(SW2[0:D, :], m_sw2).then_inc(m_weights_in, 16)
                    for half in range(2):
                        sp.dma_start(EW3[D * half:D * half + D, :, D * half:D * half + D], m_ew3.rearrange("(q r) g f -> r g q f", r=2)[half]).then_inc(m_weights_in, 16)
                    sp.wait_ge(m_weights_in, 16 * 13)

                    with sp.Fori(0, B) as i:
                        wait_apart(sp, token_ready, i + 1, sp_passed)
                        for j, lo, hi in ((0, 0, TP), (1, 0, 112), (1, 112, LAST)):
                            dst = bass.AP(tensor=out.tensor, offset=i * (NT * D) + D * (TP * j + lo), ap=[[D, hi - lo], [1, D]])
                            sp.dma_start(dst, H[lo:hi, bass.ds(i * 2 + j, 1), :].rearrange("p a f -> p (a f)")).then_inc(out_written, 16)
                    sp.wait_ge(out_written, 16 * 3 * B)

                @blk.tensor
                def _(pe):
                    for kind in range(2):
                        mturn.tensor(kind)
                    pe.wait_ge(mturn.copied0, QUARTERS)
                    pe.wait_ge(mturn.copied1, QUARTERS)
                    for t in range(TILES):
                        for s in range(3):
                            mm = nc.tensor.matmul(PS[:, 7, ME * t:ME * t + ME], XT[:, s // 2, TP * t:TP * t + TP], WS[:, s, GATE:GATE + ME], start=(s == 0), stop=(s == 2))
                    mm.then_inc(logits_done, 1)

                    def place(g):
                        return PS[:, g // 2, NTP * (g % 2):NTP * (g % 2) + NTP]

                    def first(n):
                        for g in range(GROUPS):
                            if g % 2 == 0:
                                after(pe, first_relu, (n - 1) * GROUPS + min(g + 2, GROUPS))
                            column = M1 if g == 0 else M1 + D + MH * (g - 1)
                            for s in range(3):
                                mm = nc.tensor.matmul(place(g), WS[:, s, column:column + 128], XT[:, s // 2, bass.ds(n * NTP, NTP)], start=(s == 0), stop=(s == 2))
                            mm.then_inc(first_done, 1)

                    def second(n):
                        after(pe, second_relu, n * 3)
                        pe.wait_ge(first_relu, n * GROUPS + GROUPS)
                        for q in range(ME // 2):
                            for half in range(2):
                                mm = nc.tensor.matmul(PS[D * half:D * half + D, 3, NTP * q:NTP * q + NTP], MW2[:, 2 * q + half, :], H1[:, 1 + 2 * q + half, :], start=True, stop=True)
                        mm.then_inc(second_done, 1)
                        nc.tensor.matmul(PS[:, 4, 0:NTP], SW2[:], H1[:, 0, :], start=True, stop=True).then_inc(second_done, 1)

                    def third(n):
                        after(pe, weighted, n)
                        if isinstance(n, int) and n == 0:
                            pe.wait_ge(biases_spread, 1)
                        for j in range(2):
                            nc.tensor.matmul(PS[:, 5 + j, 0:GROUPS * D], ones3[:], OB1[:], start=True, stop=False)
                        pe.wait_ge(second_relu, n * 3 + 3)
                        for j in range(2):
                            tokens = slice(TP * j, TP * j + TP)
                            for q in range(ME // 2):
                                nc.tensor.matmul(PS[:, 5 + j, 128 * q:128 * q + 128], H2[:, q, tokens], EW3[:, q, :], start=False, stop=False)
                            mm = nc.tensor.matmul(PS[:, 5 + j, ME * D:GROUPS * D], H2[:, 2, tokens], SW3[:], start=False, stop=True)
                        mm.then_inc(third_done, 1)

                    pe.wait_ge(m_weights_in, 16 * 13)
                    first(0)
                    second(0)
                    first(1)
                    third(0)
                    with pe.Fori(0, B - 2) as i:
                        second(i + 1)
                        first(i + 2)
                        third(i + 1)
                    second(B - 1)
                    third(B - 1)

                @blk.scalar
                def _(act):
                    nc.scalar.preload_act_table_set("natural_log_exp_and_others")
                    mnorm.scalar()
                    mturn.scalar(mnorm.done)
                    mturn.scalar_copies()

                    def softmax_exponentials():
                        act.wait_ge(gates_shifted, 1)
                        nc.scalar.activation(G1[:], ZL[:], ACT.Exp).then_inc(gate_exps, 1)

                    def top_exponentials():
                        act.wait_ge(gates_gap, 1)
                        nc.scalar.activation(GS[:, 4, :], GS[:, 3, :], ACT.Exp).then_inc(gate_exps, 1)

                    def first(n):
                        for g in range(GROUPS):
                            act.wait_ge(first_done, n * GROUPS + (min(g // 2 * 2 + 2, GROUPS)))
                            if g == 0:
                                after(act, second_done, n * 2)
                            nc.scalar.activation(H1[:, g, :], PS[:, g // 2, NTP * (g % 2):NTP * (g % 2) + NTP], ACT.Relu, bias=MB1[:, g:g + 1]).then_inc(first_relu, 1)

                    def second(n):
                        after(act, third_done, n)
                        for q in range(3):
                            act.wait_ge(second_done, n * 2 + (1 if q < 2 else 2))
                            src = PS[:, 3, NTP * q:NTP * q + NTP] if q < 2 else PS[:, 4, 0:NTP]
                            nc.scalar.activation(H2[:, q, :], src, ACT.Relu, bias=MB2[:, q:q + 1]).then_inc(second_relu, 1)

                    act.wait_ge(m_weights_in, 16 * 13)
                    first(0)
                    softmax_exponentials()
                    second(0)
                    first(1)
                    second(1)
                    first(2)
                    top_exponentials()
                    with act.Fori(0, B - 3) as i:
                        second(i + 2)
                        first(i + 3)
                    second(B - 1)

                @blk.vector
                def _(vec):
                    def add_attention(n):
                        vec.wait_ge(back_in[n], 16)
                        nc.vector.tensor_tensor(H[:, quarter(n), :], H[:, quarter(n), :], XR[:, quarter(n), :], ALU.add).then_inc(attention_added, 1)
                        vec.wait_ge(attention_added, n + 1)

                    mnorm.vector(add_attention)
                    mturn.vector()
                    mturn.vector_copies()
                    c = Chain(vec, gate_steps)
                    v = nc.vector

                    def each(column):
                        return column.unsqueeze(2).broadcast_to([128, TILES, ME])

                    vec.wait_ge(logits_done, 1)
                    vec.wait_ge(m_weights_in, 16 * 13)
                    c.link(v.tensor_tensor(ZL[:], PS[:, 7, 0:TILES * ME].rearrange("p (t e) -> p t e", e=ME), GBB[:].unsqueeze(1).broadcast_to([128, TILES, ME]), ALU.add))
                    c.link(v.tensor_reduce(GS[:, 0, :], ZL[:], AX.X, ALU.max))
                    v.tensor_tensor(ZL[:], ZL[:], each(GS[:, 0, :]), ALU.subtract).then_inc(gates_shifted, 1)
                    vec.wait_ge(gate_exps, 1)
                    c.link(v.tensor_reduce(GS[:, 0, :], G1[:], AX.X, ALU.add))
                    c.link(v.reciprocal(GS[:, 1, :], GS[:, 0, :]))
                    c.link(v.tensor_tensor(G1[:], G1[:], each(GS[:, 1, :]), ALU.mult))
                    others = G1[:].unsqueeze(2).broadcast_to([128, TILES, ME, ME])
                    own = G1[:].unsqueeze(3).broadcast_to([128, TILES, ME, ME])
                    earlier = RT[:, EARLIER4:EARLIER4 + ME * ME].rearrange("p (e j) -> p e j", e=ME).unsqueeze(1).broadcast_to([128, TILES, ME, ME])
                    c.step(v.tensor_tensor(GQ[:, 0], others, own, ALU.is_gt))
                    c.link(v.tensor_tensor(GQ[:, 1], others, own, ALU.is_equal))
                    c.link(v.tensor_tensor(GQ[:, 1], GQ[:, 1], earlier, ALU.mult))
                    c.link(v.tensor_tensor(GQ[:, 0], GQ[:, 0], GQ[:, 1], ALU.add))
                    c.link(v.tensor_reduce(G2[:], GQ[:, 0], AX.X, ALU.add))
                    for s in range(2):
                        c.link(v.scalar_tensor_tensor(out=GQ[:, 0, :, 0, :], in0=G2[:], scalar=float(s), in1=G1[:], op0=ALU.is_equal, op1=ALU.mult))
                        c.link(v.tensor_reduce(GS[:, 1 + s, :], GQ[:, 0, :, 0, :], AX.X, ALU.add))
                    v.tensor_tensor(GS[:, 3, :], GS[:, 2, :], GS[:, 1, :], ALU.subtract).then_inc(gates_gap, 1)
                    vec.wait_ge(gate_exps, 2)
                    c.link(v.tensor_scalar(GS[:, 0, :], GS[:, 4, :], 1.0, None, ALU.add))
                    c.link(v.reciprocal(GS[:, 1, :], GS[:, 0, :]))
                    c.link(v.tensor_tensor(GS[:, 2, :], GS[:, 4, :], GS[:, 1, :], ALU.mult))
                    for s in range(2):
                        c.link(v.scalar_tensor_tensor(out=GQ[:, s, :, 0, :], in0=G2[:], scalar=float(s), in1=each(GS[:, 1 + s, :]), op0=ALU.is_equal, op1=ALU.mult))
                    c.link(v.tensor_tensor(G5[:, :, 0:ME], GQ[:, 0, :, 0, :], GQ[:, 1, :, 0, :], ALU.add))

                    def combine(n):
                        vec.wait_ge(third_done, n + 1)
                        after(vec, sum_chain, n)
                        y = PS[:, 5:7, 0:GROUPS * D].rearrange("p j (e f) -> p j e f", f=D)
                        nc.vector.tensor_tensor(WM[:], y, G5[:, bass.ds(n * 2, 2), :].unsqueeze(3).broadcast_to([128, 2, GROUPS, D]), ALU.mult).then_inc(weighted, 1)
                        vec.wait_ge(weighted, n + 1)
                        nc.vector.tensor_reduce(MO[:], WM[:].rearrange("p j e f -> p j f e"), AX.X, ALU.add).then_inc(sum_chain, 1)
                        vec.wait_ge(sum_chain, n + 1)
                        h = H[:, bass.ds(n * 2, 2), :]
                        nc.vector.tensor_tensor(h, h, MO[:], ALU.add).then_inc(token_ready, 1)

                    combine(0)
                    with vec.Fori(0, B - 1) as i:
                        combine(i + 1)


def kernel(**inputs):
    import concourse.bacc as bacc
    from concourse.bass_utils import run_bass_kernel_spmd

    def given(name):
        return np.ascontiguousarray(np.asarray(inputs[name]))

    def head_rows(w):
        return w.reshape(D, 2, 8, DH).transpose(0, 1, 3, 2).reshape(D, 2 * 8 * DH)

    def beside(w):
        return w.transpose(1, 0, 2).reshape(D, -1)

    kv = given("L0_attn_Wkv")
    half = kv.shape[1] // 2
    arrays = {"x": given("x")}
    arrays["k64"] = np.ascontiguousarray(np.concatenate([
        head_rows(given("L0_attn_Wq")), head_rows(kv[:, :half]), kv[:, half:], given("L0_attn_Wg"),
        beside(given("L0_ffn_W1")), given("L1_ffn_sW1"), beside(given("L1_ffn_eW1")), given("L1_ffn_gW")], axis=1))
    for to, name in (("wout", "Wout"), ("bout", "bout"), ("bg", "bg"), ("lq1", "lq1"), ("lk1", "lk1"), ("lq2", "lq2"),
                     ("lk2", "lk2"), ("ln_gamma", "ln_gamma"), ("ln_beta", "ln_beta")):
        arrays[to] = given("L0_attn_" + name)
    for name in ("Wr", "br", "b1", "W2", "b2", "gamma", "beta"):
        arrays["f_" + name.lower()] = given("L0_ffn_" + name)
    for name in ("Wk", "bk", "Wq", "bq", "Wv", "bv", "Wr", "br"):
        arrays["a_" + name.lower()] = np.ascontiguousarray(given("L1_attn_" + name).T)
    for name in ("sb1", "sW2", "sb2", "sW3", "sb3", "eb1", "eW2", "eb2", "eW3", "eb3", "gb"):
        arrays["m_" + name.lower()] = given("L1_ffn_" + name)
    arrays.update(shape_constants())

    nc = bacc.Bacc("TRN2", target_bir_lowering=False, num_devices=1)
    names = {name: nc.dram_tensor(name, a.shape, mybir.dt.from_np(a.dtype), kind="ExternalInput").ap() for name, a in arrays.items()}
    out = nc.dram_tensor("out", (B, NT, D), F32, kind="ExternalOutput").ap()
    build_tower(nc, out=out, **names)
    return run_bass_kernel_spmd(nc, [arrays], core_ids=[0]).results[0]["out"]
```
